# Optimizing a Trainium2 kernel written in Bass

```python
import numpy as np
import jax
import jax.numpy as jnp

def _softmax(x, axis=-1):
    return jax.nn.softmax(x, axis=axis)

def _gelu(x):
    return jax.nn.gelu(x, approximate=True)

def _silu(x):
    return jax.nn.silu(x)

def _sigmoid(x):
    return jax.nn.sigmoid(x)

def _layernorm(x, axis=-1, eps=1e-05):
    m = jnp.mean(x, axis=axis, keepdims=True)
    v = jnp.var(x, axis=axis, keepdims=True)
    return (x - m) / jnp.sqrt(v + eps)

def _scatter_add(tgt, idx, src, axis=0):
    return tgt.at[idx].add(src)

def _segment_sum(src, seg, n):
    return jax.ops.segment_sum(src, seg, n)
kernel_name = 'mk_prb_d2_jaxref_r8_8153ef'

def setup_inputs(seed: int=0):
    np.random.seed(seed)
    _w = jnp.asarray

    def _L0_attn_setup():
        import jax, jax.numpy as jnp
        import numpy as np
        NUM_HEADS = 16
        key = jax.random.key(seed)
        kx, kq, kk, kv = jax.random.split(key, 4)
        N, S, D = (2, 512, 128)
        scale = 1.0 / np.sqrt(D)
        x = jax.random.normal(kx, (N, S, D), dtype=jnp.float32)
        Wq = jax.random.normal(kq, (D, D), dtype=jnp.float32) * scale
        Wk = jax.random.normal(kk, (D, D), dtype=jnp.float32) * scale
        Wv = jax.random.normal(kv, (D, D), dtype=jnp.float32) * scale
        return {'x': x, 'Wq': Wq, 'Wk': Wk, 'Wv': Wv}
    _L0_attn_in = _L0_attn_setup()

    def _L0_ffn_setup():
        import jax, jax.numpy as jnp
        import numpy as np
        from jax import lax
        N_HEADS = 16
        TOP_K = 2
        N_EXPERTS = 8

        def layer_norm(x, w, b, eps=1e-05):
            mu = jnp.mean(x, axis=-1, keepdims=True)
            var = jnp.mean(jnp.square(x - mu), axis=-1, keepdims=True)
            return (x - mu) * lax.rsqrt(var + eps) * w + b

        def attention(x, w_qkv, b_qkv, w_o, b_o):
            B, T, D = x.shape
            dh = D // N_HEADS
            qkv = x @ w_qkv + b_qkv
            q, k, v = jnp.split(qkv, 3, axis=-1)
            q = q.reshape(B, T, N_HEADS, dh)
            k = k.reshape(B, T, N_HEADS, dh)
            v = v.reshape(B, T, N_HEADS, dh)
            scores = jnp.einsum('bqhd,bkhd->bhqk', q, k) / jnp.sqrt(jnp.float32(dh)).astype(x.dtype)
            probs = jax.nn.softmax(scores, axis=-1)
            ctx = jnp.einsum('bhqk,bkhd->bqhd', probs, v).reshape(B, T, D)
            return ctx @ w_o + b_o

        def moe_ff(x, w_gate, w1, b1, w2, b2):
            B, T, D = x.shape
            t = x.reshape(B * T, D)
            probs = jax.nn.softmax(t @ w_gate, axis=-1)
            tw, ti = lax.top_k(probs, TOP_K)
            tw = tw / jnp.sum(tw, axis=-1, keepdims=True)
            out = jnp.zeros_like(t)
            for e in range(N_EXPERTS):
                we = jnp.sum(jnp.where(ti == e, tw, 0.0), axis=-1)
                h = jax.nn.gelu(t @ w1[e] + b1[e]) @ w2[e] + b2[e]
                out = out + we[:, None] * h
            return out.reshape(B, T, D)
        key = jax.random.key(seed)
        ks = jax.random.split(key, 8)
        B, T, D, H, E = (4, 64, 128, 512, 8)
        s = lambda d: 1.0 / np.sqrt(d)
        return {'x': jax.random.normal(ks[0], (B, T, D), jnp.float32), 'ln1_w': jnp.ones((D,), jnp.float32), 'ln1_b': jnp.zeros((D,), jnp.float32), 'ln2_w': jnp.ones((D,), jnp.float32), 'ln2_b': jnp.zeros((D,), jnp.float32), 'w_qkv': jax.random.normal(ks[1], (D, 3 * D), jnp.float32) * s(D), 'b_qkv': jnp.zeros((3 * D,), jnp.float32), 'w_o': jax.random.normal(ks[2], (D, D), jnp.float32) * s(D), 'b_o': jnp.zeros((D,), jnp.float32), 'w_gate': jax.random.normal(ks[3], (D, E), jnp.float32) * s(D), 'w1': jax.random.normal(ks[4], (E, D, H), jnp.float32) * s(D), 'b1': jnp.zeros((E, H), jnp.float32), 'w2': jax.random.normal(ks[5], (E, H, D), jnp.float32) * s(H), 'b2': jnp.zeros((E, D), jnp.float32)}
    _L0_ffn_in = _L0_ffn_setup()

    def _L1_attn_setup():
        import jax, jax.numpy as jnp
        import numpy as np
        import math
        D_K = 64
        key = jax.random.key(seed)
        ks = jax.random.split(key, 5)
        b, m, d, h, dk, dv = (8, 128, 128, 16, 64, 64)
        return {'x': jax.random.normal(ks[0], (b, m, d), dtype=jnp.float32), 'P_q': jax.random.normal(ks[1], (h, d, dk), dtype=jnp.float32) * 0.02, 'P_k': jax.random.normal(ks[2], (h, d, dk), dtype=jnp.float32) * 0.02, 'P_v': jax.random.normal(ks[3], (h, d, dv), dtype=jnp.float32) * 0.02, 'P_o': jax.random.normal(ks[4], (h, d, dv), dtype=jnp.float32) * 0.02}
    _L1_attn_in = _L1_attn_setup()

    def _L1_ffn_setup():
        import jax, jax.numpy as jnp
        import numpy as np
        D_MODEL = 128
        D_FF = 256
        NUM_EXPERTS = 16
        TOP_K = 2
        CAPACITY_FACTOR = 1.25
        BATCH, SEQ = (4, 256)
        key = jax.random.key(seed)
        k0, k1, k2, k3 = jax.random.split(key, 4)
        x = jax.random.normal(k0, (BATCH, SEQ, D_MODEL), jnp.float32)
        gate_w = jax.random.normal(k1, (NUM_EXPERTS, D_MODEL), jnp.float32) / np.float32(np.sqrt(D_MODEL))
        w1 = jax.random.normal(k2, (NUM_EXPERTS, D_MODEL, D_FF), jnp.float32) / np.float32(np.sqrt(D_MODEL))
        w2 = jax.random.normal(k3, (NUM_EXPERTS, D_FF, D_MODEL), jnp.float32) / np.float32(np.sqrt(D_FF))
        return {'x': x, 'gate_w': gate_w, 'w1': w1, 'w2': w2}
    _L1_ffn_in = _L1_ffn_setup()
    _d = {'L0_attn_x': _L0_attn_in['x'], 'L0_attn_Wq': _L0_attn_in['Wq'], 'L0_attn_Wk': _L0_attn_in['Wk'], 'L0_attn_Wv': _L0_attn_in['Wv'], 'L0_ffn_ln1_w': _L0_ffn_in['ln1_w'], 'L0_ffn_ln1_b': _L0_ffn_in['ln1_b'], 'L0_ffn_ln2_w': _L0_ffn_in['ln2_w'], 'L0_ffn_ln2_b': _L0_ffn_in['ln2_b'], 'L0_ffn_w_qkv': _L0_ffn_in['w_qkv'], 'L0_ffn_b_qkv': _L0_ffn_in['b_qkv'], 'L0_ffn_w_o': _L0_ffn_in['w_o'], 'L0_ffn_b_o': _L0_ffn_in['b_o'], 'L0_ffn_w_gate': _L0_ffn_in['w_gate'], 'L0_ffn_w1': _L0_ffn_in['w1'], 'L0_ffn_b1': _L0_ffn_in['b1'], 'L0_ffn_w2': _L0_ffn_in['w2'], 'L0_ffn_b2': _L0_ffn_in['b2'], 'L1_attn_P_q': _L1_attn_in['P_q'], 'L1_attn_P_k': _L1_attn_in['P_k'], 'L1_attn_P_v': _L1_attn_in['P_v'], 'L1_attn_P_o': _L1_attn_in['P_o'], 'L1_ffn_gate_w': _L1_ffn_in['gate_w'], 'L1_ffn_w1': _L1_ffn_in['w1'], 'L1_ffn_w2': _L1_ffn_in['w2']}
    _x0 = _d['L0_attn_x']
    _d['L0_attn_x'] = jax.random.normal(jax.random.fold_in(jax.random.key(seed), 1), (16, 256, 128), dtype=_x0.dtype)
    del _x0
    return _d

def reference(L0_attn_x, L0_attn_Wq, L0_attn_Wk, L0_attn_Wv, L0_ffn_ln1_w, L0_ffn_ln1_b, L0_ffn_ln2_w, L0_ffn_ln2_b, L0_ffn_w_qkv, L0_ffn_b_qkv, L0_ffn_w_o, L0_ffn_b_o, L0_ffn_w_gate, L0_ffn_w1, L0_ffn_b1, L0_ffn_w2, L0_ffn_b2, L1_attn_P_q, L1_attn_P_k, L1_attn_P_v, L1_attn_P_o, L1_ffn_gate_w, L1_ffn_w1, L1_ffn_w2):

    def _L0_attn_ref(x, Wq, Wk, Wv):
        import jax, jax.numpy as jnp
        import numpy as np
        NUM_HEADS = 16
        N, S, D = x.shape
        H = NUM_HEADS
        hd = D // H
        q = (x @ Wq.T).reshape(N, S, H, hd).transpose(0, 2, 1, 3)
        k = (x @ Wk.T).reshape(N, S, H, hd).transpose(0, 2, 1, 3)
        v = (x @ Wv.T).reshape(N, S, H, hd).transpose(0, 2, 1, 3)
        energy = jnp.einsum('nhqd,nhkd->nhqk', q, k)
        attn = jax.nn.softmax(energy / jnp.sqrt(jnp.float32(hd)), axis=3)
        out = jnp.einsum('nhql,nhld->nhqd', attn, v)
        return out.transpose(0, 2, 1, 3).reshape(N, S, D)

    def _L0_ffn_ref(x, ln1_w, ln1_b, ln2_w, ln2_b, w_qkv, b_qkv, w_o, b_o, w_gate, w1, b1, w2, b2):
        import jax, jax.numpy as jnp
        import numpy as np
        from jax import lax
        N_HEADS = 16
        TOP_K = 2
        N_EXPERTS = 8

        def layer_norm(x, w, b, eps=1e-05):
            mu = jnp.mean(x, axis=-1, keepdims=True)
            var = jnp.mean(jnp.square(x - mu), axis=-1, keepdims=True)
            return (x - mu) * lax.rsqrt(var + eps) * w + b

        def attention(x, w_qkv, b_qkv, w_o, b_o):
            B, T, D = x.shape
            dh = D // N_HEADS
            qkv = x @ w_qkv + b_qkv
            q, k, v = jnp.split(qkv, 3, axis=-1)
            q = q.reshape(B, T, N_HEADS, dh)
            k = k.reshape(B, T, N_HEADS, dh)
            v = v.reshape(B, T, N_HEADS, dh)
            scores = jnp.einsum('bqhd,bkhd->bhqk', q, k) / jnp.sqrt(jnp.float32(dh)).astype(x.dtype)
            probs = jax.nn.softmax(scores, axis=-1)
            ctx = jnp.einsum('bhqk,bkhd->bqhd', probs, v).reshape(B, T, D)
            return ctx @ w_o + b_o

        def moe_ff(x, w_gate, w1, b1, w2, b2):
            B, T, D = x.shape
            t = x.reshape(B * T, D)
            probs = jax.nn.softmax(t @ w_gate, axis=-1)
            tw, ti = lax.top_k(probs, TOP_K)
            tw = tw / jnp.sum(tw, axis=-1, keepdims=True)
            out = jnp.zeros_like(t)
            for e in range(N_EXPERTS):
                we = jnp.sum(jnp.where(ti == e, tw, 0.0), axis=-1)
                h = jax.nn.gelu(t @ w1[e] + b1[e]) @ w2[e] + b2[e]
                out = out + we[:, None] * h
            return out.reshape(B, T, D)
        h = x + attention(layer_norm(x, ln1_w, ln1_b), w_qkv, b_qkv, w_o, b_o)
        return h + moe_ff(layer_norm(h, ln2_w, ln2_b), w_gate, w1, b1, w2, b2)

    def _L1_attn_ref(x, P_q, P_k, P_v, P_o):
        import jax, jax.numpy as jnp
        import numpy as np
        import math
        D_K = 64
        m = x.shape[1]
        Q = jnp.einsum('bmd,hdk->bhmk', x, P_q)
        K = jnp.einsum('bmd,hdk->bhmk', x, P_k)
        V = jnp.einsum('bmd,hdv->bhmv', x, P_v)
        logits = jnp.einsum('bhmk,bhnk->bhmn', Q, K) * math.sqrt(D_K)
        causal = jnp.tril(jnp.ones((m, m), dtype=bool))
        logits = jnp.where(causal[None, None], logits, -jnp.inf)
        key_weights = jax.nn.softmax(logits, axis=-1)
        o = jnp.einsum('bhmm,bhmv->bhmv', key_weights, V)
        y = jnp.einsum('bhmv,hdv->bmd', o, P_o)
        return y

    def _L1_ffn_ref(x, gate_w, w1, w2):
        import jax, jax.numpy as jnp
        import numpy as np
        D_MODEL = 128
        D_FF = 256
        NUM_EXPERTS = 16
        TOP_K = 2
        CAPACITY_FACTOR = 1.25
        BATCH, SEQ = (4, 256)
        B, S, d = x.shape
        T = B * S
        E, K = (NUM_EXPERTS, TOP_K)
        capacity = int(CAPACITY_FACTOR * T * K / E)
        xf = x.reshape(T, d)
        logits = xf @ gate_w.T
        probs = jax.nn.sigmoid(logits)
        top_vals, sel = jax.lax.top_k(probs, K)
        weights = top_vals / (top_vals.sum(-1, keepdims=True) + 1e-06)
        flat_sel = sel.reshape(-1)
        onehot = jax.nn.one_hot(flat_sel, E, dtype=jnp.int32)
        ranks = jnp.take_along_axis(jnp.cumsum(onehot, axis=0), flat_sel[:, None], axis=1)[:, 0] - 1
        valid = ranks < capacity
        sentinel = E * capacity
        slot = jnp.where(valid, flat_sel * capacity + ranks, sentinel)
        x_rep = jnp.repeat(xf, K, axis=0)
        padded = jnp.zeros((sentinel + 1, d), xf.dtype).at[slot].set(x_rep)
        padded = padded[:sentinel].reshape(E, capacity, d)
        h = jax.nn.gelu(jnp.einsum('ecd,edf->ecf', padded, w1), approximate=False)
        out_padded = jnp.einsum('ecf,efd->ecd', h, w2).reshape(sentinel, d)
        gathered = out_padded[jnp.minimum(slot, sentinel - 1)]
        gathered = jnp.where(valid[:, None], gathered, jnp.zeros((), xf.dtype))
        out = (gathered * weights.reshape(-1)[:, None]).reshape(T, K, d).sum(axis=1)
        return out.reshape(B, S, d)
    x = L0_attn_x
    xn = _layernorm(x, axis=-1)
    x = x + _L0_attn_ref(xn, L0_attn_Wq, L0_attn_Wk, L0_attn_Wv) + _L0_ffn_ref(xn, L0_ffn_ln1_w, L0_ffn_ln1_b, L0_ffn_ln2_w, L0_ffn_ln2_b, L0_ffn_w_qkv, L0_ffn_b_qkv, L0_ffn_w_o, L0_ffn_b_o, L0_ffn_w_gate, L0_ffn_w1, L0_ffn_b1, L0_ffn_w2, L0_ffn_b2)
    xn = _layernorm(x, axis=-1)
    x = x + _L1_attn_ref(xn, L1_attn_P_q, L1_attn_P_k, L1_attn_P_v, L1_attn_P_o) + _L1_ffn_ref(xn, L1_ffn_gate_w, L1_ffn_w1, L1_ffn_w2)
    return x

_drawn_inputs = setup_inputs


def setup_inputs(seed=0):
    import zlib

    import numpy as np

    out = dict(_drawn_inputs(seed))
    spreads = {'L0_ffn_ln1_w': (1.0, 0.2),
     'L0_ffn_ln1_b': (0.0, 0.1),
     'L0_ffn_ln2_w': (1.0, 0.2),
     'L0_ffn_ln2_b': (0.0, 0.1),
     'L0_ffn_b_qkv': (0.0, 0.1),
     'L0_ffn_b_o': (0.0, 0.1),
     'L0_ffn_b1': (0.0, 0.1),
     'L0_ffn_b2': (0.0, 0.1)}
    factors = {'L1_attn_P_q': 8.0, 'L1_attn_P_k': 8.0, 'L1_attn_P_v': 6.945, 'L1_attn_P_o': 6.982}
    for name, (base, spread) in spreads.items():
        noise = np.random.default_rng([zlib.crc32(name.encode()), seed]).standard_normal(out[name].shape)
        drawn = base * np.exp(spread * noise) if base else spread * noise
        out[name] = jnp.asarray(drawn.astype(out[name].dtype))
    for name, factor in factors.items():
        out[name] = (out[name] * factor).astype(out[name].dtype)
    return out
```

```python
from contextlib import ExitStack

import concourse.bass as bass
from concourse import mybir

F32 = mybir.dt.float32
F32R = mybir.dt.float32r
BF16 = mybir.dt.bfloat16
I32 = mybir.dt.int32
U32 = mybir.dt.uint32
ALU = mybir.AluOpType
ACT = mybir.ActivationFunctionType
AX = mybir.AxisListType
ds = bass.ds

P = 128
EPS = 1e-5
NEVER = -1e38
W_LOADS = 16

SEMAPHORES = """
x_loaded w_loaded p_loaded moe_w_loaded ident_zero ident_ready consts_made zero_ready tables_zeroed dve_step
stats_taken spread_ready root_ready xn_ready yn_ready hb_ready
w_turned w_turned_copied pq_turned pq_copied pk_turned pk_copied a_made a_copied po_turned po_copied b1_turned b1_copied
xt_turned xt_copied qkv_done qk_split v_copied
s_ready s_reduced m_turned m_copied st_ready exp_done pv_done ct_copied ct_turned rec_done o_ready
ot_turned ot_copied wo_done h_added x_added rows_init
rt_staged0 rt_staged1 rt_turned rt_copied rt_logits rt_kept odds_ready sums_ready slots_ready weights_ready
scattered x_in0 x_in1 up_in0 up_in1 down_in0 down_in1 e_turned e_copied e_hidden e_gelu e_out e_added e_stored0 e_stored1
gathered0 gathered1 gathered2 gathered3 combined base_added
u_ready u_copied s0_ready s1_ready max0_ready max1_ready exp0_done exp1_done diag_masked diag_summed
share_ready v1_ready o1_ready o1_turned o1_copied y_ready y_added out_sent
""".split()


def build(nc, A, out):
    B, S, D = A["L0_attn_x"].shape
    NT = B * S // P
    QT = S // P
    HEADS = 16
    HD = D // HEADS
    GROUPS = 4
    UNITS = 8
    SCALE = 1.0 / float(HD) ** 0.5
    JOBS = 2 * B
    DK = A["L1_attn_P_q"].shape[2]
    DV = A["L1_attn_P_v"].shape[2]
    E0, _, F0 = A["L0_ffn_w1"].shape
    E1, _, F1 = A["L1_ffn_w1"].shape
    TOP = 2
    SLOTS = 256
    STEPS0 = NT * P * TOP // SLOTS + E0
    CAP = int(1.25 * NT * P * TOP / E1)
    CT = CAP // P
    ROWS0 = STEPS0 * SLOTS
    ROWS1 = E1 * CAP
    HALF = CAP // 2
    assert S == 256 and D == P and CAP % P == 0 and F0 == 512 and F1 == 256 and ROWS0 % P == 0

    with ExitStack() as ctx:
        def sb(name, shape, dt=F32, into=ctx):
            return into.enter_context(nc.sbuf_tensor(name, shape, dt))

        s = {n: ctx.enter_context(nc.semaphore(n)) for n in SEMAPHORES}
        rows_sent = [ctx.enter_context(nc.semaphore(f"rows_sent{j}")) for j in range(4)]
        m_sent = [ctx.enter_context(nc.semaphore(f"m_sent{j}")) for j in range(4)]
        xs_staged = [ctx.enter_context(nc.semaphore(f"xs_staged{j}")) for j in range(4)]
        x_in, up_in, down_in = ([s[f"{n}{p}"] for p in range(2)] for n in ("x_in", "up_in", "down_in"))
        e_stored = [s["e_stored0"], s["e_stored1"]]
        rt_staged = [s["rt_staged0"], s["rt_staged1"]]
        gathered = [s[f"gathered{k}"] for k in range(4)]

        xg = [nc.dram_tensor("xg0", (ROWS0, D), F32).ap(), nc.dram_tensor("xg1", (ROWS1 + NT * P * TOP, D), F32).ap()]
        yg = [nc.dram_tensor("yg0", (ROWS0, D), F32).ap(), nc.dram_tensor("yg1", (ROWS1, D), F32).ap()]

        X = sb("X", [P, NT, D])
        XN = sb("XN", [P, NT, D])
        YN = sb("YN", [P, NT, D])
        HB = sb("HB", [P, NT, D])
        stats = sb("stats", [P, NT, 6])
        st = sb("st", [P, 6, NT])
        ident = sb("ident", [P, P])
        identb = sb("identb", [P, P], BF16)
        ones = sb("ones", [P, P])
        before = sb("before", [P, P])
        tri0 = sb("tri0", [P, 4, P], BF16)
        tri1 = sb("tri1", [P, 2, 2 * P], BF16)
        wo = sb("wo", [P, D])
        lnw = sb("lnw", [P, 4])
        bqk = sb("bqk", [P, 2])
        bv = sb("bv", [P, D])
        bo = sb("bo", [P, D])
        wqkv = [sb(f"wqkv{a}", [P, 3, D]) for a in range(2)]
        b1T = sb("b1T", [P, E0 * F0 // P])
        wg = [sb("wg0", [P, E0]), sb("wg1", [P, E1])]
        AH = sb("AH", [P, HEADS, D])
        PoT = sb("PoT", [P, HEADS // 2, D])
        Pv = sb("Pv", [P, HEADS * DV])
        xs = [sb(f"xs{a}", [P, QT, D]) for a in range(2)]
        xT = [sb(f"xT{a}", [P, S]) for a in range(2)]

        revi = sb("revi", [P, E1], I32)
        rev = sb("rev", [P, E1])
        stepi = sb("stepi", [P, STEPS0], I32)
        stepf = sb("stepf", [P, STEPS0])
        dumpi = sb("dumpi", [P, NT, TOP], I32)
        dump = sb("dump", [P, NT, TOP])
        capi = sb("capi", [P, E1], I32)
        capb = sb("capb", [P, E1])
        top = sb("top", [P, TOP, NT])
        tj = sb("tj", [P, TOP, NT])
        tw = sb("tw", [P, TOP, NT])
        tmp = sb("tmp", [P, 4, NT])
        slot = sb("slot", [P, TOP, NT])
        slot_to = sb("slot_to", [P, TOP, NT], I32)
        slot_from = sb("slot_from", [P, TOP, NT], I32)
        cnt = sb("cnt", [P, 4, E0])
        cnti = sb("cnti", [P, E0], I32)
        emapf = sb("emapf", [P, STEPS0])
        emap = sb("emap", [P, STEPS0], I32)

        def expert_buffers(into):
            return [dict(x=sb(f"ex{p}", [P, CT, D], F32, into), w1=sb(f"ew1{p}", [P, F0], F32, into),
                         w2=sb(f"ew2{p}", [P, F0 // P, D], F32, into), b1=sb(f"eb1{p}", [P, F0 // P], F32, into),
                         b2=sb(f"eb2{p}", [P, D], F32, into), xT=sb(f"exT{p}", [P, CAP], F32, into),
                         y=sb(f"ey{p}", [P, CT, D], F32, into)) for p in range(2)]

        with ExitStack() as early:
            zeros = sb("zeros", [P, 2048], F32, early)
            wraw = sb("wraw", [P, 3, D], F32, early)
            b1raw = sb("b1raw", [E0 * F0 // P, P], F32, early)
            wg1raw = sb("wg1raw", [E1, D], F32, early)
            praw = sb("praw", [P, HEADS, DK], F32, early)
            kraw = sb("kraw", [P, HEADS, DK], F32, early)
            oraw = sb("oraw", [P, HEADS, DV], F32, early)
            PqT = sb("PqT", [P, HEADS // 2, D], F32, early)
            PkT = sb("PkT", [P, HEADS // 2, D], F32, early)
        with ExitStack() as routing:
            LG = sb("LG", [P, NT, E1], F32, routing)
            OH = sb("OH", [P, TOP, NT, E1], F32, routing)
            RK = sb("RK", [P, NT, E1], F32, routing)
            TA = sb("TA", [P, NT, E1], F32, routing)
            TB = sb("TB", [P, NT, E1], F32, routing)
            xr = [sb(f"xr{p}", [P, 4, D], F32, routing) for p in range(2)]
            rT = [sb(f"rT{p}", [P, 4 * P], F32, routing) for p in range(2)]
        ex = expert_buffers(ctx)
        got = [sb(f"got{k}", [P, D]) for k in range(4)]

        with ExitStack() as first:
            nat = [sb(f"nat{a}", [P, 4, S], F32R, first) for a in range(2)]
            rows = [sb(f"rows{j}", [P, GROUPS, 2, S], F32R, first) for j in range(4)]
            va = [sb(f"va{j}", [P, QT, HEADS, 32], F32, first) for j in range(4)]
            negm = [sb(f"negm{a}", [P, QT, HEADS], F32, first) for a in range(2)]
            mT = [sb(f"mT{a}", [HEADS, S], F32R, first) for a in range(2)]
            probs = sb("probs", [P, 2, 4, S], F32, first)
            ctxT = sb("ctxT", [P, 4, S], F32, first)
            rec = sb("rec", [P, 2 * HEADS], F32, first)
            o = sb("o", [P, QT, D], F32, first)
            oT = sb("oT", [P, S], F32, first)
        for p in range(2):
            ex[p]["g"] = sb(f"eg{p}", [P, 4, HALF])
        U = [sb(f"U{p}", [P, 4, S]) for p in range(2)]
        EX0 = [sb(f"EX0{p}", [P, 4, P]) for p in range(2)]
        EX1 = [sb(f"EX1{p}", [P, 4, S]) for p in range(2)]
        DG = [sb(f"DG{p}", [P, 2, 4, P]) for p in range(2)]
        nm = [sb(f"nm{p}", [P, 2, 4]) for p in range(2)]
        den = [sb(f"den{p}", [P, QT, HEADS]) for p in range(2)]
        num = [sb(f"num{p}", [P, QT, HEADS]) for p in range(2)]
        share = [sb(f"share{p}", [P, QT, HEADS]) for p in range(2)]
        O1 = sb("O1", [P, HEADS * DV])
        O1T = sb("O1T", [P, HEADS // 2, P])

        ps = ctx.enter_context(nc.psum_tensor("ps", [P, 8, 512], F32))
        ps_s, ps_t, ps_pv, ps_m = ps[:, 0:2, :], ps[:, 2:4, :], ps[:, 4:6, :], ps[:, 6:8, :]

        LAYER = [dict(E=E0, src=YN), dict(E=E1, src=XN)]

        def flat(ap):
            return ap.rearrange("p a d -> p (a d)")

        block = ctx.enter_context(nc.Block())

        @block.sync
        def _(sp):
            xv = A["L0_attn_x"].rearrange("b (q p) d -> p (b q) d", p=P)
            step = NT // 4
            for i in range(4):
                sp.dma_start(X[:, i * step:(i + 1) * step, :], xv[:, i * step:(i + 1) * step, :]).then_inc(s["x_loaded"], 16)
            loads = [(wraw[:, i, :], A[n]) for i, n in enumerate(("L0_attn_Wq", "L0_attn_Wk", "L0_attn_Wv"))]
            loads += [(wqkv[1][:, :, :], A["L0_ffn_w_qkv"].rearrange("d (t e) -> d t e", t=3)), (wo[:, :], A["L0_ffn_w_o"])]
            loads += [(lnw[:, i:i + 1], A[n].rearrange("(d a) -> d a", a=1))
                      for i, n in enumerate(("L0_ffn_ln1_w", "L0_ffn_ln1_b", "L0_ffn_ln2_w", "L0_ffn_ln2_b"))]
            loads += [(bqk[:, t:t + 1], A["L0_ffn_b_qkv"][t * D:(t + 1) * D].rearrange("(e a) -> e a", a=1)) for t in range(2)]
            loads += [(bv[:, :], A["L0_ffn_b_qkv"][2 * D:3 * D].rearrange("(a e) -> a e", a=1).broadcast_to([P, D])),
                      (bo[:, :], A["L0_ffn_b_o"].rearrange("(a e) -> a e", a=1).broadcast_to([P, D])),
                      (b1raw[:, :], A["L0_ffn_b1"].rearrange("e (f p) -> (e f) p", p=P)),
                      (wg[0][:, :], A["L0_ffn_w_gate"]), (wg1raw[:, :], A["L1_ffn_gate_w"])]
            for dst, src in loads:
                sp.dma_start(dst, src).then_inc(s["w_loaded"], 16)
            assert len(loads) == W_LOADS
            for dst, n in ((praw, "L1_attn_P_q"), (kraw, "L1_attn_P_k"), (oraw, "L1_attn_P_o")):
                sp.dma_start(dst[:, :, :], A[n].rearrange("h d k -> d h k")).then_inc(s["p_loaded"], 16)
            sp.dma_start(Pv[:, :].rearrange("d (h v) -> d h v", h=HEADS), A["L1_attn_P_v"].rearrange("h d v -> d h v")).then_inc(s["p_loaded"], 16)
            sp.wait_ge(s["zero_ready"], 1)
            for table, n in ((xg[0], ROWS0), (xg[1], ROWS1)):
                v = table[0:n, :].rearrange("(p r) c -> p (r c)", p=P)
                for c in range(0, n, 2048):
                    sp.dma_start(v[:, c:c + 2048], zeros[:, :]).then_inc(s["tables_zeroed"], 16)

            def stage(pas, q, j):
                src = (YN, XN)[pas]
                if not isinstance(q, int) or 4 * q + j >= 2:
                    sp.wait_ge(s["xt_turned"], 4 * q + j - 1)
                sp.dma_start(xs[j % 2][:, :, :], src[:, ds(8 * q + 2 * j - 2 * B * pas, 2), :]).then_inc(xs_staged[j], 16)

            def send_rows(q, j):
                sp.wait_ge(s["qk_split"], 16 * q + 4 * j + 4)
                for g in range(GROUPS):
                    for role, part, side, m in ((0, 2, 0, 1), (0, 1, 1, 1), (1, 0, 0, 2), (2, 2, 0, 2)):
                        sp.dma_start(rows[j][role:P:4, g, side:side + m, :].bitcast(F32),
                                     nat[j % 2][32 * g:32 * g + 32, part:part + m, :].bitcast(F32)).then_inc(rows_sent[j], 16)

            def send_m(q, j):
                sp.wait_ge(s["m_copied"], 4 * q + j + 1)
                for g in range(GROUPS):
                    sp.dma_start(rows[j][31:P:32, g, 0, :].bitcast(F32), mT[j % 2][4 * g:4 * g + 4, :].bitcast(F32)).then_inc(m_sent[j], 16)

            def attention(pas):
                q0 = JOBS // 8 * pas
                stage(pas, q0, 0)
                stage(pas, q0, 1)
                if pas == 0:
                    sp.wait_ge(s["rows_init"], 12)
                send_rows(q0, 0)
                stage(pas, q0, 2)
                send_rows(q0, 1)
                stage(pas, q0, 3)
                send_rows(q0, 2)
                send_m(q0, 0)
                send_m(q0, 1)
                last = q0 + JOBS // 8 - 1
                with sp.Fori(q0, last) as q:
                    for j in range(4):
                        stage(pas, q + 1, j)
                        send_rows(q + (j + 3) // 4, (j + 3) % 4)
                        send_m(q + (j + 2) // 4, (j + 2) % 4)
                send_rows(last, 3)
                send_m(last, 2)
                send_m(last, 3)

            def route(l):
                def pair(i):
                    for p in range(2):
                        if not (isinstance(i, int) and l == 0):
                            sp.wait_ge(s["rt_turned"], NT // 4 * l + 2 * i)
                        sp.dma_start(xr[p][:, :, :], LAYER[l]["src"][:, ds(8 * i + 4 * p, 4), :]).then_inc(rt_staged[p], 16)

                pair(0)
                with sp.Fori(1, NT // 8) as i:
                    pair(i)

            sp.wait_ge(s["yn_ready"], NT)
            attention(0)
            sp.wait_ge(s["yn_ready"], 2 * NT)
            route(0)
            attention(1)

            sp.wait_ge(s["scattered"], 16 * NT * TOP)
            sp.wait_ge(s["weights_ready"], 1)

            def load_x(i, p):
                sp.dma_start(ex[p]["x"][:, 0:2, :], xg[0][ds(i * SLOTS, SLOTS), :].rearrange("(k p) d -> p k d", p=P)).then_inc(x_in[p], 16)

            def load_up(e, p):
                sp.dma_start(ex[p]["w1"][:, :], A["L0_ffn_w1"][ds(e, 1), :, :].rearrange("a d f -> d (a f)")).then_inc(up_in[p], 16)
                sp.dma_start(ex[p]["b1"][:, :], b1T[:, ds(e * (F0 // P), F0 // P)]).then_inc(up_in[p], 16)

            def load_down(e, p):
                sp.dma_start(ex[p]["w2"][:, :, :], A["L0_ffn_w2"][ds(e, 1), :, :].rearrange("a (f p) d -> p (a f) d", p=P)).then_inc(down_in[p], 16)
                sp.dma_start(ex[p]["b2"][:, :], A["L0_ffn_b2"][ds(e, 1), :].broadcast_to([P, D])).then_inc(down_in[p], 16)

            def expert_of(i):
                return sp.value_load(emap[0:1, ds(i, 1)], min_val=0, max_val=E0 - 1)

            def store_step(i, p):
                sp.wait_ge(s["e_added"], i + 1)
                sp.dma_start(yg[0][ds(i * SLOTS, SLOTS), :].rearrange("(k p) d -> p k d", p=P), ex[p]["y"][:, 0:2, :]).then_inc(e_stored[p], 16)

            for i in range(2):
                e = expert_of(i)
                load_x(i, i)
                load_up(e, i)
                load_down(e, i)
            with sp.Fori(0, STEPS0 // 2 - 1) as h:
                for p in range(2):
                    i = 2 * h + p
                    e = expert_of(i + 2)
                    sp.wait_ge(s["e_turned"], i + 1)
                    load_x(i + 2, p)
                    sp.wait_ge(s["e_gelu"], i + 1)
                    load_up(e, p)
                    store_step(i, p)
                    load_down(e, p)
            store_step(STEPS0 - 2, 0)
            store_step(STEPS0 - 1, 1)

            sp.wait_ge(s["xn_ready"], 2 * NT)
            route(1)

            def stage1(b, p):
                if not isinstance(b, int):
                    sp.wait_ge(s["u_ready"], 5 * b - 9)
                sp.dma_start(xs[p][:, :, :], XN[:, ds(2 * b, 2), :]).then_inc(xs_staged[p], 16)

            stage1(0, 0)
            stage1(1, 1)
            with sp.Fori(0, B // 2 - 1) as h:
                for p in range(2):
                    stage1(2 * h + p + 2, p)

            sp.wait_ge(s["scattered"], 32 * NT * TOP)

            def load_tokens(e, p):
                sp.dma_start(ex[p]["x"][:, :, :], xg[1][ds(e * CAP, CAP), :].rearrange("(k p) d -> p k d", p=P)).then_inc(x_in[p], 16)

            def load_w1(e, p):
                sp.dma_start(ex[p]["w1"][:, 0:F1], A["L1_ffn_w1"][ds(e, 1), :, :].rearrange("a d f -> d (a f)")).then_inc(up_in[p], 16)

            def load_w2(e, p):
                sp.dma_start(ex[p]["w2"][:, 0:F1 // P, :], A["L1_ffn_w2"][ds(e, 1), :, :].rearrange("a (f p) d -> p (a f) d", p=P)).then_inc(down_in[p], 16)

            def store_expert(e, p):
                sp.wait_ge(s["e_added"], STEPS0 + e + 1)
                sp.dma_start(yg[1][ds(e * CAP, CAP), :].rearrange("(k p) d -> p k d", p=P), ex[p]["y"][:, :, :]).then_inc(e_stored[p], 16)

            for e in range(2):
                load_tokens(e, e)
                load_w1(e, e)
                load_w2(e, e)
            with sp.Fori(0, E1 // 2 - 1) as h:
                for p in range(2):
                    e = 2 * h + p
                    sp.wait_ge(s["e_turned"], STEPS0 + e + 1)
                    load_tokens(e + 2, p)
                    sp.wait_ge(s["e_hidden"], STEPS0 + e + 1)
                    load_w1(e + 2, p)
                    store_expert(e, p)
                    load_w2(e + 2, p)
            store_expert(E1 - 2, 0)
            store_expert(E1 - 1, 1)

            ov = out.rearrange("b (q p) d -> p (b q) d", p=P)
            for i in range(4):
                sp.wait_ge(s["combined"], TOP * NT + TOP * step * (i + 1))
                sp.dma_start(ov[:, i * step:(i + 1) * step, :], X[:, i * step:(i + 1) * step, :]).then_inc(s["out_sent"], 16)
            sp.wait_ge(s["out_sent"], 64)

        @block.gpsimd
        def _(pool):
            pool.memset(ident[:, :], 0.0).then_inc(s["ident_zero"], 1)
            pool.memset(before[:, :], 1.0).then_inc(s["ident_zero"], 1)
            pool.memset(tri0[:, :, :], 0.0).then_inc(s["ident_zero"], 1)
            pool.memset(tri1[:, :, :], 0.0).then_inc(s["ident_zero"], 1)
            pool.wait_ge(s["ident_zero"], 4)
            pool.affine_select(out=ident[:, :], in_=ident[:, :], compare_op=ALU.not_equal, fill=1.0, base=0,
                               pattern=[[-1, P]], channel_multiplier=1).then_inc(s["ident_ready"], 1)
            pool.memset(zeros[:, :], 0.0).then_inc(s["zero_ready"], 1)
            pool.affine_select(out=before[:, :], in_=before[:, :], compare_op=ALU.is_gt, fill=0.0, base=0,
                               pattern=[[1, P]], channel_multiplier=-1).then_inc(s["consts_made"], 1)
            pool.affine_select(out=tri0[:, :, :], in_=tri0[:, :, :], compare_op=ALU.is_ge, fill=NEVER, base=0,
                               pattern=[[0, 4], [-1, P]], channel_multiplier=1).then_inc(s["consts_made"], 1)
            pool.affine_select(out=tri1[:, :, :], in_=tri1[:, :, :], compare_op=ALU.is_ge, fill=NEVER, base=P,
                               pattern=[[0, 2], [-1, 2 * P]], channel_multiplier=1).then_inc(s["consts_made"], 1)
            pool.memset(ones[:, :], 1.0).then_inc(s["consts_made"], 1)
            pool.iota(revi[:, :], pattern=[[-1, E1]], base=E1, channel_multiplier=0).then_inc(s["consts_made"], 1)
            pool.iota(stepi[:, :], pattern=[[1, STEPS0]], base=0, channel_multiplier=0).then_inc(s["consts_made"], 1)
            pool.iota(dumpi[:, :, :], pattern=[[P * TOP, NT], [1, TOP]], base=ROWS1, channel_multiplier=TOP).then_inc(s["consts_made"], 1)
            pool.iota(capi[:, :], pattern=[[CAP, E1]], base=0, channel_multiplier=0).then_inc(s["consts_made"], 1)
            for j in range(4):
                pool.memset(rows[j][:, :, 0, :].bitcast(F32), 0.0).then_inc(s["rows_init"], 1)
                pool.memset(rows[j][:, :, 1, :].bitcast(F32), 1.0).then_inc(s["rows_init"], 1)
                pool.memset(va[j][:, :, :, :], 0.0).then_inc(s["ident_zero"], 1)
                pool.wait_ge(s["ident_zero"], 5 + j)
                pool.memset(va[j][:, :, :, HD:HD + 1], 1.0).then_inc(s["rows_init"], 1)

            def scatter(l, rows_of):
                for t in range(NT):
                    for k in range(TOP):
                        pool.indirect_dma_start(
                            out=xg[l], out_offset=bass.IndirectOffsetOnAxis(ap=slot_to[:, k, t:t + 1].bitcast(U32), axis=0),
                            in_=rows_of[:, t, :], in_offset=None).then_inc(s["scattered"], 16)

            def gather(l):
                for t in range(NT):
                    for k in range(TOP):
                        n = TOP * t + k
                        if n >= 4:
                            pool.wait_ge(s["combined"], TOP * NT * l + n - 3)
                        pool.indirect_dma_start(
                            out=got[n % 4][:, :], out_offset=None, in_=yg[l],
                            in_offset=bass.IndirectOffsetOnAxis(ap=slot_from[:, k, t:t + 1].bitcast(U32), axis=0)).then_inc(gathered[n % 4], 16)

            pool.wait_ge(s["tables_zeroed"], 160)
            pool.wait_ge(s["slots_ready"], 1)
            scatter(0, YN)
            for p in range(2):
                pool.wait_ge(e_stored[p], 16 * (STEPS0 // 2))
            gather(0)
            pool.wait_ge(s["slots_ready"], 2)
            scatter(1, XN)

            def diagonal(n, p):
                pool.wait_ge(s["exp0_done"], n + 1)
                if not (isinstance(n, int) and n < 2):
                    pool.wait_ge(s["diag_summed"], n - 1)
                eye = ident[:, :].unsqueeze(1).broadcast_to([P, 4, P])
                pool.tensor_tensor(DG[p][:, 0], EX0[p][:, :, :], eye, ALU.mult).then_inc(s["diag_masked"], 1)
                pool.wait_ge(s["exp1_done"], n + 1)
                pool.tensor_tensor(DG[p][:, 1], EX1[p][:, :, P:2 * P], eye, ALU.mult).then_inc(s["diag_masked"], 1)

            diagonal(0, 0)
            diagonal(1, 1)
            with pool.Fori(1, 2 * B) as h:
                for p in range(2):
                    diagonal(2 * h + p, p)

            for p in range(2):
                pool.wait_ge(e_stored[p], 16 * (STEPS0 // 2 + E1 // 2))
            gather(1)

        @block.scalar
        def _(act):
            def root(r):
                act.wait_ge(s["spread_ready"], r + 1)
                act.activation(st[:, 4, :], st[:, 3, :], ACT.Sqrt).then_inc(s["root_ready"], 1)

            act.wait_ge(s["ident_ready"], 1)
            act.activation(identb[:, :], ident[:, :], ACT.Copy).then_inc(s["consts_made"], 1)
            root(0)
            root(1)
            act.wait_ge(s["pq_turned"], 1)
            act.activation(PqT[:, :, :], ps_s.rearrange("p b (c d) -> p (b c) d", d=D), ACT.Copy).then_inc(s["pq_copied"], 1)
            act.wait_ge(s["pk_turned"], 1)
            act.activation(PkT[:, :, :], ps_t.rearrange("p b (c d) -> p (b c) d", d=D), ACT.Copy).then_inc(s["pk_copied"], 1)
            act.wait_ge(s["po_turned"], 1)
            act.activation(PoT[:, :, :], ps_m.rearrange("p b (c d) -> p (b c) d", d=D), ACT.Copy).then_inc(s["po_copied"], 1)
            act.wait_ge(s["a_made"], 1)
            act.activation(AH[:, :, :].rearrange("p (c a) d -> p a c d", a=2), ps[:, 0:4, :].rearrange("p (a b) (c d) -> p a (b c) d", a=2, d=D), ACT.Copy, scale=float(DK) ** 0.5).then_inc(s["a_copied"], 1)

            def exps(n, u, skip=False):
                act.wait_ge(s["st_ready"], 8 * n + u + 1)
                if not skip:
                    act.wait_ge(s["pv_done"], 8 * n + u - 1)
                act.activation(probs[:, u % 2, :, :], ps_t.rearrange("p b (g q) -> p (b g) q", g=2), ACT.Exp,
                               scale=SCALE).then_inc(s["exp_done"], 1)

            def attention(pas):
                q0 = JOBS // 8 * pas

                def quad(q, first=False):
                    for j in range(4):
                        n = 4 * q + j
                        for u in range(UNITS):
                            exps(n, u, first and j == 0 and u < 2)
                        act.wait_ge(s["pv_done"], 8 * n + 8)
                        if not (first and j == 0):
                            act.wait_ge(s["ct_turned"], n)
                        act.activation(ctxT[:, :, :], ps_pv.rearrange("p b (c q) -> p (b c) q", c=2), ACT.Copy).then_inc(s["ct_copied"], 1)
                        if pas == 0:
                            act.wait_ge(s["ot_turned"], n + 1)
                            act.activation(oT[:, :], ps_s[:, 1, 0:S], ACT.Copy).then_inc(s["ot_copied"], 1)

                start = q0
                if pas == 0:
                    quad(0, True)
                    start = 1
                with act.Fori(start, q0 + JOBS // 8) as q:
                    quad(q)

            attention(0)
            root(2)
            act.wait_ge(s["odds_ready"], 1)
            act.activation(tmp[:, 1, :], tmp[:, 0, :], ACT.Exp).then_inc(s["odds_ready"], 1)
            attention(1)

            def gelu0(i, p):
                act.wait_ge(s["e_hidden"], i + 1)
                if not isinstance(i, int) or i >= 2:
                    act.wait_ge(s["e_out"], i - 1)
                for f in range(F0 // P):
                    last = act.activation(ex[p]["g"][:, f, 0:SLOTS], ps[:, 2 * p + f // 2, (f % 2) * SLOTS:(f % 2 + 1) * SLOTS],
                                          ACT.Gelu_apprx_tanh, bias=ex[p]["b1"][:, f:f + 1])
                last.then_inc(s["e_gelu"], 1)

            gelu0(0, 0)
            gelu0(1, 1)
            with act.Fori(1, STEPS0 // 2) as h:
                for p in range(2):
                    gelu0(2 * h + p, p)

            root(3)
            act.wait_ge(s["odds_ready"], 3)
            act.activation(TA[:, :, :], LG[:, :, :], ACT.Exp, scale=-1.0).then_inc(s["odds_ready"], 1)

            def copy_u(b, g):
                if not (isinstance(b, int) and b == 0 and g < 2):
                    act.wait_ge(s["s1_ready"], 4 * b + g - 1)
                act.wait_ge(s["u_ready"], 5 * b + g + 2)
                act.activation(U[g % 2][:, :, :], ps_s.rearrange("p b (c q) -> p (b c) q", c=2), ACT.Copy).then_inc(s["u_copied"], 1)

            def exps1(b, g, p):
                n, gp = 4 * b + g, g % 2
                if not (isinstance(b, int) and b == 0 and g < 2):
                    act.wait_ge(s["diag_masked"], 2 * n - 2)
                act.wait_ge(s["max0_ready"], n + 1)
                for i in range(4):
                    last = act.activation(EX0[gp][:, i, :], ps[:, 2, i * P:(i + 1) * P], ACT.Exp, bias=nm[gp][:, 0, i:i + 1],
                                          accum_out=den[p][:, 0, 4 * g + i:4 * g + i + 1])
                last.then_inc(s["exp0_done"], 1)
                act.wait_ge(s["max1_ready"], n + 1)
                for i in range(4):
                    last = act.activation(EX1[gp][:, i, :], ps[:, 3 + i // 2, (i % 2) * S:(i % 2 + 1) * S], ACT.Exp, bias=nm[gp][:, 1, i:i + 1],
                                          accum_out=den[p][:, 1, 4 * g + i:4 * g + i + 1])
                last.then_inc(s["exp1_done"], 1)

            def sequence(b, p):
                if not (isinstance(b, int) and b < 2):
                    act.wait_ge(s["share_ready"], b - 1)
                copy_u(b, 0)
                copy_u(b, 1)
                exps1(b, 0, p)
                for g in range(1, 4):
                    if g < 3:
                        copy_u(b, g + 1)
                    exps1(b, g, p)

            sequence(0, 0)
            sequence(1, 1)
            with act.Fori(1, B // 2) as h:
                for p in range(2):
                    sequence(2 * h + p, p)

            def gelu1(e, p):
                act.wait_ge(s["e_hidden"], STEPS0 + e + 1)
                act.wait_ge(s["e_out"], STEPS0 + e - 1)
                act.activation(ex[p]["g"][:, :, :], ps[:, 2:6, 0:HALF], ACT.Gelu).then_inc(s["e_gelu"], 1)

            with act.Fori(0, E1 // 2) as h:
                for p in range(2):
                    gelu1(2 * h + p, p)

        @block.vector
        def _(dve):
            steps = [0]

            def then(ins):
                steps[0] += 1
                ins.then_inc(s["dve_step"], 1)
                dve.wait_ge(s["dve_step"], steps[0])

            def layer_norm(r, src, dst, ready, done):
                with dve.Fori(0, NT) as t:
                    dve.bn_stats(flat(stats[:, ds(t, 1), :]), flat(src[:, ds(t, 1), :])).then_inc(s["stats_taken"], 1)
                dve.wait_ge(s["stats_taken"], NT * (r + 1))
                me, mo, ve, vo = (stats[:, :, k] for k in (1, 4, 2, 5))
                dve.tensor_tensor(st[:, 0, :], me, mo, ALU.add).then_inc(s["dve_step"], 1)
                dve.tensor_tensor(st[:, 1, :], me, mo, ALU.subtract).then_inc(s["dve_step"], 1)
                steps[0] += 2
                then(dve.tensor_tensor(st[:, 2, :], ve, vo, ALU.add))
                then(dve.tensor_scalar(st[:, 0, :], st[:, 0, :], 0.5, None, ALU.mult))
                then(dve.scalar_tensor_tensor(out=st[:, 1, :], in0=st[:, 1, :], scalar=0.25, in1=st[:, 1, :], op0=ALU.mult, op1=ALU.mult))
                then(dve.scalar_tensor_tensor(out=st[:, 2, :], in0=st[:, 2, :], scalar=1.0 / D, in1=st[:, 1, :], op0=ALU.mult, op1=ALU.add))
                dve.tensor_scalar(st[:, 3, :], st[:, 2, :], EPS, None, ALU.add).then_inc(s["spread_ready"], 1)
                dve.wait_ge(s["root_ready"], r + 1)
                then(dve.reciprocal(st[:, 5, :], st[:, 4, :]))
                with dve.Fori(0, NT) as t:
                    dve.tensor_scalar(flat(dst[:, ds(t, 1), :]), flat(src[:, ds(t, 1), :]), st[:, 0, ds(t, 1)], st[:, 5, ds(t, 1)],
                                      ALU.subtract, ALU.mult).then_inc(s[ready], 1)
                dve.wait_ge(s[ready], done)

            dve.wait_ge(s["x_loaded"], 64)
            layer_norm(0, X, XN, "xn_ready", NT)
            layer_norm(1, XN, YN, "yn_ready", NT)
            dve.wait_ge(s["w_loaded"], 16 * W_LOADS)
            then(dve.tensor_tensor(HB[:, :, :], XN[:, :, :], bo[:, :].unsqueeze(1).broadcast_to([P, NT, D]), ALU.add))
            dve.wait_ge(s["w_turned"], 1)
            dve.tensor_copy(wqkv[0][:, :, :], ps_pv[:, 0, 0:3 * D].rearrange("p (t e) -> p t e", t=3)).then_inc(s["w_turned_copied"], 1)
            dve.tensor_copy(wg[1][:, :], ps_pv[:, 1, 0:E1]).then_inc(s["w_turned_copied"], 1)
            dve.tensor_copy(b1T[:, :], ps_pv[:, 1, E1:E1 + E0 * F0 // P]).then_inc(s["w_turned_copied"], 1)
            dve.wait_ge(s["consts_made"], 9)
            for dst, src in ((rev[:, :], revi[:, :]), (stepf[:, :], stepi[:, :]), (dump[:, :, :], dumpi[:, :, :]), (capb[:, :], capi[:, :])):
                then(dve.tensor_copy(dst, src))
            dve.wait_ge(s["rows_init"], 12)

            def attention(pas):
                q0 = JOBS // 8 * pas

                def turn(n, p):
                    dve.wait_ge(s["xt_turned"], n + 1)
                    if pas == 1:
                        dve.tensor_copy(xT[p][:, :], ps_m[:, 0, 0:S]).then_inc(s["xt_copied"], 1)
                    else:
                        dve.tensor_scalar(xT[p][:, :], ps_m[:, 0, 0:S], lnw[:, 0:1], lnw[:, 1:2], ALU.mult, ALU.add).then_inc(s["xt_copied"], 1)

                def split(n, j):
                    p = j % 2
                    dve.wait_ge(s["qkv_done"], n + 1)
                    for t, (hi, lo) in enumerate(((2, 0), (1, 3))):
                        src = ps_m[:, 1, t * S:(t + 1) * S]
                        if pas == 1:
                            dve.tensor_copy(nat[p][:, hi, :], src).then_inc(s["qk_split"], 1)
                            dve.wait_ge(s["qk_split"], 4 * n + 2 * t + 1)
                            dve.tensor_tensor(nat[p][:, lo, :], src, nat[p][:, hi, :].bitcast(F32), ALU.subtract).then_inc(s["qk_split"], 1)
                        else:
                            dve.tensor_scalar(nat[p][:, hi, :], src, bqk[:, t:t + 1], None, ALU.add).then_inc(s["qk_split"], 1)
                            dve.wait_ge(s["qk_split"], 4 * n + 2 * t + 1)
                            dve.scalar_tensor_tensor(out=nat[p][:, lo, :], in0=src, scalar=bqk[:, t:t + 1], in1=nat[p][:, hi, :].bitcast(F32),
                                                     op0=ALU.add, op1=ALU.subtract).then_inc(s["qk_split"], 1)
                    vsrc = ps_m[:, 0, S:2 * S].rearrange("p (k h e) -> p k h e", k=QT, h=HEADS)
                    for k in range(QT):
                        if pas == 1:
                            dve.tensor_copy(va[j][:, k, :, 0:HD], vsrc[:, k]).then_inc(s["v_copied"], 1)
                        else:
                            dve.tensor_tensor(va[j][:, k, :, 0:HD], vsrc[:, k], bv[:, :].rearrange("p (h e) -> p h e", h=HEADS), ALU.add).then_inc(s["v_copied"], 1)

                def reduce(n, p, u):
                    c, ip, sq = u // 4, u // 2 % 2, u % 2
                    dve.wait_ge(s["s_ready"], 8 * n + u + 1)
                    dve.tensor_reduce(negm[p][:, sq, :].rearrange("p (g i) -> p i g", i=4)[:, 2 * ip:2 * ip + 2, 2 * c:2 * c + 2],
                                      ps_s.rearrange("p b (g k) -> p b g k", g=2), AX.X, ALU.max, negate=True).then_inc(s["s_reduced"], 1)

                def copy_m(n, p):
                    dve.wait_ge(s["m_turned"], n + 1)
                    dve.tensor_copy(mT[p][:, :], ps_s[0:HEADS, 0, 0:S]).then_inc(s["m_copied"], 1)

                def normalise(n):
                    dve.wait_ge(s["ct_turned"], n + 1)
                    dve.reciprocal(rec[:, :], ps_m.rearrange("p b (k r) -> p (b k) r", r=32)[:, :, HD]).then_inc(s["rec_done"], 1)
                    dve.wait_ge(s["rec_done"], n + 1)
                    for k in range(QT):
                        wk = ps_m[:, k, :].rearrange("p (c i dg r) -> p c i dg r", c=2, i=4, dg=2)
                        rk = rec[:, 16 * k:16 * k + 16].rearrange("p (c i dg) -> p c i dg", c=2, i=4)
                        ok = o[:, k, :].rearrange("p (c dg i e) -> p c i dg e", i=4, c=2, dg=2)
                        for c in range(2):
                            dve.tensor_tensor(ok[:, c], wk[:, c, :, :, 0:HD], rk[:, c].unsqueeze(3).broadcast_to([P, 4, 2, HD]),
                                              ALU.mult).then_inc(s["o_ready"], 1)

                def add(n):
                    if pas == 0:
                        dve.wait_ge(s["wo_done"], n + 1)
                        h = HB[:, ds(2 * n, 2), :]
                        dve.tensor_tensor(h, ps_s[:, 1, S:2 * S].rearrange("p (k d) -> p k d", k=QT), h, ALU.add).then_inc(s["h_added"], 1)
                    else:
                        dve.wait_ge(s["o_ready"], 4 * n + 4)
                        x = X[:, ds(2 * n - 2 * B, 2), :]
                        dve.tensor_tensor(x, x, o[:, :, :], ALU.add).then_inc(s["x_added"], 1)
                        dve.wait_ge(s["x_added"], n - B + 1)

                for j in range(3):
                    turn(4 * q0 + j, j % 2)
                    split(4 * q0 + j, j)
                for j in range(2):
                    for u in range(UNITS):
                        reduce(4 * q0 + j, j, u)
                    copy_m(4 * q0 + j, j)

                def job(q, j, more):
                    n, p = 4 * q + j, j % 2
                    if more >= 2:
                        for u in range(UNITS):
                            reduce(n + 2, p, u)
                            if more >= 3 and u == 1:
                                turn(n + 3, 1 - p)
                            if more >= 3 and u == 3:
                                split(n + 3, (j + 3) % 4)
                        copy_m(n + 2, p)
                    normalise(n)
                    add(n)

                last = q0 + JOBS // 8 - 1
                with dve.Fori(q0, last) as q:
                    for j in range(4):
                        job(q, j, 3)
                for j in range(4):
                    job(last, j, 3 - j)

            attention(0)
            dve.wait_ge(s["h_added"], B)
            layer_norm(2, HB, YN, "yn_ready", 2 * NT)

            def all_tiles(ap):
                return ap.unsqueeze(1).broadcast_to([P, NT, ap.shape[-1]])

            def all_experts(ap, E):
                return ap.unsqueeze(2).broadcast_to([P, NT, E])

            def route(l):
                L, E = LAYER[l], LAYER[l]["E"]
                r0 = NT // 4 * l
                with dve.Fori(0, NT // 8) as i:
                    for p in range(2):
                        n = r0 + 2 * i + p
                        dve.wait_ge(s["rt_turned"], n + 1)
                        if l == 0:
                            dve.tensor_scalar(rT[p][:, :], ps[:, p, :], lnw[:, 2:3], lnw[:, 3:4], ALU.mult, ALU.add).then_inc(s["rt_copied"], 1)
                        else:
                            dve.tensor_copy(rT[p][:, :], ps[:, p, :]).then_inc(s["rt_copied"], 1)
                        dve.wait_ge(s["rt_logits"], n + 1)
                        dve.tensor_copy(LG[:, ds(8 * i + 4 * p, 4), 0:E], ps[:, 2 + p, 0:4 * E].rearrange("p (k e) -> p k e", k=4)).then_inc(s["rt_kept"], 1)
                dve.wait_ge(s["rt_kept"], r0 + NT // 4)

                lg, ta, tb, rk = (t[:, :, 0:E] for t in (LG, TA, TB, RK))
                revb = all_tiles(rev[:, E1 - E:E1])
                if l == 1:
                    dve.tensor_copy(tmp[:, 0, :], LG[:, :, 0]).then_inc(s["odds_ready"], 1)
                    dve.wait_ge(s["odds_ready"], 4)
                    then(dve.tensor_scalar(tb, ta, 1.0, None, ALU.add))
                    then(dve.reciprocal(lg, tb))
                for k in range(TOP):
                    then(dve.tensor_reduce(top[:, k, :], lg, AX.X, ALU.max))
                    then(dve.tensor_tensor(ta, lg, all_experts(top[:, k, :], E), ALU.is_equal))
                    then(dve.tensor_tensor(ta, ta, revb, ALU.mult))
                    then(dve.tensor_reduce(tj[:, k, :], ta, AX.X, ALU.max))
                    then(dve.tensor_tensor(OH[:, k, :, 0:E], revb, all_experts(tj[:, k, :], E), ALU.is_equal))
                    if k == 0:
                        then(dve.tensor_scalar(ta, OH[:, 0, :, 0:E], -1.0, 1.0, ALU.mult, ALU.add))
                        then(dve.tensor_tensor(lg, lg, ta, ALU.mult))
                        then(dve.scalar_tensor_tensor(out=lg, in0=OH[:, 0, :, 0:E], scalar=-3e38, in1=lg, op0=ALU.mult, op1=ALU.add))
                if l == 0:
                    dve.tensor_tensor(tmp[:, 0, :], top[:, 1, :], top[:, 0, :], ALU.subtract).then_inc(s["odds_ready"], 1)
                dve.tensor_tensor(rk, OH[:, 0, :, 0:E], OH[:, 1, :, 0:E], ALU.add).then_inc(s["sums_ready"], 1)
                dve.wait_ge(s["sums_ready"], 2 * l + 2)
                within = ps[:, 4, 0:NT * E].rearrange("p (t e) -> p t e", e=E)
                total = ps[:, 5, 0:NT * E].rearrange("p (t e) -> p t e", e=E)
                then(dve.tensor_copy(ta, total))
                a, b = ta, tb
                k = 1
                while k < NT:
                    dve.tensor_copy(b[:, 0:k, :], a[:, 0:k, :]).then_inc(s["dve_step"], 1)
                    steps[0] += 1
                    then(dve.tensor_tensor(b[:, k:NT, :], a[:, k:NT, :], a[:, 0:NT - k, :], ALU.add))
                    a, b, k = b, a, 2 * k
                then(dve.tensor_tensor(b, a, total, ALU.subtract))
                then(dve.tensor_tensor(rk, within, b, ALU.add))
                if l == 0:
                    then(dve.tensor_scalar(cnt[:, 0, :], a[:, NT - 1, :], float(SLOTS - 1), None, ALU.add))
                    then(dve.tensor_copy(cnti[:, :], cnt[:, 0, :]))
                    then(dve.tensor_scalar(cnti[:, :], cnti[:, :], SLOTS.bit_length() - 1, None, ALU.logical_shift_right))
                    then(dve.tensor_copy(cnt[:, 1, :], cnti[:, :]))
                    then(dve.tensor_copy(cnt[:, 2, :], cnt[:, 1, :]))
                    x, y, k = 2, 3, 1
                    while k < E:
                        then(dve.tensor_copy(cnt[:, y, 0:k], cnt[:, x, 0:k]))
                        then(dve.tensor_tensor(cnt[:, y, k:E], cnt[:, x, k:E], cnt[:, x, 0:E - k], ALU.add))
                        x, y, k = y, x, 2 * k
                    for e in range(E):
                        if e == 0:
                            then(dve.tensor_scalar(emapf[:, :], stepf[:, :], cnt[:, x, 0:1], None, ALU.is_ge))
                        else:
                            then(dve.scalar_tensor_tensor(out=emapf[:, :], in0=stepf[:, :], scalar=cnt[:, x, e:e + 1], in1=emapf[:, :],
                                                          op0=ALU.is_ge, op1=ALU.add))
                    then(dve.tensor_scalar(emap[:, :], emapf[:, :], float(E - 1), None, ALU.min))
                    then(dve.tensor_tensor(cnt[:, y, :], cnt[:, x, :], cnt[:, 1, :], ALU.subtract))
                    then(dve.tensor_scalar(cnt[:, y, :], cnt[:, y, :], float(SLOTS), None, ALU.mult))
                    then(dve.tensor_tensor(rk, rk, all_tiles(cnt[:, y, :]), ALU.add))
                else:
                    then(dve.tensor_scalar(tb if a is ta else ta, rk, float(CAP), None, ALU.is_lt))
                    ok = tb if a is ta else ta
                    spare = a
                    then(dve.tensor_tensor(rk, rk, all_tiles(capb[:, :]), ALU.add))
                for k in range(TOP):
                    w = tb if l == 0 else spare
                    then(dve.tensor_tensor(w, OH[:, k, :, 0:E], rk, ALU.mult))
                    then(dve.tensor_reduce(slot[:, k, :], w, AX.X, ALU.add))
                    if l == 1:
                        then(dve.tensor_tensor(w, OH[:, k, :, 0:E], ok, ALU.mult))
                        then(dve.tensor_reduce(tj[:, k, :], w, AX.X, ALU.add))
                        then(dve.tensor_tensor(tmp[:, 2, :], slot[:, k, :], dump[:, :, k], ALU.subtract))
                        then(dve.tensor_tensor(tmp[:, 2, :], tmp[:, 2, :], tj[:, k, :], ALU.mult))
                        then(dve.tensor_tensor(tmp[:, 2, :], tmp[:, 2, :], dump[:, :, k], ALU.add))
                        then(dve.tensor_copy(slot_to[:, k, :], tmp[:, 2, :]))
                        then(dve.tensor_tensor(slot[:, k, :], slot[:, k, :], tj[:, k, :], ALU.mult))
                    else:
                        then(dve.tensor_copy(slot_to[:, k, :], slot[:, k, :]))
                    then(dve.tensor_copy(slot_from[:, k, :], slot[:, k, :]))
                dve.tensor_copy(tmp[:, 3, :], top[:, 0, :]).then_inc(s["slots_ready"], 1)

                if l == 0:
                    dve.wait_ge(s["odds_ready"], 2)
                    then(dve.tensor_scalar(tmp[:, 2, :], tmp[:, 1, :], 1.0, None, ALU.add))
                    then(dve.reciprocal(tw[:, 0, :], tmp[:, 2, :]))
                    then(dve.tensor_tensor(tw[:, 1, :], tw[:, 0, :], tmp[:, 1, :], ALU.mult))
                else:
                    then(dve.tensor_tensor(tmp[:, 1, :], top[:, 0, :], top[:, 1, :], ALU.add))
                    then(dve.tensor_scalar(tmp[:, 1, :], tmp[:, 1, :], 1e-6, None, ALU.add))
                    then(dve.reciprocal(tmp[:, 2, :], tmp[:, 1, :]))
                    for k in range(TOP):
                        then(dve.tensor_tensor(tw[:, k, :], top[:, k, :], tmp[:, 2, :], ALU.mult))
                        then(dve.tensor_tensor(tw[:, k, :], tw[:, k, :], tj[:, k, :], ALU.mult))
                then(dve.tensor_copy(tmp[:, 0, :], tw[:, 0, :]))
                dve.tensor_copy(tmp[:, 1, :], tw[:, 1, :]).then_inc(s["weights_ready"], 1)
                dve.wait_ge(s["weights_ready"], l + 1)

            def combine(l):
                with dve.Fori(0, NT // 2) as h:
                    for n in range(4):
                        t, k = n // 2, n % 2
                        x = flat(X[:, ds(2 * h + t, 1), :])
                        dve.wait_ge(gathered[n], 16 * (NT // 2 * l + h + 1))
                        if k:
                            dve.wait_ge(s["combined"], TOP * NT * l + 4 * h + n)
                        dve.scalar_tensor_tensor(out=x, in0=got[n][:, :], scalar=tw[:, k, ds(2 * h + t, 1)], in1=x,
                                                 op0=ALU.mult, op1=ALU.add).then_inc(s["combined"], 1)
                dve.wait_ge(s["combined"], TOP * NT * (l + 1))

            route(0)
            attention(1)
            dve.wait_ge(s["x_added"], B)
            then(dve.tensor_tensor(X[:, :, :], X[:, :, :], HB[:, :, :], ALU.add))

            def turn0(i, p):
                dve.wait_ge(s["e_turned"], i + 1)
                if not isinstance(i, int) or i >= 2:
                    dve.wait_ge(s["e_hidden"], i - 1)
                dve.tensor_scalar(ex[p]["xT"][:, 0:SLOTS], ps[:, 4 + p, 0:SLOTS], lnw[:, 2:3], lnw[:, 3:4], ALU.mult, ALU.add).then_inc(s["e_copied"], 1)

            def add0(i, p, h):
                dve.wait_ge(s["e_out"], i + 1)
                if not isinstance(h, int) or h:
                    dve.wait_ge(e_stored[p], 16 * h)
                dve.tensor_tensor(ex[p]["y"][:, 0:2, :], ps[:, 6 + p, 0:SLOTS].rearrange("p (k d) -> p k d", k=2),
                                  ex[p]["b2"][:, :].unsqueeze(1).broadcast_to([P, 2, D]), ALU.add).then_inc(s["e_added"], 1)

            turn0(0, 0)
            turn0(1, 1)
            for p in range(2):
                turn0(2 + p, p)
                add0(p, p, 0)
            with dve.Fori(1, STEPS0 // 2 - 1) as h:
                for p in range(2):
                    turn0(2 * h + 2 + p, p)
                    add0(2 * h + p, p, h)
            add0(STEPS0 - 2, 0, STEPS0 // 2 - 1)
            add0(STEPS0 - 1, 1, STEPS0 // 2 - 1)
            combine(0)

            layer_norm(3, X, XN, "xn_ready", 2 * NT)
            route(1)

            def turn_l1(b, p):
                dve.wait_ge(s["u_ready"], 5 * b + 1)
                dve.tensor_copy(xT[p][:, :], ps_s[:, 0, 0:S]).then_inc(s["u_copied"], 1)

            def maxima(b, g):
                n, gp = 4 * b + g, g % 2
                if not (isinstance(n, int) and n < 2):
                    dve.wait_ge(s["exp1_done"], n - 1)
                dve.wait_ge(s["s0_ready"], n + 1)
                dve.tensor_reduce(nm[gp][:, 0, :], ps[:, 2, :].rearrange("p (i k) -> p i k", i=4), AX.X, ALU.max, negate=True).then_inc(s["max0_ready"], 1)
                dve.wait_ge(s["s1_ready"], n + 1)
                dve.tensor_reduce(nm[gp][:, 1, :], ps[:, 3:5, :].rearrange("p b (i k) -> p (b i) k", i=2), AX.X, ALU.max, negate=True).then_inc(s["max1_ready"], 1)

            def diagonal(b, g, p):
                n, gp = 4 * b + g, g % 2
                dve.wait_ge(s["diag_masked"], 2 * n + 2)
                dve.tensor_reduce(num[p][:, :, 4 * g:4 * g + 4], DG[gp][:, :, :, :], AX.X, ALU.add).then_inc(s["diag_summed"], 1)

            def shares(b, p):
                dve.wait_ge(s["exp1_done"], 4 * b + 4)
                dve.wait_ge(s["diag_summed"], 4 * b + 4)
                dve.reciprocal(share[p][:, :, :], den[p][:, :, :]).then_inc(s["rec_done"], 1)
                dve.wait_ge(s["rec_done"], JOBS + b + 1)
                dve.tensor_tensor(share[p][:, :, :], share[p][:, :, :], num[p][:, :, :], ALU.mult).then_inc(s["share_ready"], 1)
                dve.wait_ge(s["share_ready"], b + 1)

            def weigh(b, k, p):
                dve.wait_ge(s["v1_ready"], 2 * b + k + 1)
                dve.tensor_tensor(O1[:, :].rearrange("p (h v) -> p h v", h=HEADS), ps[:, 5:7, :].rearrange("p b (h v) -> p (b h) v", v=DV),
                                  share[p][:, k, :].unsqueeze(2).broadcast_to([P, HEADS, DV]), ALU.mult).then_inc(s["o1_ready"], 1)

            def copy_o(b, k):
                dve.wait_ge(s["o1_turned"], 2 * b + k + 1)
                dve.tensor_copy(O1T[:, :, :], ps[:, 5:7, :].rearrange("p b (c t) -> p (b c) t", t=P)).then_inc(s["o1_copied"], 1)

            def add_y(b, k):
                dve.wait_ge(s["y_ready"], 2 * b + k + 1)
                x = flat(X[:, ds(2 * b + k, 1), :])
                dve.tensor_tensor(x, ps[:, 7, 0:D], x, ALU.add).then_inc(s["y_added"], 1)

            def sequence(b, p, prev, nxt):
                maxima(b, 0)
                if prev:
                    diagonal(b - 1, 3, 1 - p)
                    shares(b - 1, 1 - p)
                    weigh(b - 1, 0, 1 - p)
                    copy_o(b - 1, 0)
                maxima(b, 1)
                diagonal(b, 0, p)
                if prev:
                    add_y(b - 1, 0)
                maxima(b, 2)
                if prev:
                    weigh(b - 1, 1, 1 - p)
                diagonal(b, 1, p)
                if nxt:
                    turn_l1(b + 1, 1 - p)
                if prev:
                    copy_o(b - 1, 1)
                maxima(b, 3)
                diagonal(b, 2, p)
                if prev:
                    add_y(b - 1, 1)

            turn_l1(0, 0)
            sequence(0, 0, False, True)
            with dve.Fori(0, B // 2 - 1) as h:
                for b, p in ((2 * h + 1, 1), (2 * h + 2, 0)):
                    sequence(b, p, True, True)
            sequence(B - 1, 1, True, False)
            diagonal(B - 1, 3, 1)
            shares(B - 1, 1)
            for k in range(QT):
                weigh(B - 1, k, 1)
                copy_o(B - 1, k)
                add_y(B - 1, k)
            dve.wait_ge(s["y_added"], QT * B)

            def turn1(e, p):
                dve.wait_ge(s["e_turned"], STEPS0 + e + 1)
                dve.tensor_copy(ex[p]["xT"][:, :], ps[:, 0:2, :].rearrange("p b n -> p (b n)")[:, 0:CAP]).then_inc(s["e_copied"], 1)

            def add1(e, p, h):
                dve.wait_ge(s["e_out"], STEPS0 + e + 1)
                dve.wait_ge(e_stored[p], 16 * (STEPS0 // 2) + 16 * h)
                dve.tensor_copy(ex[p]["y"][:, :, :], ps[:, 6:8, :].rearrange("p b (k d) -> p (b k) d", d=D)[:, 0:CT, :]).then_inc(s["e_added"], 1)

            turn1(0, 0)
            with dve.Fori(0, E1 // 2 - 1) as h:
                for p in range(2):
                    turn1(2 * h + p + 1, 1 - p)
                    add1(2 * h + p, p, h)
            turn1(E1 - 1, 1)
            add1(E1 - 2, 0, E1 // 2 - 1)
            add1(E1 - 1, 1, E1 // 2 - 1)
            combine(1)

        @block.tensor
        def _(pe):
            pe.wait_ge(s["ident_ready"], 1)
            pe.wait_ge(s["w_loaded"], 16 * W_LOADS)
            for t in range(3):
                pe.transpose(ps_pv[:, 0, t * D:(t + 1) * D], wraw[:, t, :], ident[:, :])
            pe.transpose(ps_pv[:, 1, 0:E1], wg1raw[:, :], ident[0:E1, 0:E1])
            nb = E0 * F0 // P
            pe.transpose(ps_pv[:, 1, E1:E1 + nb], b1raw[:, :], ident[0:nb, 0:nb]).then_inc(s["w_turned"], 1)
            pe.wait_ge(s["p_loaded"], 64)
            for raw, bank, ready in ((praw, 0, "pq_turned"), (kraw, 2, "pk_turned"), (oraw, 6, "po_turned")):
                for c in range(HEADS // 2):
                    last = pe.transpose(ps[:, bank + c // 4, (c % 4) * D:(c % 4 + 1) * D], raw[:, 2 * c:2 * c + 2, :].rearrange("p a k -> p (a k)"), ident[:, :])
                last.then_inc(s[ready], 1)
            pe.wait_ge(s["pq_copied"], 1)
            pe.wait_ge(s["pk_copied"], 1)
            for h in range(HEADS):
                r = slice(DK * (h % 2), DK * (h % 2) + DK)
                c = 8 * (h % 2) + h // 2
                last = pe.matmul(ps[:, c // 4, (c % 4) * D:(c % 4 + 1) * D], PkT[r, h // 2, :], PqT[r, h // 2, :], start=True, stop=True)
            last.then_inc(s["a_made"], 1)
            pe.wait_ge(s["w_turned_copied"], 3)
            pe.wait_ge(s["po_copied"], 1)
            pe.wait_ge(s["a_copied"], 1)

            def attention(pas):
                q0 = JOBS // 8 * pas
                n0 = 4 * q0

                def turn_x(q, j):
                    pe.wait_ge(xs_staged[j], 16 * q + 16)
                    for k in range(QT):
                        last = pe.transpose(ps_m[:, 0, k * P:(k + 1) * P], xs[j % 2][:, k, :], ident[:, :])
                    last.then_inc(s["xt_turned"], 1)

                def project(q, j):
                    w = wqkv[1 - pas]
                    pe.wait_ge(s["xt_copied"], 4 * q + j + 1)
                    for t in range(2):
                        pe.matmul(ps_m[:, 1, t * S:(t + 1) * S], w[:, t, :], xT[j % 2][:, :], start=True, stop=True)
                    for k in range(QT):
                        last = pe.matmul(ps_m[:, 0, S + k * P:S + (k + 1) * P], xT[j % 2][:, k * P:(k + 1) * P], w[:, 2, :], start=True, stop=True)
                    last.then_inc(s["qkv_done"], 1)

                def scores(n, j, u):
                    c, ip, sq = u // 4, u // 2 % 2, u % 2
                    if not (isinstance(n, int) and n == 0 and u == 0):
                        pe.wait_ge(s["s_reduced"], 8 * n + u)
                    for dg in range(2):
                        for di in range(2):
                            r = slice(32 * (2 * ip + di), 32 * (2 * ip + di) + 31)
                            last = pe.matmul(ps_s[:, di, dg * S:(dg + 1) * S], rows[j][r, 2 * c + dg, 0, sq * P:(sq + 1) * P],
                                             rows[j][r, 2 * c + dg, 1, :], start=True, stop=True)
                    last.then_inc(s["s_ready"], 1)

                def turn_m(n, p):
                    pe.wait_ge(s["s_reduced"], 8 * n + 8)
                    for k in range(QT):
                        last = pe.transpose(ps_s[0:HEADS, 0, k * P:(k + 1) * P], negm[p][:, k, :], ident[:, :])
                    last.then_inc(s["m_turned"], 1)

                def scores_t(n, j, u):
                    c, ip, kt = u // 4, u // 2 % 2, u % 2
                    if not (isinstance(n, int) and n == 0 and u == 0):
                        pe.wait_ge(s["exp_done"], 8 * n + u)
                    for dg in range(2):
                        for di in range(2):
                            r = slice(32 * (2 * ip + di), 32 * (2 * ip + di) + 32)
                            last = pe.matmul(ps_t[:, di, dg * S:(dg + 1) * S], rows[j][r, 2 * c + dg, 1, kt * P:(kt + 1) * P],
                                             rows[j][r, 2 * c + dg, 0, :], start=True, stop=True)
                    last.then_inc(s["st_ready"], 1)

                def values(n, j, u):
                    c, ip, kt = u // 4, u // 2 % 2, u % 2
                    pe.wait_ge(s["exp_done"], 8 * n + u + 1)
                    for x in range(4):
                        di, dg = x // 2, x % 2
                        last = pe.matmul(ps_pv[32 * x:32 * x + 32, c, ip * S:(ip + 1) * S], va[j][:, kt, 4 * (2 * c + dg) + 2 * ip + di, :],
                                         probs[:, u % 2, x, :], start=(kt == 0), stop=(kt == 1))
                    last.then_inc(s["pv_done"], 1)

                def turn_c(n, consumed):
                    pe.wait_ge(s["ct_copied"], n + 1)
                    pe.wait_ge(s["qk_split"], 4 * consumed)
                    pe.wait_ge(s["v_copied"], 2 * consumed)
                    for k in range(QT):
                        for blk in range(4):
                            last = pe.transpose(ps_m[:, k, blk * P:(blk + 1) * P], ctxT[:, blk, k * P:(k + 1) * P], ident[:, :])
                    last.then_inc(s["ct_turned"], 1)

                def output(n):
                    pe.wait_ge(s["o_ready"], 4 * n + 4)
                    for k in range(QT):
                        last = pe.transpose(ps_s[:, 1, k * P:(k + 1) * P], o[:, k, :], ident[:, :])
                    last.then_inc(s["ot_turned"], 1)
                    pe.wait_ge(s["ot_copied"], n + 1)
                    for k in range(QT):
                        last = pe.matmul(ps_s[:, 1, S + k * P:S + (k + 1) * P], oT[:, k * P:(k + 1) * P], wo[:, :], start=True, stop=True)
                    last.then_inc(s["wo_done"], 1)

                def job(q, j, more):
                    n, p = 4 * q + j, j % 2
                    first = isinstance(n, int) and n == 0
                    pe.wait_ge(m_sent[j], 64 * q + 64)
                    if more >= 2:
                        pe.wait_ge(rows_sent[(j + 2) % 4], 256 * (q + (j + 2) // 4) + 256)
                        pe.wait_ge(s["m_copied"], n + 2)
                        if pas == 0 and not first:
                            pe.wait_ge(s["h_added"], n)
                    for u in range(UNITS):
                        scores_t(n, j, u)
                        if more >= 2:
                            scores(n + 2, (j + 2) % 4, u)
                        if u:
                            values(n, j, u - 1)
                        elif not first:
                            pe.wait_ge(s["ct_copied"], n)
                        if more >= 3 and u == 1:
                            if not first:
                                pe.wait_ge(s["o_ready"], 4 * n)
                            turn_x(q + (j + 3) // 4, (j + 3) % 4)
                        if more >= 3 and u == 3:
                            project(q + (j + 3) // 4, (j + 3) % 4)
                    values(n, j, UNITS - 1)
                    if more >= 2:
                        turn_m(n + 2, p)
                    if more < 3:
                        pe.wait_ge(s["o_ready"], 4 * n)
                    turn_c(n, n + 4 if more >= 3 else n0 + JOBS // 2)
                    if pas == 0:
                        output(n)

                for j in range(3):
                    if j:
                        pe.wait_ge(s["qk_split"], 4 * (n0 + j))
                        pe.wait_ge(s["v_copied"], 2 * (n0 + j))
                    turn_x(q0, j)
                    project(q0, j)
                for j in range(2):
                    pe.wait_ge(rows_sent[j], 256 * q0 + 256)
                    if j:
                        pe.wait_ge(s["m_copied"], n0 + j)
                    for u in range(UNITS):
                        scores(n0 + j, j, u)
                    turn_m(n0 + j, j)
                last = q0 + JOBS // 8 - 1
                if pas == 0:
                    for j in range(4):
                        job(0, j, 3)
                with pe.Fori(q0 + 1 - pas, last) as q:
                    for j in range(4):
                        job(q, j, 3)
                for j in range(4):
                    job(last, j, 3 - j)

            def route(l):
                L, E = LAYER[l], LAYER[l]["E"]
                r0 = NT // 4 * l

                def pair(i):
                    for p in range(2):
                        n = r0 + 2 * i + p
                        pe.wait_ge(rt_staged[p], 16 * (NT // 8 * l + i) + 16)
                        if not (isinstance(i, int) and l == 0):
                            pe.wait_ge(s["rt_kept"], r0 + 2 * i)
                        for k in range(4):
                            last = pe.transpose(ps[:, p, k * P:(k + 1) * P], xr[p][:, k, :], ident[:, :])
                        last.then_inc(s["rt_turned"], 1)
                        pe.wait_ge(s["rt_copied"], n + 1)
                        for k in range(4):
                            last = pe.matmul(ps[:, 2 + p, k * E:(k + 1) * E], rT[p][:, k * P:(k + 1) * P], wg[l][:, :], start=True, stop=True)
                        last.then_inc(s["rt_logits"], 1)

                pair(0)
                with pe.Fori(1, NT // 8) as i:
                    pair(i)
                pe.wait_ge(s["sums_ready"], 2 * l + 1)
                chosen = RK[:, :, 0:E]
                pe.matmul(ps[:, 4, 0:NT * E], before[:, :], chosen, start=True, stop=True)
                pe.matmul(ps[:, 5, 0:NT * E], ones[:, :], chosen, start=True, stop=True).then_inc(s["sums_ready"], 1)

            pe.wait_ge(s["rows_init"], 12)
            attention(0)
            pe.wait_ge(s["h_added"], B)
            pe.wait_ge(s["consts_made"], 9)
            route(0)
            pe.wait_ge(s["slots_ready"], 1)
            attention(1)
            pe.wait_ge(s["x_added"], B)

            def turn(i, p, h):
                pe.wait_ge(x_in[p], 16 * h + 16)
                if not isinstance(i, int) or i >= 2:
                    pe.wait_ge(s["e_copied"], i - 1)
                for k in range(2):
                    last = pe.transpose(ps[:, 4 + p, k * P:(k + 1) * P], ex[p]["x"][:, k, :], ident[:, :])
                last.then_inc(s["e_turned"], 1)

            def hidden(i, p, h):
                pe.wait_ge(up_in[p], 32 * h + 32)
                pe.wait_ge(s["e_copied"], i + 1)
                if not isinstance(i, int) or i >= 2:
                    pe.wait_ge(s["e_gelu"], i - 1)
                for f in range(F0 // P):
                    last = pe.matmul(ps[:, 2 * p + f // 2, (f % 2) * SLOTS:(f % 2 + 1) * SLOTS], ex[p]["w1"][:, f * P:(f + 1) * P],
                                     ex[p]["xT"][:, 0:SLOTS], start=True, stop=True)
                last.then_inc(s["e_hidden"], 1)

            def result(i, p, h):
                pe.wait_ge(down_in[p], 32 * h + 32)
                pe.wait_ge(s["e_gelu"], i + 1)
                if not isinstance(i, int) or i >= 2:
                    pe.wait_ge(s["e_added"], i - 1)
                for k in range(2):
                    for f in range(F0 // P):
                        last = pe.matmul(ps[:, 6 + p, k * D:(k + 1) * D], ex[p]["g"][:, f, k * P:(k + 1) * P], ex[p]["w2"][:, f, :],
                                         start=(f == 0), stop=(f == F0 // P - 1))
                last.then_inc(s["e_out"], 1)

            turn(0, 0, 0)
            hidden(0, 0, 0)
            turn(1, 1, 0)

            def steps0(h):
                hidden(2 * h + 1, 1, h)
                turn(2 * h + 2, 0, h + 1)
                result(2 * h, 0, h)
                hidden(2 * h + 2, 0, h + 1)
                turn(2 * h + 3, 1, h + 1)
                result(2 * h + 1, 1, h)

            steps0(0)
            with pe.Fori(1, STEPS0 // 2 - 1) as h:
                steps0(h)
            half = STEPS0 // 2 - 1
            hidden(STEPS0 - 1, 1, half)
            result(STEPS0 - 2, 0, half)
            result(STEPS0 - 1, 1, half)

            route(1)
            pe.wait_ge(s["slots_ready"], 2)

            def turn_x1(b, p, h):
                if not (isinstance(b, int) and b == 0):
                    pe.wait_ge(s["u_copied"], 5 * b)
                pe.wait_ge(xs_staged[p], 16 * (JOBS // 4) + 16 * h + 16)
                for k in range(QT):
                    last = pe.transpose(ps_s[:, 0, k * P:(k + 1) * P], xs[p][:, k, :], ident[:, :])
                last.then_inc(s["u_ready"], 1)

            def keys(b, g, p):
                pe.wait_ge(s["u_copied"], 5 * b + g + 1)
                for i in range(4):
                    last = pe.matmul(ps_s[:, i // 2, (i % 2) * S:(i % 2 + 1) * S], AH[:, 4 * g + i, :], xT[p][:, :], start=True, stop=True)
                last.then_inc(s["u_ready"], 1)

            def scores1(b, g, p):
                n, gp = 4 * b + g, g % 2
                pe.wait_ge(s["u_copied"], 5 * b + g + 2)
                if not (isinstance(n, int) and n == 0):
                    pe.wait_ge(s["exp0_done"], n)
                pe.matmul(ps[:, 2, :], xT[p][:, 0:P], U[gp][:, :, 0:P], start=True, stop=False)
                pe.matmul(ps[:, 2, :], identb[:, :], tri0[:, :, :], start=False, stop=True).then_inc(s["s0_ready"], 1)
                if not (isinstance(n, int) and n == 0):
                    pe.wait_ge(s["exp1_done"], n)
                for x in range(2):
                    pe.matmul(ps[:, 3 + x, :], xT[p][:, P:2 * P], U[gp][:, 2 * x:2 * x + 2, :], start=True, stop=False)
                    last = pe.matmul(ps[:, 3 + x, :], identb[:, :], tri1[:, :, :], start=False, stop=True)
                last.then_inc(s["s1_ready"], 1)

            def values1(b, k, p):
                if not (isinstance(b, int) and b == 0 and k == 0):
                    pe.wait_ge(s["o1_copied"], 2 * b + k)
                for x in range(2):
                    last = pe.matmul(ps[:, 5 + x, :], xT[p][:, k * P:(k + 1) * P], Pv[:, x * 512:(x + 1) * 512], start=True, stop=True)
                last.then_inc(s["v1_ready"], 1)

            def turn_o(b, k):
                pe.wait_ge(s["o1_ready"], 2 * b + k + 1)
                for c in range(HEADS // 2):
                    last = pe.transpose(ps[:, 5 + c // 4, (c % 4) * P:(c % 4 + 1) * P], O1[:, c * P:(c + 1) * P], ident[:, :])
                last.then_inc(s["o1_turned"], 1)

            def output1(b, k):
                pe.wait_ge(s["o1_copied"], 2 * b + k + 1)
                if not (isinstance(b, int) and b == 0 and k == 0):
                    pe.wait_ge(s["y_added"], 2 * b + k)
                for c in range(HEADS // 2):
                    last = pe.matmul(ps[:, 7, 0:D], O1T[:, c, :], PoT[:, c, :], start=(c == 0), stop=(c == HEADS // 2 - 1))
                last.then_inc(s["y_ready"], 1)

            def sequence(b, p, h_next, prev, nxt):
                keys(b, 0, p)
                keys(b, 1, p)
                scores1(b, 0, p)
                if prev:
                    values1(b - 1, 0, 1 - p)
                keys(b, 2, p)
                if prev:
                    turn_o(b - 1, 0)
                scores1(b, 1, p)
                if prev:
                    output1(b - 1, 0)
                keys(b, 3, p)
                if prev:
                    values1(b - 1, 1, 1 - p)
                scores1(b, 2, p)
                if nxt:
                    turn_x1(b + 1, 1 - p, h_next)
                if prev:
                    turn_o(b - 1, 1)
                scores1(b, 3, p)
                if prev:
                    output1(b - 1, 1)

            turn_x1(0, 0, 0)
            sequence(0, 0, 0, False, True)
            with pe.Fori(0, B // 2 - 1) as h:
                sequence(2 * h + 1, 1, h + 1, True, True)
                sequence(2 * h + 2, 0, h + 1, True, True)
            sequence(B - 1, 1, 0, True, False)
            for k in range(QT):
                values1(B - 1, k, 1)
                turn_o(B - 1, k)
                output1(B - 1, k)

            pe.wait_ge(s["exp1_done"], 4 * B)
            half = STEPS0 // 2

            def turn_e(e, p, h):
                pe.wait_ge(x_in[p], 16 * half + 16 * h + 16)
                for k in range(CT):
                    last = pe.transpose(ps[:, k // 4, (k % 4) * P:(k % 4 + 1) * P], ex[p]["x"][:, k, :], ident[:, :])
                last.then_inc(s["e_turned"], 1)

            def hidden1(e, p, h):
                pe.wait_ge(up_in[p], 32 * half + 16 * h + 16)
                pe.wait_ge(s["e_copied"], STEPS0 + e + 1)
                pe.wait_ge(s["e_gelu"], STEPS0 + e)
                for f in range(F1 // P):
                    for c in range(2):
                        last = pe.matmul(ps[:, 2 + 2 * f + c, 0:HALF], ex[p]["w1"][:, f * P:(f + 1) * P], ex[p]["xT"][:, c * HALF:(c + 1) * HALF],
                                         start=True, stop=True)
                last.then_inc(s["e_hidden"], 1)

            def result1(e, p, h):
                pe.wait_ge(down_in[p], 32 * half + 16 * h + 16)
                pe.wait_ge(s["e_gelu"], STEPS0 + e + 1)
                pe.wait_ge(s["e_added"], STEPS0 + e)
                act_of = ex[p]["g"][:, :, :].rearrange("p (f c) n -> p f (c n)", c=2)
                for k in range(CT):
                    for f in range(F1 // P):
                        last = pe.matmul(ps[:, 6 + k // 4, (k % 4) * D:(k % 4 + 1) * D], act_of[:, f, k * P:(k + 1) * P], ex[p]["w2"][:, f, :],
                                         start=(f == 0), stop=(f == F1 // P - 1))
                last.then_inc(s["e_out"], 1)

            turn_e(0, 0, 0)
            with pe.Fori(0, E1 // 2 - 1) as h:
                for p in range(2):
                    hidden1(2 * h + p, p, h)
                    turn_e(2 * h + p + 1, 1 - p, h + p)
                    result1(2 * h + p, p, h)
            last_h = E1 // 2 - 1
            hidden1(E1 - 2, 0, last_h)
            turn_e(E1 - 1, 1, last_h)
            result1(E1 - 2, 0, last_h)
            hidden1(E1 - 1, 1, last_h)
            result1(E1 - 1, 1, last_h)


_INS = ["L0_attn_x", "L0_attn_Wq", "L0_attn_Wk", "L0_attn_Wv", "L0_ffn_ln1_w", "L0_ffn_ln1_b", "L0_ffn_ln2_w", "L0_ffn_ln2_b",
        "L0_ffn_w_qkv", "L0_ffn_b_qkv", "L0_ffn_w_o", "L0_ffn_b_o", "L0_ffn_w_gate", "L0_ffn_w1", "L0_ffn_b1", "L0_ffn_w2",
        "L0_ffn_b2", "L1_attn_P_q", "L1_attn_P_k", "L1_attn_P_v", "L1_attn_P_o", "L1_ffn_gate_w", "L1_ffn_w1", "L1_ffn_w2"]


def kernel(**inputs):
    import numpy as _np
    import concourse.bacc as _bacc
    from concourse import mybir as _mybir
    from concourse.bass_utils import run_bass_kernel_spmd as _run

    nc = _bacc.Bacc("TRN2", target_bir_lowering=False, num_devices=1)
    arrays, args = {}, {}
    for name in _INS:
        a = _np.ascontiguousarray(inputs[name])
        arrays[f"in_{name}_dram"] = a
        args[name] = nc.dram_tensor(f"in_{name}_dram", a.shape, _mybir.dt.from_np(a.dtype), kind="ExternalInput").ap()
    out = nc.dram_tensor("out_dram", args["L0_attn_x"].shape, _mybir.dt.float32, kind="ExternalOutput").ap()
    build(nc, args, out)
    r = _run(nc, [arrays], core_ids=[0])
    return r.results[0]["out_dram"]
```

```python
from contextlib import ExitStack

import concourse.bass as bass
from concourse import mybir

F32 = mybir.dt.float32
F32R = mybir.dt.float32r
BF16 = mybir.dt.bfloat16
I32 = mybir.dt.int32
U32 = mybir.dt.uint32
ALU = mybir.AluOpType
ACT = mybir.ActivationFunctionType
AX = mybir.AxisListType
ds = bass.ds

P = 128
EPS = 1e-5
NEVER = -1e38
W_LOADS = 17

SEMAPHORES = """
x_loaded w_loaded p_loaded moe_w_loaded ident_zero ident_ready consts_made zero_ready tables_zeroed dve_step
stats_taken spread_ready root_ready xn_ready yn_ready hb_ready
w_turned w_turned_copied pq_turned pq_copied pk_turned pk_copied a_made a_copied po_turned po_copied b1_turned b1_copied
xt_turned xt_copied qkv_done qk_split v_copied
s_ready s_reduced m_turned m_copied st_ready exp_done pv_done ct_copied ct_turned rec_done o_ready
ot_turned ot_copied wo_done h_added x_added rows_init
rt_turned rt_copied rt_logits rt_kept odds_ready sums_ready slots_ready weights_ready
scattered x_in0 x_in1 up_in0 up_in1 down_in0 down_in1 e_turned e_copied e_hidden e_gelu e_out e_added e_stored0 e_stored1
gathered0 gathered1 gathered2 gathered3 combined base_added
u_ready u_copied s0_ready s1_ready max0_ready max1_ready exp0_done exp1_done diag_masked diag_summed
share_ready v1_ready o1_ready o1_turned o1_copied y_ready y_added out_sent
""".split()


def build(nc, A, out):
    B, S, D = A["L0_attn_x"].shape
    NT = B * S // P
    QT = S // P
    HEADS = 16
    HD = D // HEADS
    GROUPS = 4
    UNITS = 8
    SCALE = 1.0 / float(HD) ** 0.5
    JOBS = 2 * B
    DK = A["L1_attn_P_q"].shape[2]
    DV = A["L1_attn_P_v"].shape[2]
    E0, _, F0 = A["L0_ffn_w1"].shape
    E1, _, F1 = A["L1_ffn_w1"].shape
    TOP = 2
    SLOTS = 256
    STEPS0 = NT * P * TOP // SLOTS + E0
    CAP = int(1.25 * NT * P * TOP / E1)
    CT = CAP // P
    ROWS0 = STEPS0 * SLOTS
    ROWS1 = E1 * CAP
    HALF = CAP // 2
    assert S == 256 and D == P and CAP % P == 0 and F0 == 512 and F1 == 256 and ROWS0 % P == 0

    with ExitStack() as ctx:
        def sb(name, shape, dt=F32, into=ctx):
            return into.enter_context(nc.sbuf_tensor(name, shape, dt))

        s = {n: ctx.enter_context(nc.semaphore(n)) for n in SEMAPHORES}
        rows_sent = [ctx.enter_context(nc.semaphore(f"rows_sent{j}")) for j in range(4)]
        m_sent = [ctx.enter_context(nc.semaphore(f"m_sent{j}")) for j in range(4)]
        xs_staged = [ctx.enter_context(nc.semaphore(f"xs_staged{j}")) for j in range(4)]
        x_in, up_in, down_in = ([s[f"{n}{p}"] for p in range(2)] for n in ("x_in", "up_in", "down_in"))
        e_stored = [s["e_stored0"], s["e_stored1"]]
        gathered = [s[f"gathered{k}"] for k in range(4)]

        xg = [nc.dram_tensor("xg0", (ROWS0, D), F32).ap(), nc.dram_tensor("xg1", (ROWS1 + NT * P * TOP, D), F32).ap()]
        yg = [nc.dram_tensor("yg0", (ROWS0, D), F32).ap(), nc.dram_tensor("yg1", (ROWS1, D), F32).ap()]

        X = sb("X", [P, NT, D])
        XN = sb("XN", [P, NT, D])
        YN = sb("YN", [P, NT, D])
        HB = sb("HB", [P, NT, D])
        stats = sb("stats", [P, NT, 6])
        st = sb("st", [P, 6, NT])
        ident = sb("ident", [P, P])
        identb = sb("identb", [P, P], BF16)
        ones = sb("ones", [P, P])
        before = sb("before", [P, P])
        tri0 = sb("tri0", [P, 4, P], BF16)
        tri1 = sb("tri1", [P, 2, 2 * P], BF16)
        wo = sb("wo", [P, D])
        lnw = sb("lnw", [P, 4])
        bqk = sb("bqk", [P, 2])
        bv = sb("bv", [P, D])
        bo = sb("bo", [P, D])
        wqkv = [sb(f"wqkv{a}", [P, 3, D]) for a in range(2)]
        b1T = sb("b1T", [P, E0 * F0 // P])
        b2all = sb("b2all", [P, E0, D])
        wg = [sb("wg0", [P, E0]), sb("wg1", [P, E1])]
        AH = sb("AH", [P, HEADS, D])
        PoT = sb("PoT", [P, HEADS // 2, D])
        Pv = sb("Pv", [P, HEADS * DV])
        xs = [sb(f"xs{a}", [P, QT, D]) for a in range(2)]
        xT = [sb(f"xT{a}", [P, S]) for a in range(2)]

        revi = sb("revi", [P, E1], I32)
        rev = sb("rev", [P, E1])
        stepi = sb("stepi", [P, STEPS0], I32)
        stepf = sb("stepf", [P, STEPS0])
        dumpi = sb("dumpi", [P, NT, TOP], I32)
        dump = sb("dump", [P, NT, TOP])
        capi = sb("capi", [P, E1], I32)
        capb = sb("capb", [P, E1])
        top = sb("top", [P, TOP, NT])
        tj = sb("tj", [P, TOP, NT])
        tw = sb("tw", [P, TOP, NT])
        tmp = sb("tmp", [P, 4, NT])
        slot = sb("slot", [P, TOP, NT])
        slot_to = sb("slot_to", [P, TOP, NT], I32)
        slot_from = sb("slot_from", [P, TOP, NT], I32)
        cnt = sb("cnt", [P, 4, E0])
        cnti = sb("cnti", [P, E0], I32)
        emapf = sb("emapf", [P, STEPS0])
        emap = sb("emap", [P, STEPS0], I32)

        def expert_buffers(into):
            return [dict(x=sb(f"ex{p}", [P, CT, D], F32, into), w1=sb(f"ew1{p}", [P, F0], F32, into),
                         w2=sb(f"ew2{p}", [P, F0 // P, D], F32, into), xT=sb(f"exT{p}", [P, CAP], F32, into),
                         y=sb(f"ey{p}", [P, CT, D], F32, into)) for p in range(2)]

        with ExitStack() as early:
            zeros = sb("zeros", [P, 2048], F32, early)
            wraw = sb("wraw", [P, 3, D], F32, early)
            b1raw = sb("b1raw", [E0 * F0 // P, P], F32, early)
            wg1raw = sb("wg1raw", [E1, D], F32, early)
            praw = sb("praw", [P, HEADS, DK], F32, early)
            kraw = sb("kraw", [P, HEADS, DK], F32, early)
            oraw = sb("oraw", [P, HEADS, DV], F32, early)
            PqT = sb("PqT", [P, HEADS // 2, D], F32, early)
            PkT = sb("PkT", [P, HEADS // 2, D], F32, early)
        with ExitStack() as routing:
            LG = sb("LG", [P, NT, E1], F32, routing)
            OH = sb("OH", [P, TOP, NT, E1], F32, routing)
            RK = sb("RK", [P, NT, E1], F32, routing)
            TA = sb("TA", [P, NT, E1], F32, routing)
            TB = sb("TB", [P, NT, E1], F32, routing)
            rT = [sb(f"rT{p}", [P, 4 * P], F32, routing) for p in range(2)]
        ex = expert_buffers(ctx)
        got = [sb(f"got{k}", [P, D]) for k in range(4)]

        with ExitStack() as first:
            nat = [sb(f"nat{a}", [P, 4, S], F32R, first) for a in range(2)]
            rows = [sb(f"rows{j}", [P, GROUPS, 2, S], F32R, first) for j in range(4)]
            va = [sb(f"va{j}", [P, QT, HEADS, 32], F32, first) for j in range(4)]
            negm = [sb(f"negm{a}", [P, QT, HEADS], F32, first) for a in range(2)]
            mT = [sb(f"mT{a}", [HEADS, S], F32R, first) for a in range(2)]
            probs = sb("probs", [P, 2, 4, S], F32, first)
            ctxT = sb("ctxT", [P, 4, S], F32, first)
            rec = sb("rec", [P, 2 * HEADS], F32, first)
            o = sb("o", [P, QT, D], F32, first)
            oT = sb("oT", [P, S], F32, first)
        for p in range(2):
            ex[p]["g"] = sb(f"eg{p}", [P, 4, HALF])
        U = [sb(f"U{p}", [P, 4, S]) for p in range(2)]
        EX0 = [sb(f"EX0{p}", [P, 4, P]) for p in range(2)]
        EX1 = [sb(f"EX1{p}", [P, 4, S]) for p in range(2)]
        DG = [sb(f"DG{p}", [P, 2, 4, P]) for p in range(2)]
        nm = [sb(f"nm{p}", [P, 2, 4]) for p in range(2)]
        den = [sb(f"den{p}", [P, QT, HEADS]) for p in range(2)]
        num = [sb(f"num{p}", [P, QT, HEADS]) for p in range(2)]
        share = [sb(f"share{p}", [P, QT, HEADS]) for p in range(2)]
        O1 = sb("O1", [P, HEADS * DV])
        O1T = sb("O1T", [P, HEADS // 2, P])

        ps = ctx.enter_context(nc.psum_tensor("ps", [P, 8, 512], F32))
        ps_s, ps_t, ps_pv, ps_m = ps[:, 0:2, :], ps[:, 2:4, :], ps[:, 4:6, :], ps[:, 6:8, :]

        def flat(ap):
            return ap.rearrange("p a d -> p (a d)")

        block = ctx.enter_context(nc.Block())

        @block.sync
        def _(sp):
            xv = A["L0_attn_x"].rearrange("b (q p) d -> p (b q) d", p=P)
            step = NT // 4
            for i in range(4):
                sp.dma_start(X[:, i * step:(i + 1) * step, :], xv[:, i * step:(i + 1) * step, :]).then_inc(s["x_loaded"], 16)
            loads = [(wraw[:, i, :], A[n]) for i, n in enumerate(("L0_attn_Wq", "L0_attn_Wk", "L0_attn_Wv"))]
            loads += [(wqkv[1][:, :, :], A["L0_ffn_w_qkv"].rearrange("d (t e) -> d t e", t=3)), (wo[:, :], A["L0_ffn_w_o"])]
            loads += [(lnw[:, i:i + 1], A[n].rearrange("(d a) -> d a", a=1))
                      for i, n in enumerate(("L0_ffn_ln1_w", "L0_ffn_ln1_b", "L0_ffn_ln2_w", "L0_ffn_ln2_b"))]
            loads += [(bqk[:, t:t + 1], A["L0_ffn_b_qkv"][t * D:(t + 1) * D].rearrange("(e a) -> e a", a=1)) for t in range(2)]
            loads += [(bv[:, :], A["L0_ffn_b_qkv"][2 * D:3 * D].rearrange("(a e) -> a e", a=1).broadcast_to([P, D])),
                      (bo[:, :], A["L0_ffn_b_o"].rearrange("(a e) -> a e", a=1).broadcast_to([P, D])),
                      (b2all[:, :, :], A["L0_ffn_b2"].rearrange("(a e) d -> a e d", a=1).broadcast_to([P, E0, D])),
                      (b1raw[:, :], A["L0_ffn_b1"].rearrange("e (f p) -> (e f) p", p=P)),
                      (wg[0][:, :], A["L0_ffn_w_gate"]), (wg1raw[:, :], A["L1_ffn_gate_w"])]
            for dst, src in loads:
                sp.dma_start(dst, src).then_inc(s["w_loaded"], 16)
            assert len(loads) == W_LOADS
            for dst, n in ((praw, "L1_attn_P_q"), (kraw, "L1_attn_P_k"), (oraw, "L1_attn_P_o")):
                sp.dma_start(dst[:, :, :], A[n].rearrange("h d k -> d h k")).then_inc(s["p_loaded"], 16)
            sp.dma_start(Pv[:, :].rearrange("d (h v) -> d h v", h=HEADS), A["L1_attn_P_v"].rearrange("h d v -> d h v")).then_inc(s["p_loaded"], 16)
            sp.wait_ge(s["zero_ready"], 1)
            for table, n in ((xg[0], ROWS0), (xg[1], ROWS1)):
                v = table[0:n, :].rearrange("(p r) c -> p (r c)", p=P)
                for c in range(0, n, 2048):
                    sp.dma_start(v[:, c:c + 2048], zeros[:, :]).then_inc(s["tables_zeroed"], 16)

            def stage(pas, q, j):
                q, j = q + j // 4, j % 4
                src = (YN, XN)[pas]
                if not isinstance(q, int) or 4 * q + j >= 2:
                    sp.wait_ge(s["xt_turned"], 4 * q + j - 1)
                sp.dma_start(xs[j % 2][:, :, :], src[:, ds(8 * q + 2 * j - 2 * B * pas, 2), :]).then_inc(xs_staged[j], 16)

            def send_rows(q, j):
                q, j = q + j // 4, j % 4
                sp.wait_ge(s["qk_split"], 16 * q + 4 * j + 4)
                for g in range(GROUPS):
                    for role, part, side, m in ((0, 2, 0, 1), (0, 1, 1, 1), (1, 0, 0, 2), (2, 2, 0, 2)):
                        sp.dma_start(rows[j][role:P:4, g, side:side + m, :].bitcast(F32),
                                     nat[j % 2][32 * g:32 * g + 32, part:part + m, :].bitcast(F32)).then_inc(rows_sent[j], 16)

            def send_m(q, j):
                q, j = q + j // 4, j % 4
                sp.wait_ge(s["m_copied"], 4 * q + j + 1)
                for g in range(GROUPS):
                    sp.dma_start(rows[j][31:P:32, g, 0, :].bitcast(F32), mT[j % 2][4 * g:4 * g + 4, :].bitcast(F32)).then_inc(m_sent[j], 16)

            def attention(pas):
                q0 = JOBS // 8 * pas
                stage(pas, q0, 0)
                stage(pas, q0, 1)
                if pas == 0:
                    sp.wait_ge(s["rows_init"], 12)
                send_rows(q0, 0)
                stage(pas, q0, 2)
                send_rows(q0, 1)
                stage(pas, q0, 3)
                send_rows(q0, 2)
                send_m(q0, 0)

                def job(q, j, more):
                    send_m(q, j + 1)
                    if more >= 4:
                        stage(pas, q, j + 4)
                    if more >= 3:
                        send_rows(q, j + 3)

                last = q0 + JOBS // 8 - 1
                job(q0, 0, 4)
                with sp.Fori(q0, last - 1) as q:
                    for j in range(1, 5):
                        job(q, j, 4)
                for j, more in ((1, 4), (2, 4), (3, 4), (4, 3), (5, 2), (6, 1)):
                    job(last - 1, j, more)

            sp.wait_ge(s["yn_ready"], NT)
            attention(0)
            sp.wait_ge(s["yn_ready"], 2 * NT)
            attention(1)

            sp.wait_ge(s["scattered"], 16 * NT * TOP)
            sp.wait_ge(s["weights_ready"], 1)

            def load_x(i, p):
                sp.dma_start(ex[p]["x"][:, 0:2, :], xg[0][ds(i * SLOTS, SLOTS), :].rearrange("(k p) d -> p k d", p=P)).then_inc(x_in[p], 16)

            def load_up(e, p):
                sp.dma_start(ex[p]["w1"][:, :], A["L0_ffn_w1"][ds(e, 1), :, :].rearrange("a d f -> d (a f)")).then_inc(up_in[p], 16)

            def load_down(e, p):
                sp.dma_start(ex[p]["w2"][:, :, :], A["L0_ffn_w2"][ds(e, 1), :, :].rearrange("a (f p) d -> p (a f) d", p=P)).then_inc(down_in[p], 16)

            def expert_of(i):
                return sp.value_load(emap[0:1, ds(i, 1)], min_val=0, max_val=E0 - 1)

            def store_step(i, p):
                sp.wait_ge(s["e_added"], i + 1)
                sp.dma_start(yg[0][ds(i * SLOTS, SLOTS), :].rearrange("(k p) d -> p k d", p=P), ex[p]["y"][:, 0:2, :]).then_inc(e_stored[p], 16)

            for i in range(2):
                e = expert_of(i)
                load_x(i, i)
                load_up(e, i)
                load_down(e, i)

            def next_loads(i, p, up=True, x=True, down=True):
                if up:
                    e = expert_of(i + 2)
                    sp.wait_ge(s["e_hidden"], i + 1)
                    load_up(e, p)
                e = expert_of(i + 1)
                store_step(i - 1, 1 - p)
                if x:
                    load_x(i + 3, 1 - p)
                if down:
                    load_down(e, 1 - p)

            e = expert_of(2)
            sp.wait_ge(s["e_hidden"], 1)
            load_x(2, 0)
            load_up(e, 0)
            sp.wait_ge(s["e_turned"], 2)
            load_x(3, 1)
            with sp.Fori(0, STEPS0 // 2 - 2) as h:
                for p in (1, 0):
                    next_loads(2 * h + 2 - p, p)
            next_loads(STEPS0 - 3, 1, x=False)
            next_loads(STEPS0 - 2, 0, up=False, x=False)
            store_step(STEPS0 - 2, 0)
            store_step(STEPS0 - 1, 1)

            sp.wait_ge(s["xn_ready"], 2 * NT)

            def stage1(b, p):
                if not isinstance(b, int):
                    sp.wait_ge(s["u_ready"], 5 * b - 9)
                sp.dma_start(xs[p][:, :, :], XN[:, ds(2 * b, 2), :]).then_inc(xs_staged[p], 16)

            stage1(0, 0)
            stage1(1, 1)
            with sp.Fori(0, B // 2 - 1) as h:
                for p in range(2):
                    stage1(2 * h + p + 2, p)

            sp.wait_ge(s["scattered"], 32 * NT * TOP)

            def load_tokens(e, p):
                sp.dma_start(ex[p]["x"][:, :, :], xg[1][ds(e * CAP, CAP), :].rearrange("(k p) d -> p k d", p=P)).then_inc(x_in[p], 16)

            def load_w1(e, p):
                sp.dma_start(ex[p]["w1"][:, 0:F1], A["L1_ffn_w1"][ds(e, 1), :, :].rearrange("a d f -> d (a f)")).then_inc(up_in[p], 16)

            def load_w2(e, p):
                sp.dma_start(ex[p]["w2"][:, 0:F1 // P, :], A["L1_ffn_w2"][ds(e, 1), :, :].rearrange("a (f p) d -> p (a f) d", p=P)).then_inc(down_in[p], 16)

            def store_expert(e, p):
                sp.wait_ge(s["e_added"], STEPS0 + e + 1)
                sp.dma_start(yg[1][ds(e * CAP, CAP), :].rearrange("(k p) d -> p k d", p=P), ex[p]["y"][:, :, :]).then_inc(e_stored[p], 16)

            for e in range(2):
                load_tokens(e, e)
                load_w1(e, e)
                load_w2(e, e)
            with sp.Fori(0, E1 // 2 - 1) as h:
                for p in range(2):
                    e = 2 * h + p
                    sp.wait_ge(s["e_turned"], STEPS0 + e + 1)
                    load_tokens(e + 2, p)
                    sp.wait_ge(s["e_hidden"], STEPS0 + e + 1)
                    load_w1(e + 2, p)
                    store_expert(e, p)
                    load_w2(e + 2, p)
            store_expert(E1 - 2, 0)
            store_expert(E1 - 1, 1)

            ov = out.rearrange("b (q p) d -> p (b q) d", p=P)
            for i in range(4):
                sp.wait_ge(s["combined"], TOP * NT + TOP * step * (i + 1))
                sp.dma_start(ov[:, i * step:(i + 1) * step, :], X[:, i * step:(i + 1) * step, :]).then_inc(s["out_sent"], 16)
            sp.wait_ge(s["out_sent"], 64)

        @block.gpsimd
        def _(pool):
            pool.memset(ident[:, :], 0.0).then_inc(s["ident_zero"], 1)
            pool.memset(before[:, :], 1.0).then_inc(s["ident_zero"], 1)
            pool.memset(tri0[:, :, :], 0.0).then_inc(s["ident_zero"], 1)
            pool.memset(tri1[:, :, :], 0.0).then_inc(s["ident_zero"], 1)
            pool.wait_ge(s["ident_zero"], 4)
            pool.affine_select(out=ident[:, :], in_=ident[:, :], compare_op=ALU.not_equal, fill=1.0, base=0,
                               pattern=[[-1, P]], channel_multiplier=1).then_inc(s["ident_ready"], 1)
            pool.memset(zeros[:, :], 0.0).then_inc(s["zero_ready"], 1)
            pool.affine_select(out=before[:, :], in_=before[:, :], compare_op=ALU.is_gt, fill=0.0, base=0,
                               pattern=[[1, P]], channel_multiplier=-1).then_inc(s["consts_made"], 1)
            pool.affine_select(out=tri0[:, :, :], in_=tri0[:, :, :], compare_op=ALU.is_ge, fill=NEVER, base=0,
                               pattern=[[0, 4], [-1, P]], channel_multiplier=1).then_inc(s["consts_made"], 1)
            pool.affine_select(out=tri1[:, :, :], in_=tri1[:, :, :], compare_op=ALU.is_ge, fill=NEVER, base=P,
                               pattern=[[0, 2], [-1, 2 * P]], channel_multiplier=1).then_inc(s["consts_made"], 1)
            pool.memset(ones[:, :], 1.0).then_inc(s["consts_made"], 1)
            pool.iota(revi[:, :], pattern=[[-1, E1]], base=E1, channel_multiplier=0).then_inc(s["consts_made"], 1)
            pool.iota(stepi[:, :], pattern=[[1, STEPS0]], base=0, channel_multiplier=0).then_inc(s["consts_made"], 1)
            pool.iota(dumpi[:, :, :], pattern=[[P * TOP, NT], [1, TOP]], base=ROWS1, channel_multiplier=TOP).then_inc(s["consts_made"], 1)
            pool.iota(capi[:, :], pattern=[[CAP, E1]], base=0, channel_multiplier=0).then_inc(s["consts_made"], 1)
            for j in range(4):
                pool.memset(rows[j][:, :, 0, :].bitcast(F32), 0.0).then_inc(s["rows_init"], 1)
                pool.memset(rows[j][:, :, 1, :].bitcast(F32), 1.0).then_inc(s["rows_init"], 1)
                pool.memset(va[j][:, :, :, :], 0.0).then_inc(s["ident_zero"], 1)
                pool.wait_ge(s["ident_zero"], 5 + j)
                pool.memset(va[j][:, :, :, HD:HD + 1], 1.0).then_inc(s["rows_init"], 1)

            def scatter(l, rows_of, n):
                t, k = n // TOP, n % TOP
                pool.indirect_dma_start(
                    out=xg[l], out_offset=bass.IndirectOffsetOnAxis(ap=slot_to[:, k, t:t + 1].bitcast(U32), axis=0),
                    in_=rows_of[:, t, :], in_offset=None).then_inc(s["scattered"], 16)

            def gather(l):
                for t in range(NT):
                    for k in range(TOP):
                        n = TOP * t + k
                        if n >= 4:
                            pool.wait_ge(s["combined"], TOP * NT * l + n - 3)
                        pool.indirect_dma_start(
                            out=got[n % 4][:, :], out_offset=None, in_=yg[l],
                            in_offset=bass.IndirectOffsetOnAxis(ap=slot_from[:, k, t:t + 1].bitcast(U32), axis=0)).then_inc(gathered[n % 4], 16)

            pool.wait_ge(s["tables_zeroed"], 160)
            pool.wait_ge(s["slots_ready"], 1)
            for n in range(TOP * NT):
                scatter(0, YN, n)
            for p in range(2):
                pool.wait_ge(e_stored[p], 16 * (STEPS0 // 2))
            gather(0)
            pool.wait_ge(s["slots_ready"], 2)

            def diagonal(n, p):
                pool.wait_ge(s["exp0_done"], n + 1)
                if not (isinstance(n, int) and n < 2):
                    pool.wait_ge(s["diag_summed"], n - 1)
                eye = ident[:, :].unsqueeze(1).broadcast_to([P, 4, P])
                pool.tensor_tensor(DG[p][:, 0], EX0[p][:, :, :], eye, ALU.mult).then_inc(s["diag_masked"], 1)
                pool.wait_ge(s["exp1_done"], n + 1)
                pool.tensor_tensor(DG[p][:, 1], EX1[p][:, :, P:2 * P], eye, ALU.mult).then_inc(s["diag_masked"], 1)

            for n in range(4 * B):
                diagonal(n, n % 2)
                scatter(1, XN, n)

            for p in range(2):
                pool.wait_ge(e_stored[p], 16 * (STEPS0 // 2 + E1 // 2))
            gather(1)

        @block.scalar
        def _(act):
            def root(r):
                act.wait_ge(s["spread_ready"], r + 1)
                act.activation(st[:, 4, :], st[:, 3, :], ACT.Sqrt).then_inc(s["root_ready"], 1)

            act.wait_ge(s["ident_ready"], 1)
            act.activation(identb[:, :], ident[:, :], ACT.Copy).then_inc(s["consts_made"], 1)
            root(0)
            root(1)
            act.wait_ge(s["pq_turned"], 1)
            act.activation(PqT[:, :, :], ps_s.rearrange("p b (c d) -> p (b c) d", d=D), ACT.Copy).then_inc(s["pq_copied"], 1)
            act.wait_ge(s["pk_turned"], 1)
            act.activation(PkT[:, :, :], ps_t.rearrange("p b (c d) -> p (b c) d", d=D), ACT.Copy).then_inc(s["pk_copied"], 1)
            act.wait_ge(s["po_turned"], 1)
            act.activation(PoT[:, :, :], ps_m.rearrange("p b (c d) -> p (b c) d", d=D), ACT.Copy).then_inc(s["po_copied"], 1)
            act.wait_ge(s["a_made"], 1)
            act.activation(AH[:, :, :].rearrange("p (c a) d -> p a c d", a=2), ps[:, 0:4, :].rearrange("p (a b) (c d) -> p a (b c) d", a=2, d=D), ACT.Copy, scale=float(DK) ** 0.5).then_inc(s["a_copied"], 1)

            def exps(n, u, skip=False):
                act.wait_ge(s["st_ready"], 8 * n + u + 1)
                if not skip:
                    act.wait_ge(s["pv_done"], 8 * n + u - 1)
                act.activation(probs[:, u % 2, :, :], ps_t.rearrange("p b (g q) -> p (b g) q", g=2), ACT.Exp,
                               scale=SCALE).then_inc(s["exp_done"], 1)

            def attention(pas):
                q0 = JOBS // 8 * pas

                def copy_o(n):
                    act.wait_ge(s["ot_turned"], n + 1)
                    act.activation(oT[:, :], ps_m[:, 0, 0:S], ACT.Copy).then_inc(s["ot_copied"], 1)

                def job(n, first=False, new=False):
                    for u in range(UNITS):
                        exps(n, u, new and u < 2)
                        if pas == 0 and not first and u == UNITS - 2:
                            copy_o(n - 1)
                    act.wait_ge(s["pv_done"], 8 * n + 8)
                    if not new:
                        act.wait_ge(s["ct_turned"], n)
                    act.activation(ctxT[:, :, :], ps_pv.rearrange("p b (c q) -> p (b c) q", c=2), ACT.Copy).then_inc(s["ct_copied"], 1)

                n0 = 4 * q0
                job(n0, True, pas == 0)
                with act.Fori(q0, q0 + JOBS // 8 - 1) as q:
                    for j in range(1, 5):
                        job(4 * q + j)
                for n in range(n0 + JOBS // 2 - 3, n0 + JOBS // 2):
                    job(n)
                if pas == 0:
                    copy_o(n0 + JOBS // 2 - 1)

            def route(l):
                for n in range(NT // 4):
                    act.wait_ge(s["rt_turned"], NT // 4 * l + n + 1)
                    if n >= 2:
                        act.wait_ge(s["rt_logits"], NT // 4 * l + n - 1)
                    if l == 0:
                        act.activation(rT[n % 2][:, :], ps[:, n % 2, :], ACT.Identity, scale=lnw[:, 2:3], bias=lnw[:, 3:4]).then_inc(s["rt_copied"], 1)
                    else:
                        act.activation(rT[n % 2][:, :], ps[:, n % 2, :], ACT.Copy).then_inc(s["rt_copied"], 1)

            attention(0)
            root(2)
            route(0)
            act.wait_ge(s["odds_ready"], 1)
            act.activation(tmp[:, 1, :], tmp[:, 0, :], ACT.Exp).then_inc(s["odds_ready"], 1)
            attention(1)

            def gelu0(i, p):
                e = act.value_load(emap[0:1, ds(i, 1)], min_val=0, max_val=E0 - 1)
                act.wait_ge(s["e_hidden"], i + 1)
                if not isinstance(i, int) or i >= 2:
                    act.wait_ge(s["e_out"], i - 1)
                for f in range(F0 // P):
                    last = act.activation(ex[p]["g"][:, f, 0:SLOTS], ps[:, 2 * p + f // 2, (f % 2) * SLOTS:(f % 2 + 1) * SLOTS],
                                          ACT.Gelu_apprx_tanh, bias=b1T[:, ds(e * (F0 // P) + f, 1)])
                last.then_inc(s["e_gelu"], 1)

            act.wait_ge(s["weights_ready"], 1)
            gelu0(0, 0)
            gelu0(1, 1)
            with act.Fori(1, STEPS0 // 2) as h:
                for p in range(2):
                    gelu0(2 * h + p, p)

            root(3)
            route(1)
            act.wait_ge(s["odds_ready"], 3)
            act.activation(TA[:, :, :], LG[:, :, :], ACT.Exp, scale=-1.0).then_inc(s["odds_ready"], 1)

            def copy_u(b, g):
                if not (isinstance(b, int) and b == 0 and g < 2):
                    act.wait_ge(s["s1_ready"], 4 * b + g - 1)
                act.wait_ge(s["u_ready"], 5 * b + g + 2)
                act.activation(U[g % 2][:, :, :], ps_s.rearrange("p b (c q) -> p (b c) q", c=2), ACT.Copy).then_inc(s["u_copied"], 1)

            def exps1(b, g, p):
                n, gp = 4 * b + g, g % 2
                if not (isinstance(b, int) and b == 0 and g < 2):
                    act.wait_ge(s["diag_masked"], 2 * n - 2)
                act.wait_ge(s["max0_ready"], n + 1)
                for i in range(4):
                    last = act.activation(EX0[gp][:, i, :], ps[:, 2, i * P:(i + 1) * P], ACT.Exp, bias=nm[gp][:, 0, i:i + 1],
                                          accum_out=den[p][:, 0, 4 * g + i:4 * g + i + 1])
                last.then_inc(s["exp0_done"], 1)
                act.wait_ge(s["max1_ready"], n + 1)
                for i in range(4):
                    last = act.activation(EX1[gp][:, i, :], ps[:, 3 + i // 2, (i % 2) * S:(i % 2 + 1) * S], ACT.Exp, bias=nm[gp][:, 1, i:i + 1],
                                          accum_out=den[p][:, 1, 4 * g + i:4 * g + i + 1])
                last.then_inc(s["exp1_done"], 1)

            def sequence(b, p):
                if not (isinstance(b, int) and b < 2):
                    act.wait_ge(s["share_ready"], b - 1)
                copy_u(b, 0)
                copy_u(b, 1)
                exps1(b, 0, p)
                for g in range(1, 4):
                    if g < 3:
                        copy_u(b, g + 1)
                    exps1(b, g, p)

            sequence(0, 0)
            sequence(1, 1)
            with act.Fori(1, B // 2) as h:
                for p in range(2):
                    sequence(2 * h + p, p)

            def gelu1(e, p):
                act.wait_ge(s["e_hidden"], STEPS0 + e + 1)
                act.wait_ge(s["e_out"], STEPS0 + e - 1)
                act.activation(ex[p]["g"][:, :, :], ps[:, 2:6, 0:HALF], ACT.Gelu).then_inc(s["e_gelu"], 1)

            with act.Fori(0, E1 // 2) as h:
                for p in range(2):
                    gelu1(2 * h + p, p)

        @block.vector
        def _(dve):
            steps = [0]

            def then(ins):
                steps[0] += 1
                ins.then_inc(s["dve_step"], 1)
                dve.wait_ge(s["dve_step"], steps[0])

            def take_stats(src, t):
                dve.bn_stats(flat(stats[:, ds(t, 1), :]), flat(src[:, ds(t, 1), :])).then_inc(s["stats_taken"], 1)

            def layer_norm(r, src, dst, ready, done, taken=False):
                if not taken:
                    with dve.Fori(0, NT // 8) as h:
                        for k in range(8):
                            take_stats(src, 8 * h + k)
                dve.wait_ge(s["stats_taken"], NT * (r + 1))
                me, mo, ve, vo = (stats[:, :, k] for k in (1, 4, 2, 5))
                dve.tensor_tensor(st[:, 0, :], me, mo, ALU.add).then_inc(s["dve_step"], 1)
                dve.tensor_tensor(st[:, 1, :], me, mo, ALU.subtract).then_inc(s["dve_step"], 1)
                steps[0] += 2
                then(dve.tensor_tensor(st[:, 2, :], ve, vo, ALU.add))
                then(dve.tensor_scalar(st[:, 0, :], st[:, 0, :], 0.5, None, ALU.mult))
                then(dve.scalar_tensor_tensor(out=st[:, 1, :], in0=st[:, 1, :], scalar=0.25, in1=st[:, 1, :], op0=ALU.mult, op1=ALU.mult))
                then(dve.scalar_tensor_tensor(out=st[:, 2, :], in0=st[:, 2, :], scalar=1.0 / D, in1=st[:, 1, :], op0=ALU.mult, op1=ALU.add))
                dve.tensor_scalar(st[:, 3, :], st[:, 2, :], EPS, None, ALU.add).then_inc(s["spread_ready"], 1)
                dve.wait_ge(s["root_ready"], r + 1)
                then(dve.reciprocal(st[:, 5, :], st[:, 4, :]))
                with dve.Fori(0, NT // 8) as h:
                    for k in range(8):
                        t = 8 * h + k
                        dve.tensor_scalar(flat(dst[:, ds(t, 1), :]), flat(src[:, ds(t, 1), :]), st[:, 0, ds(t, 1)], st[:, 5, ds(t, 1)],
                                          ALU.subtract, ALU.mult).then_inc(s[ready], 1)
                dve.wait_ge(s[ready], done)

            dve.wait_ge(s["x_loaded"], 64)
            layer_norm(0, X, XN, "xn_ready", NT)
            layer_norm(1, XN, YN, "yn_ready", NT)
            dve.wait_ge(s["w_loaded"], 16 * W_LOADS)
            then(dve.tensor_tensor(HB[:, :, :], XN[:, :, :], bo[:, :].unsqueeze(1).broadcast_to([P, NT, D]), ALU.add))
            dve.wait_ge(s["w_turned"], 1)
            dve.tensor_copy(wqkv[0][:, :, :], ps_pv[:, 0, 0:3 * D].rearrange("p (t e) -> p t e", t=3)).then_inc(s["w_turned_copied"], 1)
            dve.tensor_copy(wg[1][:, :], ps_pv[:, 1, 0:E1]).then_inc(s["w_turned_copied"], 1)
            dve.tensor_copy(b1T[:, :], ps_pv[:, 1, E1:E1 + E0 * F0 // P]).then_inc(s["w_turned_copied"], 1)
            dve.wait_ge(s["consts_made"], 9)
            for dst, src in ((rev[:, :], revi[:, :]), (stepf[:, :], stepi[:, :]), (dump[:, :, :], dumpi[:, :, :]), (capb[:, :], capi[:, :])):
                then(dve.tensor_copy(dst, src))
            dve.wait_ge(s["rows_init"], 12)

            def attention(pas):
                q0 = JOBS // 8 * pas

                def turn(n, p):
                    dve.wait_ge(s["xt_turned"], n + 1)
                    if pas == 1:
                        dve.tensor_copy(xT[p][:, :], ps_m[:, 1, 0:S]).then_inc(s["xt_copied"], 1)
                    else:
                        dve.tensor_scalar(xT[p][:, :], ps_m[:, 1, 0:S], lnw[:, 0:1], lnw[:, 1:2], ALU.mult, ALU.add).then_inc(s["xt_copied"], 1)

                def split(n, j, t):
                    p, hi, lo = j % 2, (2, 1)[t], (0, 3)[t]
                    if t == 0:
                        dve.wait_ge(s["qkv_done"], n + 1)
                    src = ps_m[:, 1, t * S:(t + 1) * S]
                    if pas == 1:
                        dve.tensor_copy(nat[p][:, hi, :], src).then_inc(s["qk_split"], 1)
                        dve.wait_ge(s["qk_split"], 4 * n + 2 * t + 1)
                        dve.tensor_tensor(nat[p][:, lo, :], src, nat[p][:, hi, :].bitcast(F32), ALU.subtract).then_inc(s["qk_split"], 1)
                    else:
                        dve.tensor_scalar(nat[p][:, hi, :], src, bqk[:, t:t + 1], None, ALU.add).then_inc(s["qk_split"], 1)
                        dve.wait_ge(s["qk_split"], 4 * n + 2 * t + 1)
                        dve.scalar_tensor_tensor(out=nat[p][:, lo, :], in0=src, scalar=bqk[:, t:t + 1], in1=nat[p][:, hi, :].bitcast(F32),
                                                 op0=ALU.add, op1=ALU.subtract).then_inc(s["qk_split"], 1)

                def keep_v(n, j):
                    vsrc = ps_m[:, 0, S:2 * S].rearrange("p (k h e) -> p k h e", k=QT, h=HEADS)
                    for k in range(QT):
                        if pas == 1:
                            dve.tensor_copy(va[j % 4][:, k, :, 0:HD], vsrc[:, k]).then_inc(s["v_copied"], 1)
                        else:
                            dve.tensor_tensor(va[j % 4][:, k, :, 0:HD], vsrc[:, k], bv[:, :].rearrange("p (h e) -> p h e", h=HEADS), ALU.add).then_inc(s["v_copied"], 1)

                def reduce(n, p, u):
                    c, ip, sq = u // 4, u // 2 % 2, u % 2
                    dve.wait_ge(s["s_ready"], 8 * n + u + 1)
                    dve.tensor_reduce(negm[p][:, sq, :].rearrange("p (g i) -> p i g", i=4)[:, 2 * ip:2 * ip + 2, 2 * c:2 * c + 2],
                                      ps_s.rearrange("p b (g k) -> p b g k", g=2), AX.X, ALU.max, negate=True).then_inc(s["s_reduced"], 1)

                def copy_m(n, p):
                    dve.wait_ge(s["m_turned"], n + 1)
                    dve.tensor_copy(mT[p][:, :], ps_m[0:HEADS, 0, S:2 * S]).then_inc(s["m_copied"], 1)

                def normalise(n):
                    dve.wait_ge(s["ct_turned"], n + 1)
                    dve.reciprocal(rec[:, :], ps_m.rearrange("p b (k r) -> p (b k) r", r=32)[:, :, HD]).then_inc(s["rec_done"], 1)
                    dve.wait_ge(s["rec_done"], n + 1)
                    for k in range(QT):
                        wk = ps_m[:, k, :].rearrange("p (c i dg r) -> p c i dg r", c=2, i=4, dg=2)
                        rk = rec[:, 16 * k:16 * k + 16].rearrange("p (c i dg) -> p c i dg", c=2, i=4)
                        ok = o[:, k, :].rearrange("p (c dg i e) -> p c i dg e", i=4, c=2, dg=2)
                        for c in range(2):
                            dve.tensor_tensor(ok[:, c], wk[:, c, :, :, 0:HD], rk[:, c].unsqueeze(3).broadcast_to([P, 4, 2, HD]),
                                              ALU.mult).then_inc(s["o_ready"], 1)

                def add(n):
                    if pas == 0:
                        dve.wait_ge(s["wo_done"], n + 1)
                        h = HB[:, ds(2 * n, 2), :]
                        dve.tensor_tensor(h, ps_m[:, 0, S:2 * S].rearrange("p (k d) -> p k d", k=QT), h, ALU.add).then_inc(s["h_added"], 1)
                        dve.wait_ge(s["h_added"], n + 1)
                        for k in range(QT):
                            take_stats(HB, 2 * n + k)
                    else:
                        dve.wait_ge(s["o_ready"], 4 * n + 4)
                        x = X[:, ds(2 * n - 2 * B, 2), :]
                        dve.tensor_tensor(x, x, o[:, :, :], ALU.add).then_inc(s["x_added"], 1)
                        dve.wait_ge(s["x_added"], n - B + 1)

                n0 = 4 * q0
                for j in range(3):
                    turn(n0 + j, j % 2)
                    split(n0 + j, j, 0)
                    split(n0 + j, j, 1)
                    keep_v(n0 + j, j)
                for j in range(2):
                    for u in range(UNITS):
                        reduce(n0 + j, j, u)
                    if j == 0:
                        copy_m(n0, 0)

                def job(q, j, more, first=False):
                    n, p = 4 * q + j, j % 2
                    for u in range(UNITS):
                        if more >= 2:
                            reduce(n + 2, p, u)
                        if more >= 1 and u == 0:
                            copy_m(n + 1, 1 - p)
                        if more >= 3:
                            if u == 0:
                                turn(n + 3, 1 - p)
                            if u in (1, 2):
                                split(n + 3, j + 3, u - 1)
                            if u == 3:
                                keep_v(n + 3, j + 3)
                        if u == 4 and not first:
                            normalise(n - 1)
                            if pas == 1:
                                add(n - 1)
                    if pas == 0 and not first:
                        add(n - 1)

                last = q0 + JOBS // 8 - 1
                job(q0, 0, 3, True)
                with dve.Fori(q0, last) as q:
                    for j in range(1, 5):
                        job(q, j, 3)
                for j in range(1, 4):
                    job(last, j, 3 - j)
                normalise(4 * last + 3)
                add(4 * last + 3)

            attention(0)
            dve.wait_ge(s["h_added"], B)
            layer_norm(2, HB, YN, "yn_ready", 2 * NT, taken=True)

            def all_tiles(ap):
                return ap.unsqueeze(1).broadcast_to([P, NT, ap.shape[-1]])

            def all_experts(ap, E):
                return ap.unsqueeze(2).broadcast_to([P, NT, E])

            def route(l):
                E = (E0, E1)[l]
                r0 = NT // 4 * l
                for n in range(NT // 4):
                    dve.wait_ge(s["rt_logits"], r0 + n + 1)
                    dve.tensor_copy(LG[:, 4 * n:4 * n + 4, 0:E], ps[:, 2 + n % 2, 0:4 * E].rearrange("p (k e) -> p k e", k=4)).then_inc(s["rt_kept"], 1)
                dve.wait_ge(s["rt_kept"], r0 + NT // 4)

                lg, ta, tb, rk = (t[:, :, 0:E] for t in (LG, TA, TB, RK))
                revb = all_tiles(rev[:, E1 - E:E1])
                if l == 1:
                    dve.tensor_copy(tmp[:, 0, :], LG[:, :, 0]).then_inc(s["odds_ready"], 1)
                    dve.wait_ge(s["odds_ready"], 4)
                    then(dve.tensor_scalar(tb, ta, 1.0, None, ALU.add))
                    then(dve.reciprocal(lg, tb))
                for k in range(TOP):
                    then(dve.tensor_reduce(top[:, k, :], lg, AX.X, ALU.max))
                    then(dve.tensor_tensor(ta, lg, all_experts(top[:, k, :], E), ALU.is_equal))
                    then(dve.tensor_tensor(ta, ta, revb, ALU.mult))
                    then(dve.tensor_reduce(tj[:, k, :], ta, AX.X, ALU.max))
                    then(dve.tensor_tensor(OH[:, k, :, 0:E], revb, all_experts(tj[:, k, :], E), ALU.is_equal))
                    if k == 0:
                        then(dve.tensor_scalar(ta, OH[:, 0, :, 0:E], -1.0, 1.0, ALU.mult, ALU.add))
                        then(dve.tensor_tensor(lg, lg, ta, ALU.mult))
                        then(dve.scalar_tensor_tensor(out=lg, in0=OH[:, 0, :, 0:E], scalar=-3e38, in1=lg, op0=ALU.mult, op1=ALU.add))
                if l == 0:
                    dve.tensor_tensor(tmp[:, 0, :], top[:, 1, :], top[:, 0, :], ALU.subtract).then_inc(s["odds_ready"], 1)
                dve.tensor_tensor(rk, OH[:, 0, :, 0:E], OH[:, 1, :, 0:E], ALU.add).then_inc(s["sums_ready"], 1)
                dve.wait_ge(s["sums_ready"], 2 * l + 2)
                within = ps[:, 4, 0:NT * E].rearrange("p (t e) -> p t e", e=E)
                total = ps[:, 5, 0:NT * E].rearrange("p (t e) -> p t e", e=E)
                then(dve.tensor_copy(ta, total))
                a, b = ta, tb
                k = 1
                while k < NT:
                    dve.tensor_copy(b[:, 0:k, :], a[:, 0:k, :]).then_inc(s["dve_step"], 1)
                    steps[0] += 1
                    then(dve.tensor_tensor(b[:, k:NT, :], a[:, k:NT, :], a[:, 0:NT - k, :], ALU.add))
                    a, b, k = b, a, 2 * k
                then(dve.tensor_tensor(b, a, total, ALU.subtract))
                then(dve.tensor_tensor(rk, within, b, ALU.add))
                if l == 0:
                    then(dve.tensor_scalar(cnt[:, 0, :], a[:, NT - 1, :], float(SLOTS - 1), None, ALU.add))
                    then(dve.tensor_copy(cnti[:, :], cnt[:, 0, :]))
                    then(dve.tensor_scalar(cnti[:, :], cnti[:, :], SLOTS.bit_length() - 1, None, ALU.logical_shift_right))
                    then(dve.tensor_copy(cnt[:, 1, :], cnti[:, :]))
                    then(dve.tensor_copy(cnt[:, 2, :], cnt[:, 1, :]))
                    x, y, k = 2, 3, 1
                    while k < E:
                        then(dve.tensor_copy(cnt[:, y, 0:k], cnt[:, x, 0:k]))
                        then(dve.tensor_tensor(cnt[:, y, k:E], cnt[:, x, k:E], cnt[:, x, 0:E - k], ALU.add))
                        x, y, k = y, x, 2 * k
                    for e in range(E):
                        if e == 0:
                            then(dve.tensor_scalar(emapf[:, :], stepf[:, :], cnt[:, x, 0:1], None, ALU.is_ge))
                        else:
                            then(dve.scalar_tensor_tensor(out=emapf[:, :], in0=stepf[:, :], scalar=cnt[:, x, e:e + 1], in1=emapf[:, :],
                                                          op0=ALU.is_ge, op1=ALU.add))
                    then(dve.tensor_scalar(emap[:, :], emapf[:, :], float(E - 1), None, ALU.min))
                    then(dve.tensor_tensor(cnt[:, y, :], cnt[:, x, :], cnt[:, 1, :], ALU.subtract))
                    then(dve.tensor_scalar(cnt[:, y, :], cnt[:, y, :], float(SLOTS), None, ALU.mult))
                    then(dve.tensor_tensor(rk, rk, all_tiles(cnt[:, y, :]), ALU.add))
                else:
                    then(dve.tensor_scalar(tb if a is ta else ta, rk, float(CAP), None, ALU.is_lt))
                    ok = tb if a is ta else ta
                    spare = a
                    then(dve.tensor_tensor(rk, rk, all_tiles(capb[:, :]), ALU.add))
                for k in range(TOP):
                    w = tb if l == 0 else spare
                    then(dve.tensor_tensor(w, OH[:, k, :, 0:E], rk, ALU.mult))
                    then(dve.tensor_reduce(slot[:, k, :], w, AX.X, ALU.add))
                    if l == 1:
                        then(dve.tensor_tensor(w, OH[:, k, :, 0:E], ok, ALU.mult))
                        then(dve.tensor_reduce(tj[:, k, :], w, AX.X, ALU.add))
                        then(dve.tensor_tensor(tmp[:, 2, :], slot[:, k, :], dump[:, :, k], ALU.subtract))
                        then(dve.tensor_tensor(tmp[:, 2, :], tmp[:, 2, :], tj[:, k, :], ALU.mult))
                        then(dve.tensor_tensor(tmp[:, 2, :], tmp[:, 2, :], dump[:, :, k], ALU.add))
                        then(dve.tensor_copy(slot_to[:, k, :], tmp[:, 2, :]))
                        then(dve.tensor_tensor(slot[:, k, :], slot[:, k, :], tj[:, k, :], ALU.mult))
                    else:
                        then(dve.tensor_copy(slot_to[:, k, :], slot[:, k, :]))
                    then(dve.tensor_copy(slot_from[:, k, :], slot[:, k, :]))
                dve.tensor_copy(tmp[:, 3, :], top[:, 0, :]).then_inc(s["slots_ready"], 1)

                if l == 0:
                    dve.wait_ge(s["odds_ready"], 2)
                    then(dve.tensor_scalar(tmp[:, 2, :], tmp[:, 1, :], 1.0, None, ALU.add))
                    then(dve.reciprocal(tw[:, 0, :], tmp[:, 2, :]))
                    then(dve.tensor_tensor(tw[:, 1, :], tw[:, 0, :], tmp[:, 1, :], ALU.mult))
                else:
                    then(dve.tensor_tensor(tmp[:, 1, :], top[:, 0, :], top[:, 1, :], ALU.add))
                    then(dve.tensor_scalar(tmp[:, 1, :], tmp[:, 1, :], 1e-6, None, ALU.add))
                    then(dve.reciprocal(tmp[:, 2, :], tmp[:, 1, :]))
                    for k in range(TOP):
                        then(dve.tensor_tensor(tw[:, k, :], top[:, k, :], tmp[:, 2, :], ALU.mult))
                        then(dve.tensor_tensor(tw[:, k, :], tw[:, k, :], tj[:, k, :], ALU.mult))
                then(dve.tensor_copy(tmp[:, 0, :], tw[:, 0, :]))
                dve.tensor_copy(tmp[:, 1, :], tw[:, 1, :]).then_inc(s["weights_ready"], 1)
                dve.wait_ge(s["weights_ready"], l + 1)

            def combine(l):
                with dve.Fori(0, NT // 2) as h:
                    for n in range(4):
                        t, k = n // 2, n % 2
                        x = flat(X[:, ds(2 * h + t, 1), :])
                        dve.wait_ge(gathered[n], 16 * (NT // 2 * l + h + 1))
                        if k:
                            dve.wait_ge(s["combined"], TOP * NT * l + 4 * h + n)
                        dve.scalar_tensor_tensor(out=x, in0=got[n][:, :], scalar=tw[:, k, ds(2 * h + t, 1)], in1=x,
                                                 op0=ALU.mult, op1=ALU.add).then_inc(s["combined"], 1)
                        if k and l == 0:
                            dve.wait_ge(s["combined"], TOP * NT * l + 4 * h + n + 1)
                            take_stats(X, 2 * h + t)
                dve.wait_ge(s["combined"], TOP * NT * (l + 1))

            route(0)
            attention(1)
            dve.wait_ge(s["x_added"], B)
            then(dve.tensor_tensor(X[:, :, :], X[:, :, :], HB[:, :, :], ALU.add))

            def turn0(i, p):
                dve.wait_ge(s["e_turned"], i + 1)
                if not isinstance(i, int) or i >= 2:
                    dve.wait_ge(s["e_hidden"], i - 1)
                dve.tensor_scalar(ex[p]["xT"][:, 0:SLOTS], ps[:, 4 + p, 0:SLOTS], lnw[:, 2:3], lnw[:, 3:4], ALU.mult, ALU.add).then_inc(s["e_copied"], 1)

            def add0(i, p, h):
                e = dve.value_load(emap[0:1, ds(i, 1)], min_val=0, max_val=E0 - 1)
                dve.wait_ge(s["e_out"], i + 1)
                if not isinstance(h, int) or h:
                    dve.wait_ge(e_stored[p], 16 * h)
                dve.tensor_tensor(ex[p]["y"][:, 0:2, :], ps[:, 6 + p, 0:SLOTS].rearrange("p (k d) -> p k d", k=2),
                                  b2all[:, ds(e, 1), :].broadcast_to([P, 2, D]), ALU.add).then_inc(s["e_added"], 1)

            turn0(0, 0)
            turn0(1, 1)
            for p in range(2):
                turn0(2 + p, p)
                add0(p, p, 0)
            with dve.Fori(1, STEPS0 // 2 - 1) as h:
                for p in range(2):
                    turn0(2 * h + 2 + p, p)
                    add0(2 * h + p, p, h)
            add0(STEPS0 - 2, 0, STEPS0 // 2 - 1)
            add0(STEPS0 - 1, 1, STEPS0 // 2 - 1)
            combine(0)

            layer_norm(3, X, XN, "xn_ready", 2 * NT, taken=True)
            route(1)

            def turn_l1(b, p):
                dve.wait_ge(s["u_ready"], 5 * b + 1)
                dve.tensor_copy(xT[p][:, :], ps_s[:, 0, 0:S]).then_inc(s["u_copied"], 1)

            def maxima(b, g):
                n, gp = 4 * b + g, g % 2
                if not (isinstance(n, int) and n < 2):
                    dve.wait_ge(s["exp1_done"], n - 1)
                dve.wait_ge(s["s0_ready"], n + 1)
                dve.tensor_reduce(nm[gp][:, 0, :], ps[:, 2, :].rearrange("p (i k) -> p i k", i=4), AX.X, ALU.max, negate=True).then_inc(s["max0_ready"], 1)
                dve.wait_ge(s["s1_ready"], n + 1)
                dve.tensor_reduce(nm[gp][:, 1, :], ps[:, 3:5, :].rearrange("p b (i k) -> p (b i) k", i=2), AX.X, ALU.max, negate=True).then_inc(s["max1_ready"], 1)

            def diagonal(b, g, p):
                n, gp = 4 * b + g, g % 2
                dve.wait_ge(s["diag_masked"], 2 * n + 2)
                dve.tensor_reduce(num[p][:, :, 4 * g:4 * g + 4], DG[gp][:, :, :, :], AX.X, ALU.add).then_inc(s["diag_summed"], 1)

            def shares(b, p):
                dve.wait_ge(s["exp1_done"], 4 * b + 4)
                dve.wait_ge(s["diag_summed"], 4 * b + 4)
                dve.reciprocal(share[p][:, :, :], den[p][:, :, :]).then_inc(s["rec_done"], 1)
                dve.wait_ge(s["rec_done"], JOBS + b + 1)
                dve.tensor_tensor(share[p][:, :, :], share[p][:, :, :], num[p][:, :, :], ALU.mult).then_inc(s["share_ready"], 1)
                dve.wait_ge(s["share_ready"], b + 1)

            def weigh(b, k, p):
                dve.wait_ge(s["v1_ready"], 2 * b + k + 1)
                dve.tensor_tensor(O1[:, :].rearrange("p (h v) -> p h v", h=HEADS), ps[:, 5:7, :].rearrange("p b (h v) -> p (b h) v", v=DV),
                                  share[p][:, k, :].unsqueeze(2).broadcast_to([P, HEADS, DV]), ALU.mult).then_inc(s["o1_ready"], 1)

            def copy_o(b, k):
                dve.wait_ge(s["o1_turned"], 2 * b + k + 1)
                dve.tensor_copy(O1T[:, :, :], ps[:, 5:7, :].rearrange("p b (c t) -> p (b c) t", t=P)).then_inc(s["o1_copied"], 1)

            def add_y(b, k):
                dve.wait_ge(s["y_ready"], 2 * b + k + 1)
                x = flat(X[:, ds(2 * b + k, 1), :])
                dve.tensor_tensor(x, ps[:, 7, 0:D], x, ALU.add).then_inc(s["y_added"], 1)

            def sequence(b, p, prev, nxt):
                maxima(b, 0)
                if prev:
                    diagonal(b - 1, 3, 1 - p)
                    shares(b - 1, 1 - p)
                    weigh(b - 1, 0, 1 - p)
                    copy_o(b - 1, 0)
                maxima(b, 1)
                diagonal(b, 0, p)
                if prev:
                    add_y(b - 1, 0)
                maxima(b, 2)
                if prev:
                    weigh(b - 1, 1, 1 - p)
                diagonal(b, 1, p)
                if nxt:
                    turn_l1(b + 1, 1 - p)
                if prev:
                    copy_o(b - 1, 1)
                maxima(b, 3)
                diagonal(b, 2, p)
                if prev:
                    add_y(b - 1, 1)

            turn_l1(0, 0)
            sequence(0, 0, False, True)
            with dve.Fori(0, B // 2 - 1) as h:
                for b, p in ((2 * h + 1, 1), (2 * h + 2, 0)):
                    sequence(b, p, True, True)
            sequence(B - 1, 1, True, False)
            diagonal(B - 1, 3, 1)
            shares(B - 1, 1)
            for k in range(QT):
                weigh(B - 1, k, 1)
                copy_o(B - 1, k)
                add_y(B - 1, k)
            dve.wait_ge(s["y_added"], QT * B)

            def turn1(e, p):
                dve.wait_ge(s["e_turned"], STEPS0 + e + 1)
                dve.tensor_copy(ex[p]["xT"][:, :], ps[:, 0:2, :].rearrange("p b n -> p (b n)")[:, 0:CAP]).then_inc(s["e_copied"], 1)

            def add1(e, p, h):
                dve.wait_ge(s["e_out"], STEPS0 + e + 1)
                dve.wait_ge(e_stored[p], 16 * (STEPS0 // 2) + 16 * h)
                dve.tensor_copy(ex[p]["y"][:, :, :], ps[:, 6:8, :].rearrange("p b (k d) -> p (b k) d", d=D)[:, 0:CT, :]).then_inc(s["e_added"], 1)

            turn1(0, 0)
            with dve.Fori(0, E1 // 2 - 1) as h:
                for p in range(2):
                    turn1(2 * h + p + 1, 1 - p)
                    add1(2 * h + p, p, h)
            turn1(E1 - 1, 1)
            add1(E1 - 2, 0, E1 // 2 - 1)
            add1(E1 - 1, 1, E1 // 2 - 1)
            combine(1)

        @block.tensor
        def _(pe):
            pe.wait_ge(s["ident_ready"], 1)
            pe.wait_ge(s["w_loaded"], 16 * W_LOADS)
            for t in range(3):
                pe.transpose(ps_pv[:, 0, t * D:(t + 1) * D], wraw[:, t, :], ident[:, :])
            pe.transpose(ps_pv[:, 1, 0:E1], wg1raw[:, :], ident[0:E1, 0:E1])
            nb = E0 * F0 // P
            pe.transpose(ps_pv[:, 1, E1:E1 + nb], b1raw[:, :], ident[0:nb, 0:nb]).then_inc(s["w_turned"], 1)
            pe.wait_ge(s["p_loaded"], 64)
            for raw, bank, ready in ((praw, 0, "pq_turned"), (kraw, 2, "pk_turned"), (oraw, 6, "po_turned")):
                for c in range(HEADS // 2):
                    last = pe.transpose(ps[:, bank + c // 4, (c % 4) * D:(c % 4 + 1) * D], raw[:, 2 * c:2 * c + 2, :].rearrange("p a k -> p (a k)"), ident[:, :])
                last.then_inc(s[ready], 1)
            pe.wait_ge(s["pq_copied"], 1)
            pe.wait_ge(s["pk_copied"], 1)
            for h in range(HEADS):
                r = slice(DK * (h % 2), DK * (h % 2) + DK)
                c = 8 * (h % 2) + h // 2
                last = pe.matmul(ps[:, c // 4, (c % 4) * D:(c % 4 + 1) * D], PkT[r, h // 2, :], PqT[r, h // 2, :], start=True, stop=True)
            last.then_inc(s["a_made"], 1)
            pe.wait_ge(s["w_turned_copied"], 3)
            pe.wait_ge(s["po_copied"], 1)
            pe.wait_ge(s["a_copied"], 1)

            def attention(pas):
                q0 = JOBS // 8 * pas
                n0 = 4 * q0

                def turn_x(q, j):
                    q, j = q + j // 4, j % 4
                    pe.wait_ge(xs_staged[j], 16 * q + 16)
                    for k in range(QT):
                        last = pe.transpose(ps_m[:, 1, k * P:(k + 1) * P], xs[j % 2][:, k, :], ident[:, :])
                    last.then_inc(s["xt_turned"], 1)

                def project(q, j):
                    w = wqkv[1 - pas]
                    pe.wait_ge(s["xt_copied"], 4 * q + j + 1)
                    for t in range(2):
                        pe.matmul(ps_m[:, 1, t * S:(t + 1) * S], w[:, t, :], xT[j % 2][:, :], start=True, stop=True)
                    for k in range(QT):
                        last = pe.matmul(ps_m[:, 0, S + k * P:S + (k + 1) * P], xT[j % 2][:, k * P:(k + 1) * P], w[:, 2, :], start=True, stop=True)
                    last.then_inc(s["qkv_done"], 1)

                def scores(n, j, u):
                    c, ip, sq = u // 4, u // 2 % 2, u % 2
                    if not (isinstance(n, int) and n == 0 and u == 0):
                        pe.wait_ge(s["s_reduced"], 8 * n + u)
                    for dg in range(2):
                        for di in range(2):
                            r = slice(32 * (2 * ip + di), 32 * (2 * ip + di) + 31)
                            last = pe.matmul(ps_s[:, di, dg * S:(dg + 1) * S], rows[j][r, 2 * c + dg, 0, sq * P:(sq + 1) * P],
                                             rows[j][r, 2 * c + dg, 1, :], start=True, stop=True)
                    last.then_inc(s["s_ready"], 1)

                def turn_m(n, p):
                    pe.wait_ge(s["s_reduced"], 8 * n + 8)
                    for k in range(QT):
                        last = pe.transpose(ps_m[0:HEADS, 0, S + k * P:S + (k + 1) * P], negm[p][:, k, :], ident[:, :])
                    last.then_inc(s["m_turned"], 1)

                def scores_t(n, j, u):
                    c, ip, kt = u // 4, u // 2 % 2, u % 2
                    if not (isinstance(n, int) and n == 0 and u == 0):
                        pe.wait_ge(s["exp_done"], 8 * n + u)
                    for dg in range(2):
                        for di in range(2):
                            r = slice(32 * (2 * ip + di), 32 * (2 * ip + di) + 32)
                            last = pe.matmul(ps_t[:, di, dg * S:(dg + 1) * S], rows[j][r, 2 * c + dg, 1, kt * P:(kt + 1) * P],
                                             rows[j][r, 2 * c + dg, 0, :], start=True, stop=True)
                    last.then_inc(s["st_ready"], 1)

                def values(n, j, u):
                    c, ip, kt = u // 4, u // 2 % 2, u % 2
                    pe.wait_ge(s["exp_done"], 8 * n + u + 1)
                    for x in range(4):
                        di, dg = x // 2, x % 2
                        last = pe.matmul(ps_pv[32 * x:32 * x + 32, c, ip * S:(ip + 1) * S], va[j][:, kt, 4 * (2 * c + dg) + 2 * ip + di, :],
                                         probs[:, u % 2, x, :], start=(kt == 0), stop=(kt == 1))
                    last.then_inc(s["pv_done"], 1)

                def turn_c(n):
                    pe.wait_ge(s["ct_copied"], n + 1)
                    for k in range(QT):
                        for blk in range(4):
                            last = pe.transpose(ps_m[:, k, blk * P:(blk + 1) * P], ctxT[:, blk, k * P:(k + 1) * P], ident[:, :])
                    last.then_inc(s["ct_turned"], 1)

                def turn_o(n):
                    pe.wait_ge(s["o_ready"], 4 * n + 4)
                    for k in range(QT):
                        last = pe.transpose(ps_m[:, 0, k * P:(k + 1) * P], o[:, k, :], ident[:, :])
                    last.then_inc(s["ot_turned"], 1)

                def output(n):
                    pe.wait_ge(s["ot_copied"], n + 1)
                    for k in range(QT):
                        last = pe.matmul(ps_m[:, 0, S + k * P:S + (k + 1) * P], oT[:, k * P:(k + 1) * P], wo[:, :], start=True, stop=True)
                    last.then_inc(s["wo_done"], 1)

                def projected(n):
                    pe.wait_ge(s["qk_split"], 4 * n)
                    pe.wait_ge(s["v_copied"], 2 * n)

                def job(q, j, more, first=False):
                    n, p = 4 * q + j, j % 2
                    pe.wait_ge(m_sent[j % 4], 64 * (q + j // 4) + 64)
                    if more >= 2:
                        pe.wait_ge(rows_sent[(j + 2) % 4], 256 * (q + (j + 2) // 4) + 256)
                    for u in range(UNITS):
                        scores_t(n, j % 4, u)
                        if more >= 2:
                            scores(n + 2, (j + 2) % 4, u)
                        if u:
                            values(n, j % 4, u - 1)
                        elif not (first and pas == 0):
                            pe.wait_ge(s["ct_copied"], n)
                        if u == 0:
                            if first:
                                projected(n0 + 3)
                            elif pas == 0 and not (isinstance(n, int) and n == 1):
                                pe.wait_ge(s["h_added"], n - 1)
                            elif pas == 1 or not isinstance(n, int):
                                pe.wait_ge(s["o_ready"], 4 * n - 4)
                            if more >= 1:
                                turn_m(n + 1, 1 - p)
                            if more >= 3:
                                turn_x(q, j + 3)
                        if u == 1 and more >= 3:
                            pe.wait_ge(s["m_copied"], n + 2)
                            project(q, j + 3)
                        if not first:
                            if u == 4:
                                projected(n + 4 if more >= 3 else n0 + JOBS // 2)
                                pe.wait_ge(s["m_copied"], n + 2 if more >= 1 else n + 1)
                                turn_c(n - 1)
                            if pas == 0 and u == 6:
                                turn_o(n - 1)
                            if pas == 0 and u == 7:
                                output(n - 1)
                    values(n, j % 4, UNITS - 1)

                for j in range(3):
                    if j:
                        projected(n0 + j)
                    turn_x(q0, j)
                    project(q0, j)
                projected(n0 + 3)
                for j in range(2):
                    pe.wait_ge(rows_sent[j], 256 * q0 + 256)
                    for u in range(UNITS):
                        scores(n0 + j, j, u)
                    if j == 0:
                        turn_m(n0, 0)
                last = q0 + JOBS // 8 - 1
                pe.wait_ge(s["m_copied"], n0 + 1)
                job(q0, 0, 3, True)
                with pe.Fori(q0, last) as q:
                    for j in range(1, 5):
                        job(q, j, 3)
                for j in range(1, 4):
                    job(last, j, 3 - j)
                n = 4 * last + 3
                if pas == 0:
                    pe.wait_ge(s["h_added"], n)
                else:
                    pe.wait_ge(s["o_ready"], 4 * n)
                turn_c(n)
                if pas == 0:
                    turn_o(n)
                    output(n)

            def route(l):
                E = (E0, E1)[l]
                r0 = NT // 4 * l

                src, ready = ((YN, "yn_ready"), (XN, "xn_ready"))[l]

                def turn_rows(n):
                    pe.wait_ge(s[ready], NT + 4 * n + 4)
                    if n >= 2:
                        pe.wait_ge(s["rt_copied"], r0 + n - 1)
                    for k in range(4):
                        last = pe.transpose(ps[:, n % 2, k * P:(k + 1) * P], src[:, 4 * n + k, :], ident[:, :])
                    last.then_inc(s["rt_turned"], 1)

                turn_rows(0)
                for n in range(NT // 4):
                    if n + 1 < NT // 4:
                        turn_rows(n + 1)
                    pe.wait_ge(s["rt_copied"], r0 + n + 1)
                    if n >= 2:
                        pe.wait_ge(s["rt_kept"], r0 + n - 1)
                    for k in range(4):
                        last = pe.matmul(ps[:, 2 + n % 2, k * E:(k + 1) * E], rT[n % 2][:, k * P:(k + 1) * P], wg[l][:, :], start=True, stop=True)
                    last.then_inc(s["rt_logits"], 1)
                pe.wait_ge(s["sums_ready"], 2 * l + 1)
                chosen = RK[:, :, 0:E]
                pe.matmul(ps[:, 4, 0:NT * E], before[:, :], chosen, start=True, stop=True)
                pe.matmul(ps[:, 5, 0:NT * E], ones[:, :], chosen, start=True, stop=True).then_inc(s["sums_ready"], 1)

            pe.wait_ge(s["rows_init"], 12)
            attention(0)
            pe.wait_ge(s["h_added"], B)
            pe.wait_ge(s["consts_made"], 9)
            route(0)
            pe.wait_ge(s["slots_ready"], 1)
            attention(1)
            pe.wait_ge(s["x_added"], B)

            def turn(i, p, h):
                pe.wait_ge(x_in[p], 16 * h + 16)
                if not isinstance(i, int) or i >= 2:
                    pe.wait_ge(s["e_copied"], i - 1)
                for k in range(2):
                    last = pe.transpose(ps[:, 4 + p, k * P:(k + 1) * P], ex[p]["x"][:, k, :], ident[:, :])
                last.then_inc(s["e_turned"], 1)

            def hidden(i, p, h):
                pe.wait_ge(up_in[p], 16 * h + 16)
                pe.wait_ge(s["e_copied"], i + 1)
                if not isinstance(i, int) or i >= 2:
                    pe.wait_ge(s["e_gelu"], i - 1)
                for f in range(F0 // P):
                    last = pe.matmul(ps[:, 2 * p + f // 2, (f % 2) * SLOTS:(f % 2 + 1) * SLOTS], ex[p]["w1"][:, f * P:(f + 1) * P],
                                     ex[p]["xT"][:, 0:SLOTS], start=True, stop=True)
                last.then_inc(s["e_hidden"], 1)

            def result(i, p, h):
                pe.wait_ge(down_in[p], 16 * h + 16)
                pe.wait_ge(s["e_gelu"], i + 1)
                if not isinstance(i, int) or i >= 2:
                    pe.wait_ge(s["e_added"], i - 1)
                for k in range(2):
                    for f in range(F0 // P):
                        last = pe.matmul(ps[:, 6 + p, k * D:(k + 1) * D], ex[p]["g"][:, f, k * P:(k + 1) * P], ex[p]["w2"][:, f, :],
                                         start=(f == 0), stop=(f == F0 // P - 1))
                last.then_inc(s["e_out"], 1)

            turn(0, 0, 0)
            hidden(0, 0, 0)
            turn(1, 1, 0)

            def steps0(h):
                hidden(2 * h + 1, 1, h)
                turn(2 * h + 2, 0, h + 1)
                result(2 * h, 0, h)
                hidden(2 * h + 2, 0, h + 1)
                turn(2 * h + 3, 1, h + 1)
                result(2 * h + 1, 1, h)

            steps0(0)
            with pe.Fori(1, STEPS0 // 2 - 1) as h:
                steps0(h)
            half = STEPS0 // 2 - 1
            hidden(STEPS0 - 1, 1, half)
            result(STEPS0 - 2, 0, half)
            result(STEPS0 - 1, 1, half)

            route(1)
            pe.wait_ge(s["slots_ready"], 2)

            def turn_x1(b, p, h):
                if not (isinstance(b, int) and b == 0):
                    pe.wait_ge(s["u_copied"], 5 * b)
                pe.wait_ge(xs_staged[p], 16 * (JOBS // 4) + 16 * h + 16)
                for k in range(QT):
                    last = pe.transpose(ps_s[:, 0, k * P:(k + 1) * P], xs[p][:, k, :], ident[:, :])
                last.then_inc(s["u_ready"], 1)

            def keys(b, g, p):
                pe.wait_ge(s["u_copied"], 5 * b + g + 1)
                for i in range(4):
                    last = pe.matmul(ps_s[:, i // 2, (i % 2) * S:(i % 2 + 1) * S], AH[:, 4 * g + i, :], xT[p][:, :], start=True, stop=True)
                last.then_inc(s["u_ready"], 1)

            def scores1(b, g, p):
                n, gp = 4 * b + g, g % 2
                pe.wait_ge(s["u_copied"], 5 * b + g + 2)
                if not (isinstance(n, int) and n == 0):
                    pe.wait_ge(s["exp0_done"], n)
                pe.matmul(ps[:, 2, :], xT[p][:, 0:P], U[gp][:, :, 0:P], start=True, stop=False)
                pe.matmul(ps[:, 2, :], identb[:, :], tri0[:, :, :], start=False, stop=True).then_inc(s["s0_ready"], 1)
                if not (isinstance(n, int) and n == 0):
                    pe.wait_ge(s["exp1_done"], n)
                for x in range(2):
                    pe.matmul(ps[:, 3 + x, :], xT[p][:, P:2 * P], U[gp][:, 2 * x:2 * x + 2, :], start=True, stop=False)
                    last = pe.matmul(ps[:, 3 + x, :], identb[:, :], tri1[:, :, :], start=False, stop=True)
                last.then_inc(s["s1_ready"], 1)

            def values1(b, k, p):
                if not (isinstance(b, int) and b == 0 and k == 0):
                    pe.wait_ge(s["o1_copied"], 2 * b + k)
                for x in range(2):
                    last = pe.matmul(ps[:, 5 + x, :], xT[p][:, k * P:(k + 1) * P], Pv[:, x * 512:(x + 1) * 512], start=True, stop=True)
                last.then_inc(s["v1_ready"], 1)

            def turn_o(b, k):
                pe.wait_ge(s["o1_ready"], 2 * b + k + 1)
                for c in range(HEADS // 2):
                    last = pe.transpose(ps[:, 5 + c // 4, (c % 4) * P:(c % 4 + 1) * P], O1[:, c * P:(c + 1) * P], ident[:, :])
                last.then_inc(s["o1_turned"], 1)

            def output1(b, k):
                pe.wait_ge(s["o1_copied"], 2 * b + k + 1)
                if not (isinstance(b, int) and b == 0 and k == 0):
                    pe.wait_ge(s["y_added"], 2 * b + k)
                for c in range(HEADS // 2):
                    last = pe.matmul(ps[:, 7, 0:D], O1T[:, c, :], PoT[:, c, :], start=(c == 0), stop=(c == HEADS // 2 - 1))
                last.then_inc(s["y_ready"], 1)

            def sequence(b, p, h_next, prev, nxt):
                keys(b, 0, p)
                keys(b, 1, p)
                scores1(b, 0, p)
                if prev:
                    values1(b - 1, 0, 1 - p)
                keys(b, 2, p)
                if prev:
                    turn_o(b - 1, 0)
                scores1(b, 1, p)
                if prev:
                    output1(b - 1, 0)
                keys(b, 3, p)
                if prev:
                    values1(b - 1, 1, 1 - p)
                scores1(b, 2, p)
                if nxt:
                    turn_x1(b + 1, 1 - p, h_next)
                if prev:
                    turn_o(b - 1, 1)
                scores1(b, 3, p)
                if prev:
                    output1(b - 1, 1)

            turn_x1(0, 0, 0)
            sequence(0, 0, 0, False, True)
            with pe.Fori(0, B // 2 - 1) as h:
                sequence(2 * h + 1, 1, h + 1, True, True)
                sequence(2 * h + 2, 0, h + 1, True, True)
            sequence(B - 1, 1, 0, True, False)
            for k in range(QT):
                values1(B - 1, k, 1)
                turn_o(B - 1, k)
                output1(B - 1, k)

            pe.wait_ge(s["exp1_done"], 4 * B)
            half = STEPS0 // 2

            def turn_e(e, p, h):
                pe.wait_ge(x_in[p], 16 * half + 16 * h + 16)
                for k in range(CT):
                    last = pe.transpose(ps[:, k // 4, (k % 4) * P:(k % 4 + 1) * P], ex[p]["x"][:, k, :], ident[:, :])
                last.then_inc(s["e_turned"], 1)

            def hidden1(e, p, h):
                pe.wait_ge(up_in[p], 16 * half + 16 * h + 16)
                pe.wait_ge(s["e_copied"], STEPS0 + e + 1)
                pe.wait_ge(s["e_gelu"], STEPS0 + e)
                for f in range(F1 // P):
                    for c in range(2):
                        last = pe.matmul(ps[:, 2 + 2 * f + c, 0:HALF], ex[p]["w1"][:, f * P:(f + 1) * P], ex[p]["xT"][:, c * HALF:(c + 1) * HALF],
                                         start=True, stop=True)
                last.then_inc(s["e_hidden"], 1)

            def result1(e, p, h):
                pe.wait_ge(down_in[p], 16 * half + 16 * h + 16)
                pe.wait_ge(s["e_gelu"], STEPS0 + e + 1)
                pe.wait_ge(s["e_added"], STEPS0 + e)
                act_of = ex[p]["g"][:, :, :].rearrange("p (f c) n -> p f (c n)", c=2)
                for k in range(CT):
                    for f in range(F1 // P):
                        last = pe.matmul(ps[:, 6 + k // 4, (k % 4) * D:(k % 4 + 1) * D], act_of[:, f, k * P:(k + 1) * P], ex[p]["w2"][:, f, :],
                                         start=(f == 0), stop=(f == F1 // P - 1))
                last.then_inc(s["e_out"], 1)

            turn_e(0, 0, 0)
            with pe.Fori(0, E1 // 2 - 1) as h:
                for p in range(2):
                    hidden1(2 * h + p, p, h)
                    turn_e(2 * h + p + 1, 1 - p, h + p)
                    result1(2 * h + p, p, h)
            last_h = E1 // 2 - 1
            hidden1(E1 - 2, 0, last_h)
            turn_e(E1 - 1, 1, last_h)
            result1(E1 - 2, 0, last_h)
            hidden1(E1 - 1, 1, last_h)
            result1(E1 - 1, 1, last_h)


_INS = ["L0_attn_x", "L0_attn_Wq", "L0_attn_Wk", "L0_attn_Wv", "L0_ffn_ln1_w", "L0_ffn_ln1_b", "L0_ffn_ln2_w", "L0_ffn_ln2_b",
        "L0_ffn_w_qkv", "L0_ffn_b_qkv", "L0_ffn_w_o", "L0_ffn_b_o", "L0_ffn_w_gate", "L0_ffn_w1", "L0_ffn_b1", "L0_ffn_w2",
        "L0_ffn_b2", "L1_attn_P_q", "L1_attn_P_k", "L1_attn_P_v", "L1_attn_P_o", "L1_ffn_gate_w", "L1_ffn_w1", "L1_ffn_w2"]


def kernel(**inputs):
    import numpy as _np
    import concourse.bacc as _bacc
    from concourse import mybir as _mybir
    from concourse.bass_utils import run_bass_kernel_spmd as _run

    nc = _bacc.Bacc("TRN2", target_bir_lowering=False, num_devices=1)
    arrays, args = {}, {}
    for name in _INS:
        a = _np.ascontiguousarray(inputs[name])
        arrays[f"in_{name}_dram"] = a
        args[name] = nc.dram_tensor(f"in_{name}_dram", a.shape, _mybir.dt.from_np(a.dtype), kind="ExternalInput").ap()
    out = nc.dram_tensor("out_dram", args["L0_attn_x"].shape, _mybir.dt.float32, kind="ExternalOutput").ap()
    build(nc, args, out)
    r = _run(nc, [arrays], core_ids=[0])
    return r.results[0]["out_dram"]
```

```python
from contextlib import ExitStack

import concourse.bass as bass
from concourse import mybir

F32 = mybir.dt.float32
F32R = mybir.dt.float32r
BF16 = mybir.dt.bfloat16
I32 = mybir.dt.int32
U32 = mybir.dt.uint32
ALU = mybir.AluOpType
ACT = mybir.ActivationFunctionType
AX = mybir.AxisListType
ds = bass.ds

P = 128
EPS = 1e-5
NEVER = -1e38
ROW_BANKS = (0, 1, 4)
W_LOADS = 17

SEMAPHORES = """
x_first x_loaded w_loaded p_loaded ident_zero ident_ready consts_made zero_ready tables_zeroed dve_step
stats_taken spread_ready root_ready shift_ready xn_ready yn_ready hb_ready
w_turned w_turned_copied pq_turned pq_copied pk_turned pk_copied a_made a_copied po_turned po_copied
xt_turned xt_copied qkv_done qk_split v_copied
s_ready s_reduced m_turned m_copied st_ready exp_done pv_done ct_copied ct_turned rec_done o_ready
ot_turned ot_copied wo_done h_added x_added rows_init
rt_turned rt_copied rt_logits rt_kept odds_ready sums_ready sums_kept slots_ready weights_ready
scattered x_in0 x_in1 up_in0 up_in1 down_in0 down_in1 e_turned e_copied e_half e_hidden e_gelu e_out e_added e_stored0 e_stored1
combined base_added
x1_ready x1_copied u_ready u_copied x_high pv_high pv_low s0_ready s1_ready max0_ready max1_ready exp0_done exp1_done diag_masked diag_summed
share_ready v1_ready o1_ready o1_turned o1_copied y_ready y_added out_sent
""".split()


def build(nc, A, out):
    B, S, D = A["L0_attn_x"].shape
    NT = B * S // P
    QT = S // P
    HEADS = 16
    HD = D // HEADS
    GROUPS = 4
    UNITS = 8
    SCALE = 1.0 / float(HD) ** 0.5
    JOBS = 2 * B
    DK = A["L1_attn_P_q"].shape[2]
    DV = A["L1_attn_P_v"].shape[2]
    E0, _, F0 = A["L0_ffn_w1"].shape
    E1, _, F1 = A["L1_ffn_w1"].shape
    TOP = 2
    SLOTS = 256
    STEPS0 = NT * P * TOP // SLOTS + E0
    CAP = int(1.25 * NT * P * TOP / E1)
    CT = CAP // P
    ROWS0 = STEPS0 * SLOTS
    ROWS1 = E1 * CAP
    HALF = CAP // 2
    ZEROINGS = (ROWS0 + ROWS1) // 1024
    FIRST = 8
    RANKED = 3
    BEFORE = 9
    assert S == 256 and D == P and CAP % P == 0 and F0 == 512 and F1 == 256 and ROWS0 % P == 0

    with ExitStack() as ctx:
        def sb(name, shape, dt=F32, into=ctx):
            return into.enter_context(nc.sbuf_tensor(name, shape, dt))

        s = {n: ctx.enter_context(nc.semaphore(n)) for n in SEMAPHORES}
        rows_sent = [ctx.enter_context(nc.semaphore(f"rows_sent{j}")) for j in range(4)]
        m_sent = [ctx.enter_context(nc.semaphore(f"m_sent{j}")) for j in range(4)]
        xs_staged = [ctx.enter_context(nc.semaphore(f"xs_staged{j}")) for j in range(4)]
        x_in, up_in, down_in = ([s[f"{n}{p}"] for p in range(2)] for n in ("x_in", "up_in", "down_in"))
        e_stored = [s["e_stored0"], s["e_stored1"]]
        gathered = [ctx.enter_context(nc.semaphore(f"gathered{k}")) for k in range(8)]

        xg = [nc.dram_tensor("xg0", (ROWS0, D), F32).ap(), nc.dram_tensor("xg1", (ROWS1 + NT * P * TOP, D), F32).ap()]
        yg = [nc.dram_tensor("yg0", (ROWS0, D), F32).ap(), nc.dram_tensor("yg1", (ROWS1, D), F32).ap()]

        X = sb("X", [P, NT, D])
        XN = sb("XN", [P, NT, D])
        YN = sb("YN", [P, NT, D])
        HB = sb("HB", [P, NT, D])
        stats = sb("stats", [P, NT, 6])
        st = sb("st", [P, 6, NT])
        ident = sb("ident", [P, P])
        identb = sb("identb", [P, P], BF16)
        ones = sb("ones", [P, P])
        before = sb("before", [P, P])
        tri0 = sb("tri0", [P, 4, P], BF16)
        wo = sb("wo", [P, D])
        lnw = sb("lnw", [P, 4])
        bqk = sb("bqk", [P, 2])
        bv = sb("bv", [P, D])
        bo = sb("bo", [P, D])
        wqkv = [sb(f"wqkv{a}", [P, 3, D]) for a in range(2)]
        b1T = sb("b1T", [P, E0 * F0 // P])
        b2all = sb("b2all", [P, E0, D])
        wg = [sb("wg0", [P, E0]), sb("wg1", [P, E1])]
        AH = sb("AH", [P, HEADS, D])
        PoT = sb("PoT", [P, HEADS // 2, D])
        Pv = sb("Pv", [P, HEADS * DV])
        xs = [sb(f"xs{a}", [P, QT, D]) for a in range(2)]
        xT = [sb(f"xT{a}", [P, S]) for a in range(2)]

        revi = sb("revi", [P, E1], I32)
        rev = sb("rev", [P, E1])
        stepi = sb("stepi", [P, STEPS0], I32)
        stepf = sb("stepf", [P, STEPS0])
        dumpi = sb("dumpi", [P, NT, TOP], I32)
        dump = sb("dump", [P, NT, TOP])
        capi = sb("capi", [P, E1], I32)
        capb = sb("capb", [P, E1])
        top = sb("top", [P, TOP, NT])
        tj = sb("tj", [P, TOP, NT])
        tw = sb("tw", [P, TOP, NT])
        tmp = sb("tmp", [P, 4, NT])
        slot = sb("slot", [P, TOP, NT])
        slot_to = sb("slot_to", [P, TOP, NT], I32)
        slot_from = sb("slot_from", [P, TOP, NT], I32)
        cnt = sb("cnt", [P, 4, E0])
        cnti = sb("cnti", [P, E0], I32)
        emapf = sb("emapf", [P, STEPS0])
        emap = sb("emap", [P, STEPS0], I32)

        def expert_buffers(into):
            return [dict(x=sb(f"ex{p}", [P, CT, D], F32, into), w1=sb(f"ew1{p}", [P, F0], F32, into),
                         w2=sb(f"ew2{p}", [P, F0 // P, D], F32, into), xT=sb(f"exT{p}", [P, CAP], F32, into),
                         y=sb(f"ey{p}", [P, CT, D], F32, into)) for p in range(2)]

        got = [sb(f"got{k}", [P, D]) for k in range(8)]

        with ExitStack() as early:
            zeros = sb("zeros", [P, 1024], F32, early)
            wraw = sb("wraw", [P, 3, D], F32, early)
            b1raw = sb("b1raw", [E0 * F0 // P, P], F32, early)
            wg1raw = sb("wg1raw", [E1, D], F32, early)
        with ExitStack() as early:
            praw = sb("praw", [P, HEADS, DK], F32, early)
            kraw = sb("kraw", [P, HEADS, DK], F32, early)
            oraw = sb("oraw", [P, HEADS, DV], F32, early)
            PqT = sb("PqT", [P, HEADS // 2, D], F32, early)
            PkT = sb("PkT", [P, HEADS // 2, D], F32, early)
        with ExitStack() as routing:
            LG = sb("LG", [P, NT, E1], F32, routing)
            OH = sb("OH", [P, TOP, NT, E1], F32, routing)
            RK = sb("RK", [P, NT, E1], F32, routing)
            TA = sb("TA", [P, NT, E1], F32, routing)
            TB = sb("TB", [P, NT, E1], F32, routing)
            inside = sb("inside", [P, NT, E1], F32, routing)
            total = sb("total", [P, NT, E1], F32, routing)
            rT = [sb(f"rT{p}", [P, 4 * P], F32, routing) for p in range(3)]
        ex = expert_buffers(ctx)

        with ExitStack() as first:
            nat = [sb(f"nat{a}", [P, 4, S], F32R, first) for a in range(2)]
            rows = [sb(f"rows{j}", [P, GROUPS, 2, S], F32R, first) for j in range(4)]
            va = [sb(f"va{j}", [P, QT, HEADS, 32], F32, first) for j in range(4)]
            negm = [sb(f"negm{a}", [P, QT, HEADS], F32, first) for a in range(2)]
            mT = [sb(f"mT{a}", [HEADS, S], F32R, first) for a in range(2)]
            probs = sb("probs", [P, 2, 4, S], F32, first)
            ctxT = sb("ctxT", [P, 4, S], F32, first)
            rec = sb("rec", [P, 2 * HEADS], F32, first)
            o = sb("o", [P, QT, D], F32, first)
            oT = sb("oT", [P, S], F32, first)
        for p in range(2):
            ex[p]["g"] = sb(f"eg{p}", [P, 4, HALF])
        U = [sb(f"U{p}", [P, 4, S]) for p in range(2)]
        xH, xL = ([sb(f"x{n}{p}", [P, S], F32R) for p in range(2)] for n in ("H", "L"))
        PvH, PvL = (sb(f"Pv{n}", [P, HEADS * DV], F32R) for n in ("H", "L"))
        EX0 = [sb(f"EX0{p}", [P, 4, P]) for p in range(2)]
        EX1 = [sb(f"EX1{p}", [P, 4, S]) for p in range(2)]
        DG = [sb(f"DG{p}", [P, 2, 4, P]) for p in range(2)]
        nm = [sb(f"nm{p}", [P, 2, 4]) for p in range(2)]
        den = [sb(f"den{p}", [P, QT, HEADS]) for p in range(2)]
        num = [sb(f"num{p}", [P, QT, HEADS]) for p in range(2)]
        share = [sb(f"share{p}", [P, QT, HEADS]) for p in range(2)]
        O1 = sb("O1", [P, HEADS * DV])
        O1T = sb("O1T", [P, HEADS // 2, P])

        ps = ctx.enter_context(nc.psum_tensor("ps", [P, 8, 512], F32))
        ps_s, ps_t, ps_pv, ps_m = ps[:, 0:2, :], ps[:, 2:4, :], ps[:, 4:6, :], ps[:, 6:8, :]

        def flat(ap):
            return ap.rearrange("p a d -> p (a d)")

        block = ctx.enter_context(nc.Block())

        @block.sync
        def _(sp):
            xv = A["L0_attn_x"].rearrange("b (q p) d -> p (b q) d", p=P)
            step = NT // 4
            for i in range(4):
                sp.dma_start(X[:, i * step:(i + 1) * step, :], xv[:, i * step:(i + 1) * step, :]).then_inc(s["x_loaded" if i else "x_first"], 16)
            loads = [(wraw[:, i, :], A[n]) for i, n in enumerate(("L0_attn_Wq", "L0_attn_Wk", "L0_attn_Wv"))]
            loads += [(wqkv[1][:, :, :], A["L0_ffn_w_qkv"].rearrange("d (t e) -> d t e", t=3)), (wo[:, :], A["L0_ffn_w_o"])]
            loads += [(lnw[:, i:i + 1], A[n].rearrange("(d a) -> d a", a=1))
                      for i, n in enumerate(("L0_ffn_ln1_w", "L0_ffn_ln1_b", "L0_ffn_ln2_w", "L0_ffn_ln2_b"))]
            loads += [(bqk[:, t:t + 1], A["L0_ffn_b_qkv"][t * D:(t + 1) * D].rearrange("(e a) -> e a", a=1)) for t in range(2)]
            loads += [(bv[:, :], A["L0_ffn_b_qkv"][2 * D:3 * D].rearrange("(a e) -> a e", a=1).broadcast_to([P, D])),
                      (bo[:, :], A["L0_ffn_b_o"].rearrange("(a e) -> a e", a=1).broadcast_to([P, D])),
                      (b2all[:, :, :], A["L0_ffn_b2"].rearrange("(a e) d -> a e d", a=1).broadcast_to([P, E0, D])),
                      (b1raw[:, :], A["L0_ffn_b1"].rearrange("e (f p) -> (e f) p", p=P)),
                      (wg[0][:, :], A["L0_ffn_w_gate"]), (wg1raw[:, :], A["L1_ffn_gate_w"])]
            for dst, src in loads:
                sp.dma_start(dst, src).then_inc(s["w_loaded"], 16)
            assert len(loads) == W_LOADS
            def stage(pas, q, j):
                q, j = q + j // 4, j % 4
                pas = pas if not isinstance(q, int) else q // (JOBS // 8)
                src = (YN, XN)[pas]
                if not isinstance(q, int) or 4 * q + j >= 2:
                    sp.wait_ge(s["xt_turned"], 4 * q + j - 1)
                sp.dma_start(xs[j % 2][:, :, :], src[:, ds(8 * q + 2 * j - 2 * B * pas, 2), :]).then_inc(xs_staged[j], 16)

            def send_rows(q, j):
                q, j = q + j // 4, j % 4
                sp.wait_ge(s["qk_split"], 16 * q + 4 * j + 4)
                for g in range(GROUPS):
                    for role, part, side, m in ((0, 2, 0, 1), (0, 1, 1, 1), (1, 0, 0, 2), (2, 2, 0, 2)):
                        sp.dma_start(rows[j][role:P:4, g, side:side + m, :].bitcast(F32),
                                     nat[j % 2][32 * g:32 * g + 32, part:part + m, :].bitcast(F32)).then_inc(rows_sent[j], 16)

            def send_m(q, j):
                q, j = q + j // 4, j % 4
                sp.wait_ge(s["m_copied"], 4 * q + j + 1)
                for g in range(GROUPS):
                    sp.dma_start(rows[j][31:P:32, g, 0, :].bitcast(F32), mT[j % 2][4 * g:4 * g + 4, :].bitcast(F32)).then_inc(m_sent[j], 16)

            def job(pas, q, j, more=4):
                send_m(q, j + 1)
                if more >= 4:
                    stage(pas, q, j + 4)
                if more >= 3:
                    send_rows(q, j + 3)

            sp.wait_ge(s["yn_ready"], FIRST)
            stage(0, 0, 0)
            stage(0, 0, 1)
            sp.wait_ge(s["rows_init"], 12)
            send_rows(0, 0)
            stage(0, 0, 2)
            send_rows(0, 1)
            stage(0, 0, 3)
            send_rows(0, 2)
            send_m(0, 0)
            sp.wait_ge(s["yn_ready"], NT)
            half_q = JOBS // 8
            for pas in range(2):
                q0 = half_q * pas
                job(pas, q0, 0)
                with sp.Fori(q0, q0 + half_q - 2) as q:
                    for j in range(1, 5):
                        job(pas, q, j)
                for j, more in ((1, 4), (2, 4), (3, 4), (4, 3)):
                    job(pas, q0 + half_q - 2, j, more if pas else 4)
                if pas == 0:
                    for j in range(5, 8):
                        job(pas, half_q - 2, j)

            sp.wait_ge(s["scattered"], 16 * NT * TOP)
            sp.wait_ge(s["weights_ready"], 1)

            def load_x(i, p):
                sp.dma_start(ex[p]["x"][:, 0:2, :], xg[0][ds(i * SLOTS, SLOTS), :].rearrange("(k p) d -> p k d", p=P)).then_inc(x_in[p], 16)

            def load_up(e, p):
                sp.dma_start(ex[p]["w1"][:, :], A["L0_ffn_w1"][ds(e, 1), :, :].rearrange("a d f -> d (a f)")).then_inc(up_in[p], 16)

            def load_down(e, p):
                sp.dma_start(ex[p]["w2"][:, :, :], A["L0_ffn_w2"][ds(e, 1), :, :].rearrange("a (f p) d -> p (a f) d", p=P)).then_inc(down_in[p], 16)

            def expert_of(i):
                return sp.value_load(emap[0:1, ds(i, 1)], min_val=0, max_val=E0 - 1)

            def store_step(i, p):
                sp.wait_ge(s["e_added"], i + 1)
                sp.dma_start(yg[0][ds(i * SLOTS, SLOTS), :].rearrange("(k p) d -> p k d", p=P), ex[p]["y"][:, 0:2, :]).then_inc(e_stored[p], 16)

            for i in range(2):
                e = expert_of(i)
                load_x(i, i)
                load_up(e, i)
                load_down(e, i)

            def next_loads(i, p, up=True, x=True, down=True):
                if up:
                    e = expert_of(i + 2)
                    sp.wait_ge(s["e_hidden"], i + 1)
                    load_up(e, p)
                e = expert_of(i + 1)
                store_step(i - 1, 1 - p)
                if x:
                    load_x(i + 3, 1 - p)
                if down:
                    load_down(e, 1 - p)

            e = expert_of(2)
            sp.wait_ge(s["e_hidden"], 1)
            load_x(2, 0)
            load_up(e, 0)
            sp.wait_ge(s["e_turned"], 2)
            load_x(3, 1)
            with sp.Fori(0, STEPS0 // 2 - 2) as h:
                for p in (1, 0):
                    next_loads(2 * h + 2 - p, p)
            next_loads(STEPS0 - 3, 1, x=False)
            next_loads(STEPS0 - 2, 0, up=False, x=False)
            store_step(STEPS0 - 2, 0)
            store_step(STEPS0 - 1, 1)
            for j, more in ((5, 2), (6, 1)):
                job(1, JOBS // 4 - 2, j, more)
            for p in range(2):
                sp.wait_ge(e_stored[p], 16 * (STEPS0 // 2))
            for i, (dst, n) in enumerate(((praw, "L1_attn_P_q"), (kraw, "L1_attn_P_k"), (oraw, "L1_attn_P_o"))):
                sp.wait_ge(s["combined"], 16 * i + 12)
                sp.dma_start(dst[:, :, :], A[n].rearrange("h d k -> d h k")).then_inc(s["p_loaded"], 16)
            sp.dma_start(Pv[:, :].rearrange("d (h v) -> d h v", h=HEADS), A["L1_attn_P_v"].rearrange("h d v -> d h v")).then_inc(s["p_loaded"], 16)

            sp.wait_ge(s["xn_ready"], 2 * NT)

            def stage1(b, p):
                if not isinstance(b, int):
                    sp.wait_ge(s["x1_ready"], b - 1)
                sp.dma_start(xs[p][:, :, :], XN[:, ds(2 * b, 2), :]).then_inc(xs_staged[p], 16)

            stage1(0, 0)
            stage1(1, 1)
            with sp.Fori(0, BEFORE // 2) as h:
                for p in range(2):
                    stage1(2 * h + p + 2, p)

            sp.wait_ge(s["scattered"], 32 * NT * TOP)
            sp.wait_ge(s["weights_ready"], 2)

            def load_tokens(e, p):
                sp.dma_start(ex[p]["x"][:, :, :], xg[1][ds(e * CAP, CAP), :].rearrange("(k p) d -> p k d", p=P)).then_inc(x_in[p], 16)

            def load_w1(e, p):
                sp.dma_start(ex[p]["w1"][:, 0:F1], A["L1_ffn_w1"][ds(e, 1), :, :].rearrange("a d f -> d (a f)")).then_inc(up_in[p], 16)

            def load_w2(e, p):
                sp.dma_start(ex[p]["w2"][:, 0:F1 // P, :], A["L1_ffn_w2"][ds(e, 1), :, :].rearrange("a (f p) d -> p (a f) d", p=P)).then_inc(down_in[p], 16)

            def store_expert(e, p):
                sp.wait_ge(s["e_added"], STEPS0 + e + 1)
                sp.dma_start(yg[1][ds(e * CAP, CAP), :].rearrange("(k p) d -> p k d", p=P), ex[p]["y"][:, :, :]).then_inc(e_stored[p], 16)

            for e in range(2):
                load_tokens(e, e)
                load_w1(e, e)
                load_w2(e, e)
            with sp.Fori(0, E1 // 2 - 1) as h:
                for p in range(2):
                    e = 2 * h + p
                    sp.wait_ge(s["e_turned"], STEPS0 + e + 1)
                    load_tokens(e + 2, p)
                    sp.wait_ge(s["e_hidden"], STEPS0 + e + 1)
                    load_w1(e + 2, p)
                    store_expert(e, p)
                    load_w2(e + 2, p)
            store_expert(E1 - 2, 0)
            store_expert(E1 - 1, 1)
            with sp.Fori(BEFORE // 2, B // 2 - 1) as h:
                for p in range(2):
                    stage1(2 * h + p + 2, p)

            ov = out.rearrange("b (q p) d -> p (b q) d", p=P)
            ends = [step, 2 * step, 3 * step, NT - QT, NT]
            for first_tile, end in zip([0] + ends, ends):
                sp.wait_ge(s["combined"], TOP * NT + TOP * end)
                if end == NT:
                    sp.wait_ge(s["y_added"], NT)
                sp.dma_start(ov[:, first_tile:end, :], X[:, first_tile:end, :]).then_inc(s["out_sent"], 16)
            sp.wait_ge(s["out_sent"], 16 * len(ends))

        @block.gpsimd
        def _(pool):
            pool.memset(ident[:, :], 0.0).then_inc(s["ident_zero"], 1)
            pool.memset(before[:, :], 1.0).then_inc(s["ident_zero"], 1)
            pool.memset(tri0[:, :, :], 0.0).then_inc(s["ident_zero"], 1)
            pool.wait_ge(s["ident_zero"], 3)
            pool.affine_select(out=ident[:, :], in_=ident[:, :], compare_op=ALU.not_equal, fill=1.0, base=0,
                               pattern=[[-1, P]], channel_multiplier=1).then_inc(s["ident_ready"], 1)
            pool.memset(zeros[:, :], 0.0).then_inc(s["zero_ready"], 1)
            pool.affine_select(out=before[:, :], in_=before[:, :], compare_op=ALU.is_gt, fill=0.0, base=0,
                               pattern=[[1, P]], channel_multiplier=-1).then_inc(s["consts_made"], 1)
            pool.affine_select(out=tri0[:, :, :], in_=tri0[:, :, :], compare_op=ALU.is_ge, fill=NEVER, base=0,
                               pattern=[[0, 4], [-1, P]], channel_multiplier=1).then_inc(s["consts_made"], 1)
            pool.memset(ones[:, :], 1.0).then_inc(s["consts_made"], 1)
            pool.iota(revi[:, :], pattern=[[-1, E1]], base=E1, channel_multiplier=0).then_inc(s["consts_made"], 1)
            pool.iota(stepi[:, :], pattern=[[1, STEPS0]], base=0, channel_multiplier=0).then_inc(s["consts_made"], 1)
            pool.iota(dumpi[:, :, :], pattern=[[P * TOP, NT], [1, TOP]], base=ROWS1, channel_multiplier=TOP).then_inc(s["consts_made"], 1)
            pool.iota(capi[:, :], pattern=[[CAP, E1]], base=0, channel_multiplier=0).then_inc(s["consts_made"], 1)
            for j in range(4):
                pool.memset(rows[j][:, :, 0, :].bitcast(F32), 0.0).then_inc(s["rows_init"], 1)
                pool.memset(rows[j][:, :, 1, :].bitcast(F32), 1.0).then_inc(s["rows_init"], 1)
                pool.memset(va[j][:, :, :, :], 0.0).then_inc(s["ident_zero"], 1)
                pool.wait_ge(s["ident_zero"], 4 + j)
                pool.memset(va[j][:, :, :, HD:HD + 1], 1.0).then_inc(s["rows_init"], 1)

            def scatter(l, rows_of, n):
                t, k = n // TOP, n % TOP
                pool.indirect_dma_start(
                    out=xg[l], out_offset=bass.IndirectOffsetOnAxis(ap=slot_to[:, k, t:t + 1].bitcast(U32), axis=0),
                    in_=rows_of[:, t, :], in_offset=None).then_inc(s["scattered"], 16)

            def gather(l, n):
                t, k = n // TOP, n % TOP
                if n >= 8:
                    pool.wait_ge(s["combined"], TOP * NT * l + n - 7)
                pool.indirect_dma_start(
                    out=got[n % 8][:, :], out_offset=None, in_=yg[l],
                    in_offset=bass.IndirectOffsetOnAxis(ap=slot_from[:, k, t:t + 1].bitcast(U32), axis=0)).then_inc(gathered[n % 8], 16)

            pool.wait_ge(s["xn_ready"], NT)
            pool.wait_ge(s["w_loaded"], 16 * W_LOADS)
            pool.tensor_tensor(HB[:, :, :], XN[:, :, :], bo[:, :].unsqueeze(1).broadcast_to([P, NT, D]), ALU.add).then_inc(s["hb_ready"], 1)
            pool.wait_ge(s["zero_ready"], 1)
            pool.wait_ge(s["exp_done"], 1)
            sent = 0
            for table, n in ((xg[0], ROWS0), (xg[1], ROWS1)):
                v = table[0:n, :].rearrange("(p r) c -> p (r c)", p=P)
                for c in range(0, n, 1024):
                    if sent:
                        pool.wait_ge(s["tables_zeroed"], 16 * sent)
                    pool.dma_start(v[:, c:c + 1024], zeros[:, :]).then_inc(s["tables_zeroed"], 16)
                    sent += 1
            pool.wait_ge(s["h_added"], B)
            pool.tensor_tensor(X[:, :, :], X[:, :, :], HB[:, :, :], ALU.add).then_inc(s["base_added"], 1)
            pool.wait_ge(s["tables_zeroed"], 16 * sent)
            pool.wait_ge(s["slots_ready"], 1)
            for n in range(TOP * NT):
                scatter(0, YN, n)
            for p in range(2):
                pool.wait_ge(e_stored[p], 16 * (STEPS0 // 2))
            for n in range(TOP * NT):
                gather(0, n)

            def diagonal(n, p):
                pool.wait_ge(s["exp0_done"], n + 1)
                if not (isinstance(n, int) and n < 2):
                    pool.wait_ge(s["diag_summed"], n - 1)
                eye = ident[:, :].unsqueeze(1).broadcast_to([P, 4, P])
                pool.tensor_tensor(DG[p][:, 0], EX0[p][:, :, :], eye, ALU.mult).then_inc(s["diag_masked"], 1)
                pool.wait_ge(s["exp1_done"], n + 1)
                pool.tensor_tensor(DG[p][:, 1], EX1[p][:, :, P:2 * P], eye, ALU.mult).then_inc(s["diag_masked"], 1)

            for n in range(4 * BEFORE):
                if n == 4 * RANKED:
                    pool.wait_ge(s["slots_ready"], 2)
                diagonal(n, n % 2)
                m = 3 * (n - 4 * RANKED)
                for m in range(max(m, 0), min(max(m + 3, 0), TOP * NT)):
                    scatter(1, XN, m)
            for p in range(2):
                pool.wait_ge(e_stored[p], 16 * (STEPS0 // 2 + E1 // 2))
            sent = 0
            for n in range(4 * BEFORE, 4 * B):
                diagonal(n, n % 2)
                if (n % 4 or n == 4 * BEFORE) if n < 4 * (BEFORE + 4) else n % 4 == 1:
                    for m in range(sent, min(sent + 4, TOP * NT)):
                        gather(1, m)
                    sent = min(sent + 4, TOP * NT)

        @block.scalar
        def _(act):
            def root(r, a=0, b=NT):
                act.wait_ge(s["spread_ready"], r + 1)
                act.activation(st[:, 4, a:b], st[:, 3, a:b], ACT.Sqrt).then_inc(s["root_ready"], 1)

            act.wait_ge(s["ident_ready"], 1)
            act.activation(identb[:, :], ident[:, :], ACT.Copy).then_inc(s["consts_made"], 1)
            root(0, 0, FIRST)
            root(1, 0, FIRST)
            for r, (src, dst, ready) in ((2, (X, XN, "xn_ready")), (3, (XN, YN, "yn_ready"))):
                root(r, FIRST, NT)
                act.wait_ge(s["shift_ready"], r - 1)
                for t in range(FIRST, NT):
                    act.activation(dst[:, t, :], src[:, t, :], ACT.Identity, scale=st[:, 5, t:t + 1], bias=st[:, 0, t:t + 1]).then_inc(s[ready], 1)
            def exps(n, u, skip=False):
                act.wait_ge(s["st_ready"], 8 * n + u + 1)
                if not skip:
                    act.wait_ge(s["pv_done"], 8 * n + u - 1)
                act.activation(probs[:, u % 2, :, :], ps_t.rearrange("p b (g q) -> p (b g) q", g=2), ACT.Exp,
                               scale=SCALE).then_inc(s["exp_done"], 1)

            def experts():
                def gelu0(i, p):
                    e = act.value_load(emap[0:1, ds(i, 1)], min_val=0, max_val=E0 - 1)
                    act.wait_ge(s["e_hidden"], i + 1)
                    if not isinstance(i, int) or i >= 2:
                        act.wait_ge(s["e_out"], i - 1)
                    for f in range(F0 // P):
                        last = act.activation(ex[p]["g"][:, f, 0:SLOTS], ps[:, 2 * p + f // 2, (f % 2) * SLOTS:(f % 2 + 1) * SLOTS],
                                              ACT.Gelu_apprx_tanh, bias=b1T[:, ds(e * (F0 // P) + f, 1)])
                    last.then_inc(s["e_gelu"], 1)

                act.wait_ge(s["weights_ready"], 1)
                gelu0(0, 0)
                gelu0(1, 1)
                with act.Fori(1, STEPS0 // 2) as h:
                    for p in range(2):
                        gelu0(2 * h + p, p)

            def attention(pas):
                q0 = JOBS // 8 * pas

                def copy_o(n):
                    act.wait_ge(s["ot_turned"], n + 1)
                    act.activation(oT[:, :], ps_m[:, 0, 0:S], ACT.Copy).then_inc(s["ot_copied"], 1)

                def job(n, first=False, new=False):
                    for u in range(UNITS):
                        exps(n, u, new and u < 2)
                        if pas == 0 and not first and u == UNITS - 2:
                            copy_o(n - 1)
                    act.wait_ge(s["pv_done"], 8 * n + 8)
                    if not new:
                        act.wait_ge(s["ct_turned"], n)
                    act.activation(ctxT[:, :, :], ps_pv.rearrange("p b (c q) -> p (b c) q", c=2), ACT.Copy).then_inc(s["ct_copied"], 1)

                n0 = 4 * q0
                last3 = range(n0 + JOBS // 2 - 3, n0 + JOBS // 2)
                if pas == 0:
                    job(n0, True, True)
                else:
                    job(n0 + 1)
                    act.wait_ge(s["odds_ready"], 1)
                    act.activation(tmp[:, 1, :], tmp[:, 0, :], ACT.Exp).then_inc(s["odds_ready"], 1)
                    for n in range(n0 + 2, n0 + 5):
                        job(n)
                with act.Fori(q0 + pas, q0 + JOBS // 8 - 1) as q:
                    for j in range(1, 5):
                        job(4 * q + j)
                if pas:
                    experts()
                for n in last3:
                    job(n)
                if pas == 0:
                    job(n0 + JOBS // 2)

            def route(l):
                for n in range(NT // 4):
                    act.wait_ge(s["rt_turned"], NT // 4 * l + n + 1)
                    if n >= 3:
                        act.wait_ge(s["rt_logits"], NT // 4 * l + n - 2)
                    if l == 0:
                        act.activation(rT[n % 3][:, :], ps[:, ROW_BANKS[n % 3], :], ACT.Identity, scale=lnw[:, 2:3], bias=lnw[:, 3:4]).then_inc(s["rt_copied"], 1)
                    else:
                        act.activation(rT[n % 3][:, :], ps[:, ROW_BANKS[n % 3], :], ACT.Copy).then_inc(s["rt_copied"], 1)

            attention(0)
            root(4)
            act.wait_ge(s["tables_zeroed"], 16 * ZEROINGS)
            route(0)
            attention(1)

            act.wait_ge(s["pq_turned"], 1)
            act.activation(PqT[:, :, :], ps_s.rearrange("p b (c d) -> p (b c) d", d=D), ACT.Copy).then_inc(s["pq_copied"], 1)
            act.wait_ge(s["pk_turned"], 1)
            act.activation(PkT[:, :, :], ps_t.rearrange("p b (c d) -> p (b c) d", d=D), ACT.Copy).then_inc(s["pk_copied"], 1)
            act.wait_ge(s["po_turned"], 1)
            act.activation(PoT[:, :, :], ps_m.rearrange("p b (c d) -> p (b c) d", d=D), ACT.Copy).then_inc(s["po_copied"], 1)
            act.wait_ge(s["a_made"], 1)
            act.activation(AH[:, :, :].rearrange("p (c a) d -> p a c d", a=2), ps[:, 0:4, :].rearrange("p (a b) (c d) -> p a (b c) d", a=2, d=D), ACT.Copy, scale=float(DK) ** 0.5).then_inc(s["a_copied"], 1)
            root(5)
            route(1)
            act.wait_ge(s["odds_ready"], 3)
            act.activation(TA[:, :, :], LG[:, :, :], ACT.Exp, scale=-1.0).then_inc(s["odds_ready"], 1)

            def copy_u(b, g):
                if not (isinstance(b, int) and b == 0 and g < 2):
                    act.wait_ge(s["s1_ready"], 4 * b + g - 1)
                act.wait_ge(s["u_ready"], 4 * b + g + 1)
                act.activation(U[g % 2][:, :, :], ps_s.rearrange("p b (c q) -> p (b c) q", c=2), ACT.Copy).then_inc(s["u_copied"], 1)

            def exps1(b, g, p):
                n, gp = 4 * b + g, g % 2
                if not (isinstance(b, int) and b == 0 and g < 2):
                    act.wait_ge(s["diag_masked"], 2 * n - 2)
                act.wait_ge(s["max0_ready"], n + 1)
                for i in range(4):
                    last = act.activation(EX0[gp][:, i, :], ps[:, 2, i * P:(i + 1) * P], ACT.Exp, bias=nm[gp][:, 0, i:i + 1],
                                          accum_out=den[p][:, 0, 4 * g + i:4 * g + i + 1])
                last.then_inc(s["exp0_done"], 1)
                act.wait_ge(s["max1_ready"], n + 1)
                for i in range(4):
                    last = act.activation(EX1[gp][:, i, :], ps[:, 3 + i // 2, (i % 2) * S:(i % 2 + 1) * S], ACT.Exp, bias=nm[gp][:, 1, i:i + 1],
                                          accum_out=den[p][:, 1, 4 * g + i:4 * g + i + 1])
                last.then_inc(s["exp1_done"], 1)

            def ahead(b, g):
                copy_u(b + (g + 2) // 4, (g + 2) % 4)

            def copy_o(b, k, dst=O1T[:, :, :], bank=5):
                act.wait_ge(s["o1_turned"], 2 * b + k + 1)
                act.activation(dst, ps[:, bank:bank + 2, :].rearrange("p b (c t) -> p (b c) t", t=P), ACT.Copy).then_inc(s["o1_copied"], 1)

            def sequence(b, p, last=False, prev=True):
                if not (isinstance(b, int) and b < 2):
                    act.wait_ge(s["share_ready"], b - 1)
                for g in range(4):
                    exps1(b, g, p)
                    if not (last and g >= 2):
                        ahead(b, g)
                    if prev and g % 2 == 0:
                        copy_o(b - 1, g // 2)

            def gelu1(e, p):
                act.wait_ge(s["e_out"], STEPS0 + e - 1)
                for f in range(F1 // P):
                    if f:
                        act.wait_ge(s["e_hidden"], STEPS0 + e + 1)
                    else:
                        act.wait_ge(s["e_half"], e + 1)
                    last = act.activation(ex[p]["g"][:, 2 * f:2 * f + 2, :], ps[:, 2 + 2 * f:4 + 2 * f, 0:HALF], ACT.Gelu)
                last.then_inc(s["e_gelu"], 1)

            copy_u(0, 0)
            copy_u(0, 1)
            sequence(0, 0, prev=False)
            sequence(1, 1)
            sequence(2, 0)
            with act.Fori(1, BEFORE // 2) as h:
                for p in (1, 0):
                    sequence(2 * h + 2 - p, p)
            for e in range(E1):
                gelu1(e, e % 2)
            with act.Fori(BEFORE // 2, B // 2 - 1) as h:
                for p in (1, 0):
                    sequence(2 * h + 2 - p, p)
            sequence(B - 1, 1, last=True)
            copy_o(B - 1, 0)
            copy_o(B - 1, 1, U[1][:, :, :].rearrange("p i (c t) -> p (i c) t", t=P), bank=3)

        @block.vector
        def _(dve):
            steps = [0]

            def then(ins):
                steps[0] += 1
                ins.then_inc(s["dve_step"], 1)
                dve.wait_ge(s["dve_step"], steps[0])

            def take_stats(src, t):
                dve.bn_stats(flat(stats[:, ds(t, 1), :]), flat(src[:, ds(t, 1), :])).then_inc(s["stats_taken"], 1)

            def layer_norm(r, src, dst, ready, done, taken, a=0, b=NT, stats_too=False, by_act=False):
                if stats_too:
                    for t in range(a, b):
                        dve.bn_stats(stats[:, t, :], src[:, t, :]).then_inc(s["stats_taken"], 1)
                dve.wait_ge(s["stats_taken"], taken)
                me, mo, ve, vo = (stats[:, a:b, k] for k in (1, 4, 2, 5))
                mean, dif, var, spread, deviation, over = (st[:, k, a:b] for k in range(6))
                dve.tensor_tensor(mean, me, mo, ALU.add).then_inc(s["dve_step"], 1)
                dve.tensor_tensor(dif, me, mo, ALU.subtract).then_inc(s["dve_step"], 1)
                steps[0] += 2
                then(dve.tensor_tensor(var, ve, vo, ALU.add))
                then(dve.tensor_scalar(mean, mean, 0.5, None, ALU.mult))
                then(dve.scalar_tensor_tensor(out=dif, in0=dif, scalar=0.25, in1=dif, op0=ALU.mult, op1=ALU.mult))
                then(dve.scalar_tensor_tensor(out=var, in0=var, scalar=1.0 / D, in1=dif, op0=ALU.mult, op1=ALU.add))
                dve.tensor_scalar(spread, var, EPS, None, ALU.add).then_inc(s["spread_ready"], 1)
                if by_act:
                    dve.wait_ge(s["root_ready"], r + 1)
                    then(dve.reciprocal(over, deviation))
                    dve.scalar_tensor_tensor(out=mean, in0=mean, scalar=-1.0, in1=over, op0=ALU.mult, op1=ALU.mult).then_inc(s["shift_ready"], 1)
                    return
                mean_of = st[:, 0, a:a + 8].unsqueeze(2).broadcast_to([P, 8, D])
                dve.tensor_tensor(dst[:, a:a + 8, :], src[:, a:a + 8, :], mean_of, ALU.subtract).then_inc(s["dve_step"], 1)
                steps[0] += 1
                dve.wait_ge(s["dve_step"], steps[0])
                dve.wait_ge(s["root_ready"], r + 1)
                then(dve.reciprocal(over, deviation))
                over_of = st[:, 5, a:a + 8].unsqueeze(2).broadcast_to([P, 8, D])
                dve.tensor_tensor(dst[:, a:a + 8, :], dst[:, a:a + 8, :], over_of, ALU.mult).then_inc(s[ready], 8)
                for t in range(a + 8, b):
                    dve.tensor_scalar(dst[:, t, :], src[:, t, :], st[:, 0, t:t + 1], st[:, 5, t:t + 1], ALU.subtract, ALU.mult).then_inc(s[ready], 1)
                dve.wait_ge(s[ready], done)

            dve.wait_ge(s["x_first"], 16)
            layer_norm(0, X, XN, "xn_ready", FIRST, FIRST, 0, FIRST, stats_too=True)
            layer_norm(1, XN, YN, "yn_ready", FIRST, 2 * FIRST, 0, FIRST, stats_too=True)
            dve.wait_ge(s["w_loaded"], 16 * W_LOADS)

            def set_up():
                dve.wait_ge(s["w_turned"], 1)
                dve.tensor_copy(wqkv[0][:, :, :], ps_pv[:, 0, 0:3 * D].rearrange("p (t e) -> p t e", t=3)).then_inc(s["w_turned_copied"], 1)
                dve.tensor_copy(wg[1][:, :], ps_pv[:, 1, 0:E1]).then_inc(s["w_turned_copied"], 1)
                dve.tensor_copy(b1T[:, :], ps_pv[:, 1, E1:E1 + E0 * F0 // P]).then_inc(s["w_turned_copied"], 1)
                dve.wait_ge(s["consts_made"], 8)
                for dst, src in ((rev[:, :], revi[:, :]), (stepf[:, :], stepi[:, :]), (dump[:, :, :], dumpi[:, :, :]), (capb[:, :], capi[:, :])):
                    then(dve.tensor_copy(dst, src))

            dve.wait_ge(s["rows_init"], 12)

            def attention(pas):
                q0 = JOBS // 8 * pas
                n0 = 4 * q0

                def turn(n, p, pas=pas):
                    dve.wait_ge(s["xt_turned"], n + 1)
                    if pas == 1:
                        dve.tensor_copy(xT[p][:, :], ps_m[:, 1, 0:S]).then_inc(s["xt_copied"], 1)
                    else:
                        dve.tensor_scalar(xT[p][:, :], ps_m[:, 1, 0:S], lnw[:, 0:1], lnw[:, 1:2], ALU.mult, ALU.add).then_inc(s["xt_copied"], 1)

                def split(n, j, t, pas=pas):
                    p, hi, lo = j % 2, (2, 1)[t], (0, 3)[t]
                    if t == 0:
                        dve.wait_ge(s["qkv_done"], n + 1)
                    src = ps_m[:, 1, t * S:(t + 1) * S]
                    if pas == 1:
                        dve.tensor_copy(nat[p][:, hi, :], src).then_inc(s["qk_split"], 1)
                        dve.wait_ge(s["qk_split"], 4 * n + 2 * t + 1)
                        dve.tensor_tensor(nat[p][:, lo, :], src, nat[p][:, hi, :].bitcast(F32), ALU.subtract).then_inc(s["qk_split"], 1)
                    else:
                        dve.tensor_scalar(nat[p][:, hi, :], src, bqk[:, t:t + 1], None, ALU.add).then_inc(s["qk_split"], 1)
                        dve.wait_ge(s["qk_split"], 4 * n + 2 * t + 1)
                        dve.scalar_tensor_tensor(out=nat[p][:, lo, :], in0=src, scalar=bqk[:, t:t + 1], in1=nat[p][:, hi, :].bitcast(F32),
                                                 op0=ALU.add, op1=ALU.subtract).then_inc(s["qk_split"], 1)

                def keep_v(n, j, pas=pas):
                    vsrc = ps_m[:, 0, S:2 * S].rearrange("p (k h e) -> p k h e", k=QT, h=HEADS)
                    for k in range(QT):
                        if pas == 1:
                            dve.tensor_copy(va[j % 4][:, k, :, 0:HD], vsrc[:, k]).then_inc(s["v_copied"], 1)
                        else:
                            dve.tensor_tensor(va[j % 4][:, k, :, 0:HD], vsrc[:, k], bv[:, :].rearrange("p (h e) -> p h e", h=HEADS), ALU.add).then_inc(s["v_copied"], 1)

                def reduce(n, p, u, src=ps_s):
                    c, ip, sq = u // 4, u // 2 % 2, u % 2
                    dve.wait_ge(s["s_ready"], 8 * n + u + 1)
                    dve.tensor_reduce(negm[p][:, sq, :].rearrange("p (g i) -> p i g", i=4)[:, 2 * ip:2 * ip + 2, 2 * c:2 * c + 2],
                                      src.rearrange("p b (g k) -> p b g k", g=2), AX.X, ALU.max, negate=True).then_inc(s["s_reduced"], 1)

                def copy_m(n, p):
                    dve.wait_ge(s["m_turned"], n + 1)
                    dve.tensor_copy(mT[p][:, :], ps_m[0:HEADS, 0, S:2 * S]).then_inc(s["m_copied"], 1)

                def normalise(n):
                    dve.wait_ge(s["ct_turned"], n + 1)
                    dve.reciprocal(rec[:, :], ps_m.rearrange("p b (k r) -> p (b k) r", r=32)[:, :, HD]).then_inc(s["rec_done"], 1)
                    dve.wait_ge(s["rec_done"], n + 1)
                    for k in range(QT):
                        wk = ps_m[:, k, :].rearrange("p (c i dg r) -> p c i dg r", c=2, i=4, dg=2)
                        rk = rec[:, 16 * k:16 * k + 16].rearrange("p (c i dg) -> p c i dg", c=2, i=4)
                        ok = o[:, k, :].rearrange("p (c dg i e) -> p c i dg e", i=4, c=2, dg=2)
                        for c in range(2):
                            dve.tensor_tensor(ok[:, c], wk[:, c, :, :, 0:HD], rk[:, c].unsqueeze(3).broadcast_to([P, 4, 2, HD]),
                                              ALU.mult).then_inc(s["o_ready"], 1)

                def add(n):
                    if pas == 0:
                        dve.wait_ge(s["wo_done"], n + 1)
                        h = HB[:, ds(2 * n, 2), :]
                        dve.tensor_tensor(h, ps_m[:, 0, S:2 * S].rearrange("p (k d) -> p k d", k=QT), h, ALU.add).then_inc(s["h_added"], 1)
                        dve.wait_ge(s["h_added"], n + 1)
                        for k in range(QT):
                            take_stats(HB, 2 * n + k)
                    else:
                        dve.wait_ge(s["o_ready"], 4 * n + 4)
                        x = X[:, ds(2 * n - 2 * B, 2), :]
                        dve.tensor_tensor(x, x, o[:, :, :], ALU.add).then_inc(s["x_added"], 1)
                        dve.wait_ge(s["x_added"], n - B + 1)

                if pas == 0:
                    for j in range(3):
                        turn(j, j % 2)
                        split(j, j, 0)
                        split(j, j, 1)
                        keep_v(j, j)
                        if j == 1:
                            dve.wait_ge(s["x_loaded"], 48)
                            layer_norm(2, X, XN, "xn_ready", NT, NT + FIRST, FIRST, NT, stats_too=True, by_act=True)
                    dve.wait_ge(s["xn_ready"], NT)
                    layer_norm(3, XN, YN, "yn_ready", NT, 2 * NT, FIRST, NT, stats_too=True, by_act=True)
                    set_up()
                    for j in range(2):
                        for u in range(UNITS):
                            reduce(j, j, u, (ps_s, ps_t)[u % 2])
                        if j == 0:
                            copy_m(0, 0)

                def job(q, j, more, first=False, chain=None, steps_each=0):
                    n, p = 4 * q + j, j % 2
                    of = pas if not isinstance(n, int) else (n + 3) // (JOBS // 2)
                    for u in range(UNITS):
                        if more >= 2:
                            reduce(n + 2, p, u)
                        for _ in range(steps_each):
                            next(chain, None)
                        if more >= 1 and u == 0:
                            copy_m(n + 1, 1 - p)
                        if more >= 3:
                            if u == 0:
                                turn(n + 3, 1 - p, of)
                            if u in (1, 2):
                                split(n + 3, j + 3, u - 1, of)
                            if u == 3:
                                keep_v(n + 3, j + 3, of)
                        if u == 4 and not first:
                            normalise(n - 1)
                            if pas == 1:
                                add(n - 1)
                        if isinstance(n, int) and n > n0 + JOBS // 2 - 4 and pas == 1 and u % 2:
                            combine(0, 2 * (n - n0 - JOBS // 2 + 3) + u // 4, u // 2 % 2)
                    if pas == 0 and not first:
                        add(n - 1)

                last = q0 + JOBS // 8 - 1
                chain = ranking(0) if pas else iter(())
                if pas == 0:
                    dve.wait_ge(s["hb_ready"], 1)
                if pas == 0:
                    job(q0, 0, 3, True)
                if pas:
                    for j in range(1, 5):
                        job(q0, j, 3, False, chain, 2)
                    for _ in chain:
                        pass
                with dve.Fori(q0 + pas, last) as q:
                    for j in range(1, 5):
                        job(q, j, 3)
                if pas:
                    experts()
                for j in range(1, 5 - pas):
                    job(last, j, 3 if pas == 0 else 3 - j)
                if pas:
                    normalise(4 * last + 3)
                    add(4 * last + 3)

            def experts():
                def turn0(i, p):
                    dve.wait_ge(s["e_turned"], i + 1)
                    if not isinstance(i, int) or i >= 2:
                        dve.wait_ge(s["e_hidden"], i - 1)
                    dve.tensor_scalar(ex[p]["xT"][:, 0:SLOTS], ps[:, 4 + p, 0:SLOTS], lnw[:, 2:3], lnw[:, 3:4], ALU.mult, ALU.add).then_inc(s["e_copied"], 1)

                def add0(i, p, h):
                    e = dve.value_load(emap[0:1, ds(i, 1)], min_val=0, max_val=E0 - 1)
                    dve.wait_ge(s["e_out"], i + 1)
                    if not isinstance(h, int) or h:
                        dve.wait_ge(e_stored[p], 16 * h)
                    dve.tensor_tensor(ex[p]["y"][:, 0:2, :], ps[:, 6 + p, 0:SLOTS].rearrange("p (k d) -> p k d", k=2),
                                      b2all[:, ds(e, 1), :].broadcast_to([P, 2, D]), ALU.add).then_inc(s["e_added"], 1)

                turn0(0, 0)
                turn0(1, 1)
                for p in range(2):
                    turn0(2 + p, p)
                    add0(p, p, 0)
                with dve.Fori(1, STEPS0 // 2 - 1) as h:
                    for p in range(2):
                        turn0(2 * h + 2 + p, p)
                        add0(2 * h + p, p, h)
                add0(STEPS0 - 2, 0, STEPS0 // 2 - 1)
                add0(STEPS0 - 1, 1, STEPS0 // 2 - 1)

            def combine(l, half, parity, after_y=True):
                h = 2 * half + parity
                added, last = (("x_added", h + 1), ("y_added", 2 * h + 2))[l]
                if after_y:
                    dve.wait_ge(s[added], last)
                for n in range(4):
                    t, k = n // 2, n % 2
                    x = flat(X[:, ds(2 * h + t, 1), :])
                    dve.wait_ge(gathered[4 * parity + n], 16 * (NT // 4 * l + half + 1))
                    if k:
                        dve.wait_ge(s["combined"], TOP * NT * l + 4 * h + n)
                    dve.scalar_tensor_tensor(out=x, in0=got[4 * parity + n][:, :], scalar=tw[:, k, ds(2 * h + t, 1)], in1=x,
                                             op0=ALU.mult, op1=ALU.add).then_inc(s["combined"], 1)
                    if k and l == 0:
                        dve.wait_ge(s["combined"], 4 * h + n + 1)
                        take_stats(X, 2 * h + t)

            attention(0)
            dve.wait_ge(s["h_added"], B)
            layer_norm(4, HB, YN, "yn_ready", 2 * NT, 3 * NT)

            def all_tiles(ap):
                return ap.unsqueeze(1).broadcast_to([P, NT, ap.shape[-1]])

            def all_experts(ap, E):
                return ap.unsqueeze(2).broadcast_to([P, NT, E])

            def route(l):
                E = (E0, E1)[l]
                r0 = NT // 4 * l
                for n in range(NT // 4):
                    dve.wait_ge(s["rt_logits"], r0 + n + 1)
                    dve.tensor_copy(LG[:, 4 * n:4 * n + 4, 0:E], ps[:, 2 + n % 2, 0:4 * E].rearrange("p (k e) -> p k e", k=4)).then_inc(s["rt_kept"], 1)
                dve.wait_ge(s["rt_kept"], r0 + NT // 4)

                if l == 1:
                    dve.tensor_copy(tmp[:, 0, :], LG[:, :, 0]).then_inc(s["odds_ready"], 1)

            def ranking(l):
                E = (E0, E1)[l]
                lg, ta, tb, rk = (t[:, :, 0:E] for t in (LG, TA, TB, RK))
                revb = all_tiles(rev[:, E1 - E:E1])
                if l == 1:
                    dve.wait_ge(s["odds_ready"], 4)
                    then(dve.tensor_scalar(tb, ta, 1.0, None, ALU.add))
                    yield
                    then(dve.reciprocal(lg, tb))
                    yield
                for k in range(TOP):
                    then(dve.tensor_reduce(top[:, k, :], lg, AX.X, ALU.max))
                    yield
                    then(dve.tensor_tensor(ta, lg, all_experts(top[:, k, :], E), ALU.is_equal))
                    yield
                    then(dve.tensor_tensor(ta, ta, revb, ALU.mult))
                    yield
                    then(dve.tensor_reduce(tj[:, k, :], ta, AX.X, ALU.max))
                    yield
                    then(dve.tensor_tensor(OH[:, k, :, 0:E], revb, all_experts(tj[:, k, :], E), ALU.is_equal))
                    yield
                    if k == 0:
                        then(dve.tensor_scalar(ta, OH[:, 0, :, 0:E], -1.0, 1.0, ALU.mult, ALU.add))
                        yield
                        then(dve.tensor_tensor(lg, lg, ta, ALU.mult))
                        yield
                        then(dve.scalar_tensor_tensor(out=lg, in0=OH[:, 0, :, 0:E], scalar=-3e38, in1=lg, op0=ALU.mult, op1=ALU.add))
                        yield
                if l == 0:
                    dve.tensor_tensor(tmp[:, 0, :], top[:, 1, :], top[:, 0, :], ALU.subtract).then_inc(s["odds_ready"], 1)
                dve.tensor_tensor(rk, OH[:, 0, :, 0:E], OH[:, 1, :, 0:E], ALU.add).then_inc(s["sums_ready"], 1)
                yield
                dve.wait_ge(s["sums_ready"], 2 * l + 2)
                tot, own = total[:, :, 0:E], inside[:, :, 0:E]
                at = (ps_m[:, 0, 0:NT * E], ps_m[:, 0, NT * E:2 * NT * E]) if l == 0 else (ps[:, 5, :], ps[:, 6, :])
                then(dve.tensor_copy(own, at[0].rearrange("p (t e) -> p t e", e=E)))
                yield
                then(dve.tensor_copy(tot, at[1].rearrange("p (t e) -> p t e", e=E)))
                yield
                dve.tensor_copy(ta, tot).then_inc(s["sums_kept"], 1)
                dve.wait_ge(s["sums_kept"], l + 1)
                a, b = ta, tb
                k = 1
                while k < NT:
                    dve.tensor_copy(b[:, 0:k, :], a[:, 0:k, :]).then_inc(s["dve_step"], 1)
                    steps[0] += 1
                    then(dve.tensor_tensor(b[:, k:NT, :], a[:, k:NT, :], a[:, 0:NT - k, :], ALU.add))
                    yield
                    a, b, k = b, a, 2 * k
                then(dve.tensor_tensor(b, a, tot, ALU.subtract))
                yield
                then(dve.tensor_tensor(rk, own, b, ALU.add))
                yield
                if l == 0:
                    then(dve.tensor_scalar(cnt[:, 0, :], a[:, NT - 1, :], float(SLOTS - 1), None, ALU.add))
                    yield
                    then(dve.tensor_copy(cnti[:, :], cnt[:, 0, :]))
                    yield
                    then(dve.tensor_scalar(cnti[:, :], cnti[:, :], SLOTS.bit_length() - 1, None, ALU.logical_shift_right))
                    yield
                    then(dve.tensor_copy(cnt[:, 1, :], cnti[:, :]))
                    yield
                    then(dve.tensor_copy(cnt[:, 2, :], cnt[:, 1, :]))
                    yield
                    x, y, k = 2, 3, 1
                    while k < E:
                        then(dve.tensor_copy(cnt[:, y, 0:k], cnt[:, x, 0:k]))
                        yield
                        then(dve.tensor_tensor(cnt[:, y, k:E], cnt[:, x, k:E], cnt[:, x, 0:E - k], ALU.add))
                        yield
                        x, y, k = y, x, 2 * k
                    for e in range(E):
                        if e == 0:
                            then(dve.tensor_scalar(emapf[:, :], stepf[:, :], cnt[:, x, 0:1], None, ALU.is_ge))
                            yield
                        else:
                            then(dve.scalar_tensor_tensor(out=emapf[:, :], in0=stepf[:, :], scalar=cnt[:, x, e:e + 1], in1=emapf[:, :],
                                                          op0=ALU.is_ge, op1=ALU.add))
                            yield
                    then(dve.tensor_scalar(emap[:, :], emapf[:, :], float(E - 1), None, ALU.min))
                    yield
                    then(dve.tensor_tensor(cnt[:, y, :], cnt[:, x, :], cnt[:, 1, :], ALU.subtract))
                    yield
                    then(dve.tensor_scalar(cnt[:, y, :], cnt[:, y, :], float(SLOTS), None, ALU.mult))
                    yield
                    then(dve.tensor_tensor(rk, rk, all_tiles(cnt[:, y, :]), ALU.add))
                    yield
                else:
                    then(dve.tensor_scalar(tb if a is ta else ta, rk, float(CAP), None, ALU.is_lt))
                    yield
                    ok = tb if a is ta else ta
                    spare = a
                    then(dve.tensor_tensor(rk, rk, all_tiles(capb[:, :]), ALU.add))
                    yield
                for k in range(TOP):
                    w = tb if l == 0 else spare
                    then(dve.tensor_tensor(w, OH[:, k, :, 0:E], rk, ALU.mult))
                    yield
                    then(dve.tensor_reduce(slot[:, k, :], w, AX.X, ALU.add))
                    yield
                    if l == 1:
                        then(dve.tensor_tensor(w, OH[:, k, :, 0:E], ok, ALU.mult))
                        yield
                        then(dve.tensor_reduce(tj[:, k, :], w, AX.X, ALU.add))
                        yield
                        then(dve.tensor_tensor(tmp[:, 2, :], slot[:, k, :], dump[:, :, k], ALU.subtract))
                        yield
                        then(dve.tensor_tensor(tmp[:, 2, :], tmp[:, 2, :], tj[:, k, :], ALU.mult))
                        yield
                        then(dve.tensor_tensor(tmp[:, 2, :], tmp[:, 2, :], dump[:, :, k], ALU.add))
                        yield
                        then(dve.tensor_copy(slot_to[:, k, :], tmp[:, 2, :]))
                        yield
                        then(dve.tensor_tensor(slot[:, k, :], slot[:, k, :], tj[:, k, :], ALU.mult))
                        yield
                    else:
                        then(dve.tensor_copy(slot_to[:, k, :], slot[:, k, :]))
                        yield
                    then(dve.tensor_copy(slot_from[:, k, :], slot[:, k, :]))
                    yield
                dve.tensor_copy(tmp[:, 3, :], top[:, 0, :]).then_inc(s["slots_ready"], 1)

                if l == 0:
                    dve.wait_ge(s["odds_ready"], 2)
                    then(dve.tensor_scalar(tmp[:, 2, :], tmp[:, 1, :], 1.0, None, ALU.add))
                    yield
                    then(dve.reciprocal(tw[:, 0, :], tmp[:, 2, :]))
                    yield
                    then(dve.tensor_tensor(tw[:, 1, :], tw[:, 0, :], tmp[:, 1, :], ALU.mult))
                    yield
                else:
                    then(dve.tensor_tensor(tmp[:, 1, :], top[:, 0, :], top[:, 1, :], ALU.add))
                    yield
                    then(dve.tensor_scalar(tmp[:, 1, :], tmp[:, 1, :], 1e-6, None, ALU.add))
                    yield
                    then(dve.reciprocal(tmp[:, 2, :], tmp[:, 1, :]))
                    yield
                    for k in range(TOP):
                        then(dve.tensor_tensor(tw[:, k, :], top[:, k, :], tmp[:, 2, :], ALU.mult))
                        yield
                        then(dve.tensor_tensor(tw[:, k, :], tw[:, k, :], tj[:, k, :], ALU.mult))
                        yield
                then(dve.tensor_copy(tmp[:, 0, :], tw[:, 0, :]))
                yield
                dve.tensor_copy(tmp[:, 1, :], tw[:, 1, :]).then_inc(s["weights_ready"], 1)
                dve.wait_ge(s["weights_ready"], l + 1)

            dve.wait_ge(s["tables_zeroed"], 16 * ZEROINGS)
            route(0)
            dve.wait_ge(s["base_added"], 1)
            attention(1)
            for h in range(12, NT // 2):
                combine(0, h // 2, h % 2)

            layer_norm(5, X, XN, "xn_ready", 2 * NT, 4 * NT)
            route(1)

            def turn_l1(b, p):
                dve.wait_ge(s["x1_ready"], b + 1)
                dve.tensor_copy(xT[p][:, :], ps[:, 7, P:P + S]).then_inc(s["x_high"], 1)
                dve.tensor_copy(xH[p][:, :], ps[:, 7, P:P + S]).then_inc(s["x_high"], 1)
                dve.wait_ge(s["x_high"], 2 * b + 2)
                dve.tensor_tensor(xL[p][:, :], ps[:, 7, P:P + S], xH[p][:, :].bitcast(F32), ALU.subtract).then_inc(s["x1_copied"], 1)

            def maxima(b, g):
                n, gp = 4 * b + g, g % 2
                if not (isinstance(n, int) and n < 2):
                    dve.wait_ge(s["exp1_done"], n - 1)
                dve.wait_ge(s["s0_ready"], n + 1)
                dve.tensor_reduce(nm[gp][:, 0, :], ps[:, 2, :].rearrange("p (i k) -> p i k", i=4), AX.X, ALU.max, negate=True).then_inc(s["max0_ready"], 1)
                dve.wait_ge(s["s1_ready"], n + 1)
                dve.tensor_reduce(nm[gp][:, 1, :], ps[:, 3:5, :].rearrange("p b (i k) -> p (b i) k", i=2), AX.X, ALU.max, negate=True).then_inc(s["max1_ready"], 1)

            def diagonal(b, g, p):
                n, gp = 4 * b + g, g % 2
                dve.wait_ge(s["diag_masked"], 2 * n + 2)
                dve.tensor_reduce(num[p][:, :, 4 * g:4 * g + 4], DG[gp][:, :, :, :], AX.X, ALU.add).then_inc(s["diag_summed"], 1)

            def shares(b, p):
                dve.wait_ge(s["exp1_done"], 4 * b + 4)
                dve.wait_ge(s["diag_summed"], 4 * b + 4)
                dve.reciprocal(share[p][:, :, :], den[p][:, :, :]).then_inc(s["rec_done"], 1)
                dve.wait_ge(s["rec_done"], JOBS + b + 1)
                dve.tensor_tensor(share[p][:, :, :], share[p][:, :, :], num[p][:, :, :], ALU.mult).then_inc(s["share_ready"], 1)
                dve.wait_ge(s["share_ready"], b + 1)

            def weigh(b, k, p, dst=O1[:, :], bank=5):
                dve.wait_ge(s["v1_ready"], 2 * b + k + 1)
                dve.tensor_tensor(dst.rearrange("p (h v) -> p h v", h=HEADS), ps[:, bank:bank + 2, :].rearrange("p b (h v) -> p (b h) v", v=DV),
                                  share[p][:, k, :].unsqueeze(2).broadcast_to([P, HEADS, DV]), ALU.mult).then_inc(s["o1_ready"], 1)

            def add_y(b, k, bank=7):
                dve.wait_ge(s["y_ready"], 2 * b + k + 1)
                x = flat(X[:, ds(2 * b + k, 1), :])
                dve.tensor_tensor(x, ps[:, bank, 0:D], x, ALU.add).then_inc(s["y_added"], 1)

            def experts1():
                def turn1(e, p):
                    dve.wait_ge(s["e_turned"], STEPS0 + e + 1)
                    dve.tensor_copy(ex[p]["xT"][:, :], ps[:, 0:2, :].rearrange("p b n -> p (b n)")[:, 0:CAP]).then_inc(s["e_copied"], 1)

                def add1(e, p, h):
                    dve.wait_ge(s["e_out"], STEPS0 + e + 1)
                    dve.wait_ge(e_stored[p], 16 * (STEPS0 // 2) + 16 * h)
                    dve.tensor_copy(ex[p]["y"][:, :, :], ps[:, 6:8, :].rearrange("p b (k d) -> p (b k) d", d=D)[:, 0:CT, :]).then_inc(s["e_added"], 1)

                turn1(0, 0)
                with dve.Fori(0, E1 // 2 - 1) as h:
                    for p in range(2):
                        turn1(2 * h + p + 1, 1 - p)
                        add1(2 * h + p, p, h)
                turn1(E1 - 1, 1)
                add1(E1 - 2, 0, E1 // 2 - 1)
                add1(E1 - 1, 1, E1 // 2 - 1)

            def sequence(b, p, prev=True, nxt=True, pair=None, chain=None, steps_each=0, late=None):
                def rank():
                    for _ in range(steps_each):
                        next(chain, None)

                maxima(b, 0)
                rank()
                if prev:
                    diagonal(b - 1, 3, 1 - p)
                    shares(b - 1, 1 - p)
                    weigh(b - 1, 0, 1 - p)
                maxima(b, 1)
                rank()
                diagonal(b, 0, p)
                if prev:
                    weigh(b - 1, 1, 1 - p)
                if nxt:
                    turn_l1(b + 1, 1 - p)
                if pair is not None:
                    combine(1, *pair)
                maxima(b, 2)
                rank()
                if prev:
                    add_y(b - 1, 0)
                diagonal(b, 1, p)
                if pair is not None:
                    combine(1, pair[0] + pair[1], 1 - pair[1])
                maxima(b, 3)
                rank()
                if prev:
                    add_y(b - 1, 1)
                diagonal(b, 2, p)
                if pair is not None:
                    combine(1, pair[0] + 1, pair[1])
                if late is not None:
                    combine(1, late // 2, late % 2)

            turn_l1(0, 0)
            dve.tensor_copy(PvH[:, :], Pv[:, :]).then_inc(s["pv_high"], 1)
            dve.wait_ge(s["pv_high"], 1)
            dve.tensor_tensor(PvL[:, :], Pv[:, :], PvH[:, :].bitcast(F32), ALU.subtract).then_inc(s["pv_low"], 1)
            chain = ranking(1)
            sequence(0, 0, prev=False, chain=chain, steps_each=6)
            for b in range(1, RANKED):
                sequence(b, b % 2, chain=chain, steps_each=6)
            for _ in chain:
                pass
            with dve.Fori(RANKED // 2, BEFORE // 2) as h:
                for p in (1, 0):
                    sequence(2 * h + 2 - p, p)
            experts1()
            with dve.Fori(BEFORE // 2, BEFORE // 2 + 2) as h:
                sequence(2 * h + 1, 1, pair=(3 * h - 3 * (BEFORE // 2), 0))
                sequence(2 * h + 2, 0, pair=(3 * h - 3 * (BEFORE // 2) + 1, 1))
            for b in range(BEFORE + 4, B):
                sequence(b, b % 2, nxt=(b < B - 1), late=b - 1)
            diagonal(B - 1, 3, 1)
            shares(B - 1, 1)
            weigh(B - 1, 0, 1)
            weigh(B - 1, 1, 1, flat(U[0]), bank=0)
            combine(1, (B - 1) // 2, (B - 1) % 2, after_y=False)
            dve.wait_ge(s["combined"], 2 * TOP * NT)
            add_y(B - 1, 0)
            add_y(B - 1, 1, bank=2)


        @block.tensor
        def _(pe):
            pe.wait_ge(s["ident_ready"], 1)
            pe.wait_ge(s["w_loaded"], 16 * W_LOADS)
            for t in range(3):
                pe.transpose(ps_pv[:, 0, t * D:(t + 1) * D], wraw[:, t, :], ident[:, :])
            pe.transpose(ps_pv[:, 1, 0:E1], wg1raw[:, :], ident[0:E1, 0:E1])
            nb = E0 * F0 // P
            pe.transpose(ps_pv[:, 1, E1:E1 + nb], b1raw[:, :], ident[0:nb, 0:nb]).then_inc(s["w_turned"], 1)

            def attention(pas):
                q0 = JOBS // 8 * pas
                n0 = 4 * q0

                def turn_x(q, j):
                    q, j = q + j // 4, j % 4
                    pe.wait_ge(xs_staged[j], 16 * q + 16)
                    for k in range(QT):
                        last = pe.transpose(ps_m[:, 1, k * P:(k + 1) * P], xs[j % 2][:, k, :], ident[:, :])
                    last.then_inc(s["xt_turned"], 1)

                def project(q, j):
                    w = wqkv[1 - (pas if not isinstance(q, int) else (4 * q + j) // (JOBS // 2))]
                    pe.wait_ge(s["xt_copied"], 4 * q + j + 1)
                    for t in range(2):
                        pe.matmul(ps_m[:, 1, t * S:(t + 1) * S], w[:, t, :], xT[j % 2][:, :], start=True, stop=True)
                    for k in range(QT):
                        last = pe.matmul(ps_m[:, 0, S + k * P:S + (k + 1) * P], xT[j % 2][:, k * P:(k + 1) * P], w[:, 2, :], start=True, stop=True)
                    last.then_inc(s["qkv_done"], 1)

                def scores(n, j, u, dst=ps_s, ahead=0):
                    c, ip, sq = u // 4, u // 2 % 2, u % 2
                    if not isinstance(n, int) or 8 * n + u > ahead:
                        pe.wait_ge(s["s_reduced"], 8 * n + u - ahead)
                    for dg in range(2):
                        for di in range(2):
                            r = slice(32 * (2 * ip + di), 32 * (2 * ip + di) + 31)
                            last = pe.matmul(dst[:, di, dg * S:(dg + 1) * S], rows[j][r, 2 * c + dg, 0, sq * P:(sq + 1) * P],
                                             rows[j][r, 2 * c + dg, 1, :], start=True, stop=True)
                    last.then_inc(s["s_ready"], 1)

                def turn_m(n, p):
                    pe.wait_ge(s["s_reduced"], 8 * n + 8)
                    for k in range(QT):
                        last = pe.transpose(ps_m[0:HEADS, 0, S + k * P:S + (k + 1) * P], negm[p][:, k, :], ident[:, :])
                    last.then_inc(s["m_turned"], 1)

                def scores_t(n, j, u):
                    c, ip, kt = u // 4, u // 2 % 2, u % 2
                    if not (isinstance(n, int) and n == 0 and u == 0):
                        pe.wait_ge(s["exp_done"], 8 * n + u)
                    for dg in range(2):
                        for di in range(2):
                            r = slice(32 * (2 * ip + di), 32 * (2 * ip + di) + 32)
                            last = pe.matmul(ps_t[:, di, dg * S:(dg + 1) * S], rows[j][r, 2 * c + dg, 1, kt * P:(kt + 1) * P],
                                             rows[j][r, 2 * c + dg, 0, :], start=True, stop=True)
                    last.then_inc(s["st_ready"], 1)

                def values(n, j, u):
                    c, ip, kt = u // 4, u // 2 % 2, u % 2
                    pe.wait_ge(s["exp_done"], 8 * n + u + 1)
                    for x in range(4):
                        di, dg = x // 2, x % 2
                        last = pe.matmul(ps_pv[32 * x:32 * x + 32, c, ip * S:(ip + 1) * S], va[j][:, kt, 4 * (2 * c + dg) + 2 * ip + di, :],
                                         probs[:, u % 2, x, :], start=(kt == 0), stop=(kt == 1))
                    last.then_inc(s["pv_done"], 1)

                def turn_c(n):
                    pe.wait_ge(s["ct_copied"], n + 1)
                    for k in range(QT):
                        for blk in range(4):
                            last = pe.transpose(ps_m[:, k, blk * P:(blk + 1) * P], ctxT[:, blk, k * P:(k + 1) * P], ident[:, :])
                    last.then_inc(s["ct_turned"], 1)

                def turn_o(n):
                    pe.wait_ge(s["o_ready"], 4 * n + 4)
                    for k in range(QT):
                        last = pe.transpose(ps_m[:, 0, k * P:(k + 1) * P], o[:, k, :], ident[:, :])
                    last.then_inc(s["ot_turned"], 1)

                def output(n):
                    pe.wait_ge(s["ot_copied"], n + 1)
                    for k in range(QT):
                        last = pe.matmul(ps_m[:, 0, S + k * P:S + (k + 1) * P], oT[:, k * P:(k + 1) * P], wo[:, :], start=True, stop=True)
                    last.then_inc(s["wo_done"], 1)

                def projected(n):
                    pe.wait_ge(s["qk_split"], 4 * n)
                    pe.wait_ge(s["v_copied"], 2 * n)

                def job(q, j, more, first=False):
                    n, p = 4 * q + j, j % 2
                    pe.wait_ge(m_sent[j % 4], 64 * (q + j // 4) + 64)
                    if more >= 2:
                        pe.wait_ge(rows_sent[(j + 2) % 4], 256 * (q + (j + 2) // 4) + 256)
                    for u in range(UNITS):
                        scores_t(n, j % 4, u)
                        if more >= 2:
                            scores(n + 2, (j + 2) % 4, u)
                        if u:
                            values(n, j % 4, u - 1)
                        elif not (first and pas == 0):
                            pe.wait_ge(s["ct_copied"], n)
                        if u == 0:
                            if first:
                                projected(n0 + 3)
                            elif pas == 0 and not (isinstance(n, int) and n == 1):
                                pe.wait_ge(s["h_added"], n - 1)
                            elif pas == 1 or not isinstance(n, int):
                                pe.wait_ge(s["o_ready"], 4 * n - 4)
                            if isinstance(n, int) and n == JOBS // 2 + 2:
                                pe.wait_ge(s["sums_kept"], 1)
                            if more >= 1:
                                turn_m(n + 1, 1 - p)
                            if more >= 3:
                                turn_x(q, j + 3)
                        if u == 1 and more >= 3:
                            pe.wait_ge(s["m_copied"], n + 2)
                            project(q, j + 3)
                        if not first:
                            if u == 4:
                                projected(n + 4 if more >= 3 else 2 * B)
                                pe.wait_ge(s["m_copied"], n + 2 if more >= 1 else n + 1)
                                turn_c(n - 1)
                            if pas == 0 and u == 6:
                                turn_o(n - 1)
                            if pas == 0 and u == 7:
                                output(n - 1)
                            if u == 7 and isinstance(n, int) and n == JOBS // 2 + 1:
                                pe.wait_ge(s["o_ready"], 4 * n)
                                sums(0, ps_m[:, 0, 0:NT * E0], ps_m[:, 0, NT * E0:2 * NT * E0])
                    values(n, j % 4, UNITS - 1)

                if pas == 0:
                    for j in range(3):
                        if j:
                            projected(j)
                        turn_x(0, j)
                        project(0, j)
                    projected(3)
                    for j in range(2):
                        pe.wait_ge(rows_sent[j], 256)
                        for u in range(UNITS):
                            scores(j, j, u, (ps_s, ps_t)[u % 2], ahead=1)
                        if j == 0:
                            turn_m(0, 0)
                last = q0 + JOBS // 8 - 1
                if pas == 0:
                    pe.wait_ge(s["m_copied"], 1)
                    pe.wait_ge(s["s_reduced"], 2 * UNITS)
                    pe.wait_ge(s["w_turned_copied"], 3)
                    job(0, 0, 3, True)
                else:
                    for j in range(1, 5):
                        job(q0, j, 3)
                with pe.Fori(q0 + pas, last) as q:
                    for j in range(1, 5):
                        job(q, j, 3)
                n = 4 * last + 1
                if pas:
                    pe.wait_ge(s["ct_copied"], n)
                    pe.wait_ge(s["s_reduced"], 8 * n + 16)
                    pe.wait_ge(s["o_ready"], 4 * n - 4)
                    projected(2 * B)
                    experts()
                    pe.wait_ge(s["e_added"], STEPS0)
                for j in range(1, 5 - pas):
                    job(last, j, 3 if pas == 0 else 3 - j)
                if pas:
                    n = 4 * last + 3
                    pe.wait_ge(s["o_ready"], 4 * n)
                    turn_c(n)

            def experts():
                def turn(i, p, h):
                    pe.wait_ge(x_in[p], 16 * h + 16)
                    if not isinstance(i, int) or i >= 2:
                        pe.wait_ge(s["e_copied"], i - 1)
                    for k in range(2):
                        last = pe.transpose(ps[:, 4 + p, k * P:(k + 1) * P], ex[p]["x"][:, k, :], ident[:, :])
                    last.then_inc(s["e_turned"], 1)

                def hidden(i, p, h):
                    pe.wait_ge(up_in[p], 16 * h + 16)
                    pe.wait_ge(s["e_copied"], i + 1)
                    if not isinstance(i, int) or i >= 2:
                        pe.wait_ge(s["e_gelu"], i - 1)
                    for f in range(F0 // P):
                        last = pe.matmul(ps[:, 2 * p + f // 2, (f % 2) * SLOTS:(f % 2 + 1) * SLOTS], ex[p]["w1"][:, f * P:(f + 1) * P],
                                         ex[p]["xT"][:, 0:SLOTS], start=True, stop=True)
                    last.then_inc(s["e_hidden"], 1)

                def result(i, p, h):
                    pe.wait_ge(down_in[p], 16 * h + 16)
                    pe.wait_ge(s["e_gelu"], i + 1)
                    if not isinstance(i, int) or i >= 2:
                        pe.wait_ge(s["e_added"], i - 1)
                    for k in range(2):
                        for f in range(F0 // P):
                            last = pe.matmul(ps[:, 6 + p, k * D:(k + 1) * D], ex[p]["g"][:, f, k * P:(k + 1) * P], ex[p]["w2"][:, f, :],
                                             start=(f == 0), stop=(f == F0 // P - 1))
                    last.then_inc(s["e_out"], 1)

                turn(0, 0, 0)
                hidden(0, 0, 0)
                turn(1, 1, 0)

                def steps0(h):
                    hidden(2 * h + 1, 1, h)
                    turn(2 * h + 2, 0, h + 1)
                    result(2 * h, 0, h)
                    hidden(2 * h + 2, 0, h + 1)
                    turn(2 * h + 3, 1, h + 1)
                    result(2 * h + 1, 1, h)

                steps0(0)
                with pe.Fori(1, STEPS0 // 2 - 1) as h:
                    steps0(h)
                half = STEPS0 // 2 - 1
                hidden(STEPS0 - 1, 1, half)
                result(STEPS0 - 2, 0, half)
                result(STEPS0 - 1, 1, half)

            def route(l):
                E = (E0, E1)[l]
                r0 = NT // 4 * l

                src, ready = ((YN, "yn_ready"), (XN, "xn_ready"))[l]

                def turn_rows(n):
                    pe.wait_ge(s[ready], NT + 4 * n + 4)
                    if n >= 3:
                        pe.wait_ge(s["rt_copied"], r0 + n - 2)
                    for k in range(4):
                        last = pe.transpose(ps[:, ROW_BANKS[n % 3], k * P:(k + 1) * P], src[:, 4 * n + k, :], ident[:, :])
                    last.then_inc(s["rt_turned"], 1)

                for n in range(2):
                    turn_rows(n)
                for n in range(NT // 4):
                    if n + 2 < NT // 4:
                        turn_rows(n + 2)
                    pe.wait_ge(s["rt_copied"], r0 + n + 1)
                    if n >= 2:
                        pe.wait_ge(s["rt_kept"], r0 + n - 1)
                    for k in range(4):
                        last = pe.matmul(ps[:, 2 + n % 2, k * E:(k + 1) * E], rT[n % 3][:, k * P:(k + 1) * P], wg[l][:, :], start=True, stop=True)
                    last.then_inc(s["rt_logits"], 1)
                pe.wait_ge(s["rt_kept"], r0 + NT // 4)

            def sums(l, inside_at, total_at):
                pe.wait_ge(s["sums_ready"], 2 * l + 1)
                chosen = RK[:, :, 0:(E0, E1)[l]]
                pe.matmul(inside_at, before[:, :], chosen, start=True, stop=True)
                pe.matmul(total_at, ones[:, :], chosen, start=True, stop=True).then_inc(s["sums_ready"], 1)

            pe.wait_ge(s["rows_init"], 12)
            attention(0)
            pe.wait_ge(s["h_added"], B)
            pe.wait_ge(s["s_reduced"], UNITS * (B + 3))
            pe.wait_ge(s["ct_copied"], B + 1)
            pe.wait_ge(s["consts_made"], 8)
            route(0)
            attention(1)
            pe.wait_ge(s["x_added"], B)

            pe.wait_ge(s["p_loaded"], 64)
            for raw, bank, ready in ((praw, 0, "pq_turned"), (kraw, 2, "pk_turned"), (oraw, 6, "po_turned")):
                for c in range(HEADS // 2):
                    last = pe.transpose(ps[:, bank + c // 4, (c % 4) * D:(c % 4 + 1) * D], raw[:, 2 * c:2 * c + 2, :].rearrange("p a k -> p (a k)"), ident[:, :])
                last.then_inc(s[ready], 1)
            pe.wait_ge(s["pq_copied"], 1)
            pe.wait_ge(s["pk_copied"], 1)
            for h in range(HEADS):
                r = slice(DK * (h % 2), DK * (h % 2) + DK)
                c = 8 * (h % 2) + h // 2
                last = pe.matmul(ps[:, c // 4, (c % 4) * D:(c % 4 + 1) * D], PkT[r, h // 2, :], PqT[r, h // 2, :], start=True, stop=True)
            last.then_inc(s["a_made"], 1)
            pe.wait_ge(s["po_copied"], 1)
            pe.wait_ge(s["a_copied"], 1)

            route(1)

            def turn_x1(b, p, h):
                if not isinstance(b, int) or b > 2:
                    pe.wait_ge(s["y_added"], 2 * b - 4)
                pe.wait_ge(xs_staged[p], 16 * (JOBS // 4) + 16 * h + 16)
                for k in range(QT):
                    last = pe.transpose(ps[:, 7, (k + 1) * P:(k + 2) * P], xs[p][:, k, :], ident[:, :])
                last.then_inc(s["x1_ready"], 1)

            def keys(b, g, p):
                pe.wait_ge(s["x1_copied"], b + 1)
                if not isinstance(b, int) or 4 * b + g:
                    pe.wait_ge(s["u_copied"], 4 * b + g)
                for i in range(4):
                    last = pe.matmul(ps_s[:, i // 2, (i % 2) * S:(i % 2 + 1) * S], AH[:, 4 * g + i, :], xT[p][:, :], start=True, stop=True)
                last.then_inc(s["u_ready"], 1)

            def scores1(b, g, p):
                n, gp = 4 * b + g, g % 2
                pe.wait_ge(s["u_copied"], 4 * b + g + 1)
                if not (isinstance(n, int) and n == 0):
                    pe.wait_ge(s["exp0_done"], n)
                pe.matmul(ps[:, 2, :], xT[p][:, 0:P], U[gp][:, :, 0:P], start=True, stop=False)
                pe.matmul(ps[:, 2, :], identb[:, :], tri0[:, :, :], start=False, stop=True).then_inc(s["s0_ready"], 1)
                if not (isinstance(n, int) and n == 0):
                    pe.wait_ge(s["exp1_done"], n)
                for x in range(2):
                    pe.matmul(ps[:, 3 + x, :], xT[p][:, P:2 * P], U[gp][:, 2 * x:2 * x + 2, :], start=True, stop=False)
                    late = ps[:, 3 + x, :].rearrange("p (i k) -> p i k", i=2)[:, :, P:2 * P]
                    last = pe.matmul(late, identb[:, :], tri0[:, 0:2, :], start=False, stop=True)
                last.then_inc(s["s1_ready"], 1)

            def values1(b, k, p, bank=5):
                if bank == 5 and not (isinstance(b, int) and b == 0 and k == 0):
                    pe.wait_ge(s["o1_copied"], 2 * b + k)
                for x in range(2):
                    for i, (x_part, v_part) in enumerate(((xL[p], PvH), (xH[p], PvL), (xH[p], PvH))):
                        last = pe.matmul(ps[:, bank + x, :], x_part[:, k * P:(k + 1) * P], v_part[:, x * 512:(x + 1) * 512], start=(i == 0), stop=(i == 2))
                last.then_inc(s["v1_ready"], 1)

            def turn_o(b, k, src=O1, bank=5):
                pe.wait_ge(s["o1_ready"], 2 * b + k + 1)
                for c in range(HEADS // 2):
                    last = pe.transpose(ps[:, bank + c // 4, (c % 4) * P:(c % 4 + 1) * P], src[:, c * P:(c + 1) * P], ident[:, :])
                last.then_inc(s["o1_turned"], 1)

            def output1(b, k, src=O1T, bank=7):
                pe.wait_ge(s["o1_copied"], 2 * b + k + 1)
                pe.wait_ge(s["x1_copied"], min(b + 3, B) if isinstance(b, int) else b + 3)
                if bank == 7 and not (isinstance(b, int) and b == 0 and k == 0):
                    pe.wait_ge(s["y_added"], 2 * b + k)
                for c in range(HEADS // 2):
                    last = pe.matmul(ps[:, bank, 0:D], src[:, c, :], PoT[:, c, :], start=(c == 0), stop=(c == HEADS // 2 - 1))
                last.then_inc(s["y_ready"], 1)

            def experts1():
                half = STEPS0 // 2

                def turn_e(e, p, h):
                    pe.wait_ge(x_in[p], 16 * half + 16 * h + 16)
                    for k in range(CT):
                        last = pe.transpose(ps[:, k // 4, (k % 4) * P:(k % 4 + 1) * P], ex[p]["x"][:, k, :], ident[:, :])
                    last.then_inc(s["e_turned"], 1)

                def hidden1(e, p, h):
                    pe.wait_ge(up_in[p], 16 * half + 16 * h + 16)
                    pe.wait_ge(s["e_copied"], STEPS0 + e + 1)
                    pe.wait_ge(s["e_gelu"], STEPS0 + e)
                    for f in range(F1 // P):
                        for c in range(2):
                            last = pe.matmul(ps[:, 2 + 2 * f + c, 0:HALF], ex[p]["w1"][:, f * P:(f + 1) * P], ex[p]["xT"][:, c * HALF:(c + 1) * HALF],
                                             start=True, stop=True)
                        if f < F1 // P - 1:
                            last.then_inc(s["e_half"], 1)
                    last.then_inc(s["e_hidden"], 1)

                def result1(e, p, h):
                    pe.wait_ge(down_in[p], 16 * half + 16 * h + 16)
                    pe.wait_ge(s["e_gelu"], STEPS0 + e + 1)
                    pe.wait_ge(s["e_added"], STEPS0 + e)
                    act_of = ex[p]["g"][:, :, :].rearrange("p (f c) n -> p f (c n)", c=2)
                    for k in range(CT):
                        for f in range(F1 // P):
                            last = pe.matmul(ps[:, 6 + k // 4, (k % 4) * D:(k % 4 + 1) * D], act_of[:, f, k * P:(k + 1) * P], ex[p]["w2"][:, f, :],
                                             start=(f == 0), stop=(f == F1 // P - 1))
                    last.then_inc(s["e_out"], 1)

                turn_e(0, 0, 0)
                with pe.Fori(0, E1 // 2 - 1) as h:
                    for p in range(2):
                        hidden1(2 * h + p, p, h)
                        turn_e(2 * h + p + 1, 1 - p, h + p)
                        result1(2 * h + p, p, h)
                last_h = E1 // 2 - 1
                hidden1(E1 - 2, 0, last_h)
                turn_e(E1 - 1, 1, last_h)
                result1(E1 - 2, 0, last_h)
                hidden1(E1 - 1, 1, last_h)
                result1(E1 - 1, 1, last_h)

            def sequence(b, p, h_next, prev=True, nxt=True):
                scores1(b, 0, p)
                if prev:
                    values1(b - 1, 0, 1 - p)
                keys(b, 2, p)
                scores1(b, 1, p)
                if prev:
                    turn_o(b - 1, 0)
                keys(b, 3, p)
                if prev:
                    values1(b - 1, 1, 1 - p)
                if nxt:
                    turn_x1(b + 1, 1 - p, h_next)
                scores1(b, 2, p)
                if prev:
                    output1(b - 1, 0)
                if nxt:
                    keys(b + 1, 0, 1 - p)
                if prev:
                    turn_o(b - 1, 1)
                if isinstance(b, int) and b == 0:
                    sums(1, ps[:, 5, 0:NT * E1], ps[:, 6, 0:NT * E1])
                scores1(b, 3, p)
                if prev:
                    output1(b - 1, 1)
                if nxt:
                    keys(b + 1, 1, 1 - p)

            turn_x1(0, 0, 0)
            keys(0, 0, 0)
            keys(0, 1, 0)
            sequence(0, 0, 0, prev=False)
            pe.wait_ge(s["sums_kept"], 2)
            pe.wait_ge(s["pv_low"], 1)
            sequence(1, 1, 1)
            sequence(2, 0, 1)
            with pe.Fori(1, BEFORE // 2) as h:
                sequence(2 * h + 1, 1, h + 1)
                sequence(2 * h + 2, 0, h + 1)
            pe.wait_ge(s["u_copied"], 4 * BEFORE + 2)
            pe.wait_ge(s["x1_copied"], BEFORE + 1)
            pe.wait_ge(s["exp1_done"], 4 * BEFORE)
            pe.wait_ge(s["o1_copied"], 2 * BEFORE - 2)
            pe.wait_ge(s["y_added"], 2 * BEFORE - 2)
            experts1()
            pe.wait_ge(s["e_added"], STEPS0 + E1)
            with pe.Fori(BEFORE // 2, B // 2 - 1) as h:
                sequence(2 * h + 1, 1, h + 1)
                sequence(2 * h + 2, 0, h + 1)
            sequence(B - 1, 1, 0, nxt=False)
            values1(B - 1, 0, 1)
            values1(B - 1, 1, 1, bank=0)
            turn_o(B - 1, 0)
            pe.wait_ge(s["exp1_done"], 4 * B)
            turn_o(B - 1, 1, flat(U[0]), bank=3)
            output1(B - 1, 0, O1T)
            output1(B - 1, 1, U[1][:, :, :].rearrange("p i (c t) -> p (i c) t", t=P), bank=2)


_INS = ["L0_attn_x", "L0_attn_Wq", "L0_attn_Wk", "L0_attn_Wv", "L0_ffn_ln1_w", "L0_ffn_ln1_b", "L0_ffn_ln2_w", "L0_ffn_ln2_b",
        "L0_ffn_w_qkv", "L0_ffn_b_qkv", "L0_ffn_w_o", "L0_ffn_b_o", "L0_ffn_w_gate", "L0_ffn_w1", "L0_ffn_b1", "L0_ffn_w2",
        "L0_ffn_b2", "L1_attn_P_q", "L1_attn_P_k", "L1_attn_P_v", "L1_attn_P_o", "L1_ffn_gate_w", "L1_ffn_w1", "L1_ffn_w2"]


def kernel(**inputs):
    import numpy as _np
    import concourse.bacc as _bacc
    from concourse import mybir as _mybir
    from concourse.bass_utils import run_bass_kernel_spmd as _run

    nc = _bacc.Bacc("TRN2", target_bir_lowering=False, num_devices=1)
    arrays, args = {}, {}
    for name in _INS:
        a = _np.ascontiguousarray(inputs[name])
        arrays[f"in_{name}_dram"] = a
        args[name] = nc.dram_tensor(f"in_{name}_dram", a.shape, _mybir.dt.from_np(a.dtype), kind="ExternalInput").ap()
    out = nc.dram_tensor("out_dram", args["L0_attn_x"].shape, _mybir.dt.float32, kind="ExternalOutput").ap()
    build(nc, args, out)
    r = _run(nc, [arrays], core_ids=[0])
    return r.results[0]["out_dram"]
```
